# Optimizing a Trainium2 kernel written in Bass

```python
import numpy as np
import jax
import jax.numpy as jnp

def _softmax(x, axis=-1):
    return jax.nn.softmax(x, axis=axis)

def _gelu(x):
    return jax.nn.gelu(x, approximate=True)

def _silu(x):
    return jax.nn.silu(x)

def _sigmoid(x):
    return jax.nn.sigmoid(x)

def _layernorm(x, axis=-1, eps=1e-05):
    m = jnp.mean(x, axis=axis, keepdims=True)
    v = jnp.var(x, axis=axis, keepdims=True)
    return (x - m) / jnp.sqrt(v + eps)

def _scatter_add(tgt, idx, src, axis=0):
    return tgt.at[idx].add(src)

def _segment_sum(src, seg, n):
    return jax.ops.segment_sum(src, seg, n)
kernel_name = 'mk_gnn_preln_d4_gnn_r16_55f4eb'

def setup_inputs(seed: int=0):
    np.random.seed(seed)
    _w = jnp.asarray

    def _rec_inputs():
        import jax
        import jax.numpy as jnp
        _gk = jax.random.key(seed)
        x = -0.0003713 + 1 * jax.random.normal(jax.random.fold_in(_gk, 1), (6250, 128), jnp.float32)
        src = jax.random.randint(jax.random.fold_in(_gk, 2), (200000,), 0, 6250, jnp.int32)
        dst = jnp.minimum((6250 * jax.random.uniform(jax.random.fold_in(_gk, 3), (200000,)) ** 2.0).astype(jnp.int32), 99999)
        _o = jnp.argsort(dst, stable=True)
        src = src[_o]
        dst = dst[_o]
        return (x, src, dst)
    x, src, dst = _rec_inputs()

    def _L0_gnn_setup():
        import jax, jax.numpy as jnp
        import numpy as np
        N = 6250
        E = 31250
        D_IN = 128
        D_OUT = 128
        key = jax.random.key(seed)
        k1, k2, k3 = jax.random.split(key, 3)
        x = jax.random.normal(k1, (N, D_IN), dtype=jnp.float32)
        edge_index = jax.random.randint(k2, (2, E), 0, N, dtype=jnp.int32)
        W = jax.random.normal(k3, (D_IN, D_OUT), dtype=jnp.float32) * (1.0 / np.sqrt(D_IN))
        b = jnp.zeros((D_OUT,), dtype=jnp.float32)
        return {'x': x, 'edge_index': edge_index, 'W': W, 'b': b}
    _L0_gnn_all = _L0_gnn_setup()
    _L0_gnn_in = {k: v for k, v in _L0_gnn_all.items() if k in ('W', 'b')}
    del _L0_gnn_all

    def _L1_gnn_setup():
        import jax, jax.numpy as jnp
        import numpy as np
        N_NODES = 3125
        N_EDGES = 37500
        D = 128
        key = jax.random.key(seed)
        k1, k2, k3, k4 = jax.random.split(key, 4)
        feature = jax.random.normal(k1, (N_NODES, D), dtype=jnp.float32)
        src = jax.random.randint(k2, (N_EDGES,), 0, N_NODES, dtype=jnp.int32)
        dst = jax.random.randint(k3, (N_EDGES,), 0, N_NODES, dtype=jnp.int32)
        W = jax.random.normal(k4, (D, D), dtype=jnp.float32) * (1.0 / np.sqrt(D))
        b = jnp.zeros((D,), dtype=jnp.float32)
        return {'feature': feature, 'src': src, 'dst': dst, 'W': W, 'b': b}
    _L1_gnn_all = _L1_gnn_setup()
    _L1_gnn_in = {k: v for k, v in _L1_gnn_all.items() if k in ('W', 'b')}
    del _L1_gnn_all

    def _L2_gnn_setup():
        import jax, jax.numpy as jnp
        import numpy as np
        NUM_STEPS = 1

        def _seg_mean(vals, idx, num_nodes):
            s = jax.ops.segment_sum(vals, idx, num_segments=num_nodes)
            cnt = jax.ops.segment_sum(jnp.ones((vals.shape[0],), vals.dtype), idx, num_segments=num_nodes)
            return s / jnp.maximum(cnt, 1.0)[:, None]

        def _gru_cell(a, h, w_ih, w_hh, b_ih, b_hh):
            gi = a @ w_ih.T + b_ih
            gh = h @ w_hh.T + b_hh
            H = h.shape[1]
            i_r, i_z, i_n = (gi[:, :H], gi[:, H:2 * H], gi[:, 2 * H:])
            h_r, h_z, h_n = (gh[:, :H], gh[:, H:2 * H], gh[:, 2 * H:])
            r = jax.nn.sigmoid(i_r + h_r)
            z = jax.nn.sigmoid(i_z + h_z)
            n = jnp.tanh(i_n + r * h_n)
            return (1.0 - z) * n + z * h
        key = jax.random.key(seed)
        ks = jax.random.split(key, 8)
        N, E, H = (6250, 40000, 128)
        sc = 1.0 / np.sqrt(H)
        feat = jax.random.normal(ks[0], (N, H), jnp.float32)
        src = jax.random.randint(ks[1], (E,), 0, N, jnp.int32)
        dst = jax.random.randint(ks[2], (E,), 0, N, jnp.int32)
        W_in = jax.random.normal(ks[3], (H, H), jnp.float32) * sc
        W_out = jax.random.normal(ks[4], (H, H), jnp.float32) * sc
        w_ih = jax.random.normal(ks[5], (3 * H, 2 * H), jnp.float32) * sc
        w_hh = jax.random.normal(ks[6], (3 * H, H), jnp.float32) * sc
        return {'feat': feat, 'src': src, 'dst': dst, 'W_in': W_in, 'b_in': jnp.zeros((H,), jnp.float32), 'W_out': W_out, 'b_out': jnp.zeros((H,), jnp.float32), 'w_ih': w_ih, 'w_hh': w_hh, 'b_ih': jnp.zeros((3 * H,), jnp.float32), 'b_hh': jnp.zeros((3 * H,), jnp.float32)}
    _L2_gnn_all = _L2_gnn_setup()
    _L2_gnn_in = {k: v for k, v in _L2_gnn_all.items() if k in ('W_in', 'b_in', 'W_out', 'b_out', 'w_ih', 'w_hh', 'b_ih', 'b_hh')}
    del _L2_gnn_all

    def _L3_gnn_setup():
        import jax, jax.numpy as jnp
        import numpy as np
        N = 6250
        E = 100000
        IN = 128
        OUT = 128
        H = 4
        FH = OUT // H
        EPS = 1e-05
        NEG_SLOPE = 0.2

        def _gat(x, src, dst, W, a_src, a_dst, b):
            n = x.shape[0]
            xw = (x @ W).reshape(n, H, FH)
            al_s = jnp.einsum('nhf,hf->nh', xw, a_src)
            al_d = jnp.einsum('nhf,hf->nh', xw, a_dst)
            e = jax.nn.leaky_relu(al_s[src] + al_d[dst], NEG_SLOPE)
            m = jax.ops.segment_max(e, dst, num_segments=n)
            ee = jnp.exp(e - m[dst])
            den = jax.ops.segment_sum(ee, dst, num_segments=n)
            alpha = ee / den[dst]
            out = jax.ops.segment_sum(alpha[:, :, None] * xw[src], dst, num_segments=n)
            return out.reshape(n, H * FH) + b

        def _bn(x, gamma, beta):
            mu = x.mean(0)
            var = x.var(0)
            return gamma * (x - mu) * jax.lax.rsqrt(var + EPS) + beta
        key = jax.random.key(seed)
        ks = jax.random.split(key, 10)
        x = jax.random.normal(ks[0], (N, IN), jnp.float32)
        edge_index = jax.random.randint(ks[1], (2, E), 0, N, dtype=jnp.int32)
        W1 = jax.random.normal(ks[2], (IN, OUT), jnp.float32) / np.float32(np.sqrt(IN))
        a1_src = jax.random.normal(ks[3], (H, FH), jnp.float32) * 0.1
        a1_dst = jax.random.normal(ks[4], (H, FH), jnp.float32) * 0.1
        b1 = jnp.zeros((OUT,), jnp.float32)
        g1 = jnp.ones((OUT,), jnp.float32)
        beta1 = jnp.zeros((OUT,), jnp.float32)
        W2 = jax.random.normal(ks[5], (OUT, OUT), jnp.float32) / np.float32(np.sqrt(OUT))
        a2_src = jax.random.normal(ks[6], (H, FH), jnp.float32) * 0.1
        a2_dst = jax.random.normal(ks[7], (H, FH), jnp.float32) * 0.1
        b2 = jnp.zeros((OUT,), jnp.float32)
        g2 = jnp.ones((OUT,), jnp.float32)
        beta2 = jnp.zeros((OUT,), jnp.float32)
        return dict(x=x, edge_index=edge_index, W1=W1, a1_src=a1_src, a1_dst=a1_dst, b1=b1, g1=g1, beta1=beta1, W2=W2, a2_src=a2_src, a2_dst=a2_dst, b2=b2, g2=g2, beta2=beta2)
    _L3_gnn_all = _L3_gnn_setup()
    _L3_gnn_in = {k: v for k, v in _L3_gnn_all.items() if k in ('W1', 'a1_src', 'a1_dst', 'b1', 'g1', 'beta1', 'W2', 'a2_src', 'a2_dst', 'b2', 'g2', 'beta2')}
    del _L3_gnn_all
    return {'x': x, 'src': src, 'dst': dst, 'L0_gnn_W': _L0_gnn_in['W'], 'L0_gnn_b': _L0_gnn_in['b'], 'L1_gnn_W': _L1_gnn_in['W'], 'L1_gnn_b': _L1_gnn_in['b'], 'L2_gnn_W_in': _L2_gnn_in['W_in'], 'L2_gnn_b_in': _L2_gnn_in['b_in'], 'L2_gnn_W_out': _L2_gnn_in['W_out'], 'L2_gnn_b_out': _L2_gnn_in['b_out'], 'L2_gnn_w_ih': _L2_gnn_in['w_ih'], 'L2_gnn_w_hh': _L2_gnn_in['w_hh'], 'L2_gnn_b_ih': _L2_gnn_in['b_ih'], 'L2_gnn_b_hh': _L2_gnn_in['b_hh'], 'L3_gnn_W1': _L3_gnn_in['W1'], 'L3_gnn_a1_src': _L3_gnn_in['a1_src'], 'L3_gnn_a1_dst': _L3_gnn_in['a1_dst'], 'L3_gnn_b1': _L3_gnn_in['b1'], 'L3_gnn_g1': _L3_gnn_in['g1'], 'L3_gnn_beta1': _L3_gnn_in['beta1'], 'L3_gnn_W2': _L3_gnn_in['W2'], 'L3_gnn_a2_src': _L3_gnn_in['a2_src'], 'L3_gnn_a2_dst': _L3_gnn_in['a2_dst'], 'L3_gnn_b2': _L3_gnn_in['b2'], 'L3_gnn_g2': _L3_gnn_in['g2'], 'L3_gnn_beta2': _L3_gnn_in['beta2']}

def reference(x, src, dst, L0_gnn_W, L0_gnn_b, L1_gnn_W, L1_gnn_b, L2_gnn_W_in, L2_gnn_b_in, L2_gnn_W_out, L2_gnn_b_out, L2_gnn_w_ih, L2_gnn_w_hh, L2_gnn_b_ih, L2_gnn_b_hh, L3_gnn_W1, L3_gnn_a1_src, L3_gnn_a1_dst, L3_gnn_b1, L3_gnn_g1, L3_gnn_beta1, L3_gnn_W2, L3_gnn_a2_src, L3_gnn_a2_dst, L3_gnn_b2, L3_gnn_g2, L3_gnn_beta2):
    import jax
    import jax.numpy as jnp

    def _L0_gnn_ref(x, edge_index, W, b):
        import jax, jax.numpy as jnp
        import numpy as np
        N = 6250
        E = 31250
        D_IN = 128
        D_OUT = 128
        h = x @ W
        src, dst = (edge_index[0], edge_index[1])
        loop = jnp.arange(N, dtype=edge_index.dtype)
        src = jnp.concatenate([src, loop])
        dst = jnp.concatenate([dst, loop])
        deg = jax.ops.segment_sum(jnp.ones(src.shape, dtype=h.dtype), dst, num_segments=N)
        dinv = jnp.where(deg > 0, jax.lax.rsqrt(deg), 0.0)
        norm = dinv[src] * dinv[dst]
        msg = h[src] * norm[:, None]
        out = jax.ops.segment_sum(msg, dst, num_segments=N) + b
        return jax.nn.relu(out)

    def _L1_gnn_ref(feature, src, dst, W, b):
        import jax, jax.numpy as jnp
        import numpy as np
        N_NODES = 3125
        N_EDGES = 37500
        D = 128
        msgs = feature[src]
        agg = jax.ops.segment_sum(msgs, dst, num_segments=feature.shape[0])
        h = agg + feature
        return h @ W.T + b

    def _L2_gnn_ref(feat, src, dst, W_in, b_in, W_out, b_out, w_ih, w_hh, b_ih, b_hh):
        import jax, jax.numpy as jnp
        import numpy as np
        NUM_STEPS = 1

        def _seg_mean(vals, idx, num_nodes):
            s = jax.ops.segment_sum(vals, idx, num_segments=num_nodes)
            cnt = jax.ops.segment_sum(jnp.ones((vals.shape[0],), vals.dtype), idx, num_segments=num_nodes)
            return s / jnp.maximum(cnt, 1.0)[:, None]

        def _gru_cell(a, h, w_ih, w_hh, b_ih, b_hh):
            gi = a @ w_ih.T + b_ih
            gh = h @ w_hh.T + b_hh
            H = h.shape[1]
            i_r, i_z, i_n = (gi[:, :H], gi[:, H:2 * H], gi[:, 2 * H:])
            h_r, h_z, h_n = (gh[:, :H], gh[:, H:2 * H], gh[:, 2 * H:])
            r = jax.nn.sigmoid(i_r + h_r)
            z = jax.nn.sigmoid(i_z + h_z)
            n = jnp.tanh(i_n + r * h_n)
            return (1.0 - z) * n + z * h
        N = feat.shape[0]
        h = feat
        for _ in range(NUM_STEPS):
            feat_in = h @ W_in.T + b_in
            feat_out = h @ W_out.T + b_out
            a_in = _seg_mean(feat_in[src], dst, N)
            a_out = _seg_mean(feat_out[dst], src, N)
            a = jnp.concatenate((a_in, a_out), axis=1)
            h = _gru_cell(a, h, w_ih, w_hh, b_ih, b_hh)
        return h

    def _L3_gnn_ref(x, edge_index, W1, a1_src, a1_dst, b1, g1, beta1, W2, a2_src, a2_dst, b2, g2, beta2):
        import jax, jax.numpy as jnp
        import numpy as np
        N = 6250
        E = 100000
        IN = 128
        OUT = 128
        H = 4
        FH = OUT // H
        EPS = 1e-05
        NEG_SLOPE = 0.2

        def _gat(x, src, dst, W, a_src, a_dst, b):
            n = x.shape[0]
            xw = (x @ W).reshape(n, H, FH)
            al_s = jnp.einsum('nhf,hf->nh', xw, a_src)
            al_d = jnp.einsum('nhf,hf->nh', xw, a_dst)
            e = jax.nn.leaky_relu(al_s[src] + al_d[dst], NEG_SLOPE)
            m = jax.ops.segment_max(e, dst, num_segments=n)
            ee = jnp.exp(e - m[dst])
            den = jax.ops.segment_sum(ee, dst, num_segments=n)
            alpha = ee / den[dst]
            out = jax.ops.segment_sum(alpha[:, :, None] * xw[src], dst, num_segments=n)
            return out.reshape(n, H * FH) + b

        def _bn(x, gamma, beta):
            mu = x.mean(0)
            var = x.var(0)
            return gamma * (x - mu) * jax.lax.rsqrt(var + EPS) + beta
        n = x.shape[0]
        loops = jnp.arange(n, dtype=edge_index.dtype)
        src = jnp.concatenate([edge_index[0], loops])
        dst = jnp.concatenate([edge_index[1], loops])
        h = jax.nn.elu(_bn(_gat(x, src, dst, W1, a1_src, a1_dst, b1), g1, beta1))
        h = jax.nn.elu(_bn(_gat(h, src, dst, W2, a2_src, a2_dst, b2), g2, beta2))
        return h
    edge_index = jnp.stack([src, dst])
    h = jnp.maximum(_layernorm(x, axis=-1), 0.0)
    x = x + _L0_gnn_ref(h, edge_index, L0_gnn_W, L0_gnn_b)
    h = jnp.maximum(_layernorm(x, axis=-1), 0.0)
    x = x + _L1_gnn_ref(h, src, dst, L1_gnn_W, L1_gnn_b)
    h = jnp.maximum(_layernorm(x, axis=-1), 0.0)
    x = x + _L2_gnn_ref(h, src, dst, L2_gnn_W_in, L2_gnn_b_in, L2_gnn_W_out, L2_gnn_b_out, L2_gnn_w_ih, L2_gnn_w_hh, L2_gnn_b_ih, L2_gnn_b_hh)
    h = jnp.maximum(_layernorm(x, axis=-1), 0.0)
    x = x + _L3_gnn_ref(h, edge_index, L3_gnn_W1, L3_gnn_a1_src, L3_gnn_a1_dst, L3_gnn_b1, L3_gnn_g1, L3_gnn_beta1, L3_gnn_W2, L3_gnn_a2_src, L3_gnn_a2_dst, L3_gnn_b2, L3_gnn_g2, L3_gnn_beta2)
    return x

_drawn_inputs = setup_inputs


def setup_inputs(seed=0):
    import zlib

    import numpy as np

    out = dict(_drawn_inputs(seed))
    spreads = {'L0_gnn_b': (0.0, 0.1),
     'L1_gnn_b': (0.0, 0.8),
     'L2_gnn_b_in': (0.0, 2.0),
     'L2_gnn_b_out': (0.0, 2.0),
     'L2_gnn_b_ih': (0.0, 2.0),
     'L2_gnn_b_hh': (0.0, 2.0),
     'L3_gnn_b1': (0.0, 2.0),
     'L3_gnn_g1': (1.0, 0.6),
     'L3_gnn_beta1': (0.0, 2.0),
     'L3_gnn_b2': (0.0, 2.0),
     'L3_gnn_g2': (1.0, 0.6),
     'L3_gnn_beta2': (0.0, 2.0)}
    factors = {'L2_gnn_W_in': 5.466,
     'L2_gnn_W_out': 5.35,
     'L2_gnn_w_ih': 3.715,
     'L2_gnn_w_hh': 25.522,
     'L3_gnn_a1_src': 8.0,
     'L3_gnn_a1_dst': 32.248,
     'L3_gnn_a2_src': 4.314,
     'L3_gnn_a2_dst': 25.238}
    for name, (base, spread) in spreads.items():
        noise = np.random.default_rng([zlib.crc32(name.encode()), seed]).standard_normal(out[name].shape)
        drawn = base * np.exp(spread * noise) if base else spread * noise
        out[name] = jnp.asarray(drawn.astype(out[name].dtype))
    for name, factor in factors.items():
        out[name] = (out[name] * factor).astype(out[name].dtype)
    return out
```

```python
import concourse.bass as bass
from concourse import mybir
from contextlib import ExitStack


def gnn_kernel(nc, a, out, stop_after=9):
    f32, bf16 = mybir.dt.float32, mybir.dt.bfloat16
    i32, u32, i16, u16 = mybir.dt.int32, mybir.dt.uint32, mybir.dt.int16, mybir.dt.uint16
    ALU, ACT, AX = mybir.AluOpType, mybir.ActivationFunctionType, mybir.AxisListType
    ds = bass.ds

    P = 128
    N, D = a["x"].shape
    E = a["src"].shape[0]
    NB = -(-N // P)
    NP = NB * P
    TAIL = N - (NB - 1) * P
    H, FH = a["L3_gnn_a1_src"].shape
    EPS = 1e-5
    SLOPE = 0.2
    RW = D + H
    G = 8
    HALVES = 2
    TILES = -(-E // P)
    STEPS = -(-(TILES + NB - 1) // (G * HALVES)) * G * HALVES
    TILES = STEPS - NB + 1
    GROUPS = STEPS // G
    ROWS = TILES * P
    EP = 125
    EC = E // EP
    assert EP * EC == E and EC % (2 * G) == 0
    CH = -(-TILES // P)
    NO_KEY = 20000
    FAR = -1.0e30
    MG = 7
    NMG = NB // MG
    assert MG * NMG == NB
    PER_BANK = 3

    def dram(name, shape, dt):
        return nc.dram_tensor(name, shape, dt, kind="Internal").ap()

    list_d = [dram(f"edge_list{l}", [ROWS, 2], i32) for l in range(2)]
    table_d = [dram(f"table{k}", [NP, RW], f32) for k in range(5)]
    spill_d = dram("gathered_rows", [GROUPS, P, G * RW], f32)

    ctx = ExitStack()
    with ctx:
        def sb(name, shape, dt):
            return ctx.enter_context(nc.sbuf_tensor(name, shape, dt))

        def sem(name):
            return ctx.enter_context(nc.semaphore(name))

        X = sb("X", [P, NB, D], f32)
        TAB = sb("TAB", [P, NB, RW], f32)
        ACC = sb("ACC", [P, NB, RW], f32)
        U = sb("U", [P, 2, NB * RW], f32)
        UA = U[:, 0, 0:NB * D].rearrange("p (b f) -> p b f", f=D)
        UB = U[:, 1, 0:NB * D].rearrange("p (b f) -> p b f", f=D)
        ACC2 = U[:, 1, :].rearrange("p (b f) -> p b f", f=RW)
        rows = sb("rows", [P, HALVES, G, RW], f32)
        onehot = sb("onehot", [P, HALVES, G, P], f32)
        far = onehot[:, :, :, :].rearrange("p h g d -> p h (g d)").bitcast(bf16)
        ohT = sb("ohT", [P, G, P], f32)
        other = [sb(f"other{l}", [P, STEPS], u16) for l in range(2)]
        rel_key = [sb(f"rel_key{l}", [P, STEPS + G], i16) for l in range(2)]
        block_of = [sb(f"block_of{l}", [1, STEPS + G], i32) for l in range(2)]
        idx_slot = sb("idx_slot", [P, HALVES, G], u32)
        rec_slot = sb("rec_slot", [EP, HALVES, G, 2], i32)
        first_tile = [sb(f"first_tile{l}", [1, NB], i32) for l in range(2)]
        dinv = sb("dinv", [P, NB], f32)
        stat = sb("stat", [P, 4, NB], f32)
        deg = sb("deg", [P, NB], f32)
        has = sb("has", [P, 2, NB], f32)
        inv = sb("inv", [P, 2, NB], f32)
        M = sb("M", [P, NB, H], f32)
        T2 = sb("T2", [P, NB, 2 * H], f32)
        wself = sb("wself", [P, NB, H], f32)
        wtmp = sb("wtmp", [P, NB, H], f32)
        small = sb("small", [P, HALVES, G, H], f32)
        small2 = sb("small2", [P, HALVES, G, H], f32)
        tmax = sb("tmax", [P, G, H], f32)
        iota_row = sb("iota_row", [P, P], f32)
        ident = sb("ident", [P, P], f32)
        below = sb("below", [P, P], f32)
        far_ident = sb("far_ident", [P, H, P], bf16)
        ones = sb("ones", [P, P], f32)
        pad_rec = sb("pad_rec", [(ROWS - E) // 8, 8, 2], i32)
        step_cnt = sb("step_cnt", [P, 2], f32)
        cnt = sb("cnt", [P, 4, NB], f32)
        cnt_i = sb("cnt_i", [P, NB], i32)
        W_names = ["L0_gnn_W", "L1_gnn_W", "L2_gnn_W_in", "L2_gnn_W_out", "L3_gnn_W1", "L3_gnn_W2"]
        Wt = sb("Wt", [P, len(W_names), D], f32)
        wih = sb("wih", [P, 2, 3 * D], f32)
        whh = sb("whh", [P, 3 * D], f32)
        vec_names = ["L0_gnn_b", "L1_gnn_b", "L2_gnn_b_in", "L2_gnn_b_out", "L3_gnn_b1", "L3_gnn_g1", "L3_gnn_beta1",
                     "L3_gnn_b2", "L3_gnn_g2", "L3_gnn_beta2", "L3_gnn_a1_src", "L3_gnn_a1_dst", "L3_gnn_a2_src",
                     "L3_gnn_a2_dst"]
        vec = sb("vec", [P, len(vec_names), D], f32)

        def V(name):
            return vec[:, vec_names.index(name), :]

        def W(name):
            return Wt[:, W_names.index(name), :]

        gru_b = sb("gru_b", [1, 2, 3 * D], f32)
        gate_b = sb("gate_b", [1, 4 * D], f32)
        stage, stageT = (onehot[:, :, :, :].rearrange("p h g d -> p (h g d)")[:, t * MG * D:(t + 1) * MG * D]
                         .rearrange("p (k f) -> p k f", f=D) for t in range(2))
        a2 = sb("a2", [P, 2, D], f32)
        aT = sb("aT", [P, 2, D], f32)
        rz = sb("rz", [P, 2, D], f32)
        nn = sb("nn", [P, D], f32)
        gt = sb("gt", [P, D], f32)
        bn = ohT[:, 0:4, :]

        PS = ctx.enter_context(nc.psum_tensor("PS", [P, 8, 512], f32))

        s = {}
        for name in ["edges_loaded", "vec_loaded", "w_loaded", "x_loaded", "const_ready", "pad_ready", "pad_stored",
                     "counts_ready", "prefix_ready", "placed0", "placed1", "rec_copied", "rec_landed0", "rec_landed1",
                     "rec_issued", "scattered", "chunk_loaded", "chunk_split", "chunk_turned", "chunk_free",
                     "tables_ready", "idx_copied", "pool_turn", "rows_landed0", "rows_landed1", "rows_landed2", "rows_landed3",
                     "onehot_ready", "groups_done", "sums_used", "far_ready", "max_ready", "max_used", "spilled0",
                     "spilled1", "reload0", "reload1", "turned", "turn_copied", "expanded", "logits", "weights",
                     "weighted", "dve_chain", "var_ready", "sd_ready", "mm_src_ready", "stage_ready", "tr_done",
                     "stageT_ready", "mm_ready", "mm_used", "table_ready", "table_stored", "gru_src", "gru_stage",
                     "gru_tr", "gru_T", "gru_a", "gru_a2", "gru_a2T", "gru_aT", "gru_gates", "gru_rz", "gru_pre",
                     "gru_n", "gru_used", "bn_src", "bn_sum", "elu_src", "elu_exp", "self_logit", "self_w", "out_ready",
                     "out_stored", "act_turn", "dve_turn", "t2_ready", "deg_ready"]:
            s[name] = sem(name)

        block = ctx.enter_context(nc.Block())

        def need(eng, name, value):
            if not (isinstance(value, int) and value <= 0):
                eng.wait_ge(s[name], value)

        def pairs(eng, body, groups=GROUPS, peel_last=False):
            last = groups - HALVES if peel_last else groups
            for h in range(HALVES):
                body(h, h)
            with eng.Fori(HALVES, last - 1, HALVES) as g0:
                for h in range(HALVES):
                    body(g0 + h, h)
            for g in range(last, groups):
                body(g, g % HALVES)

        PASSES = [("deg", 0, None), ("agg", 0, 0), ("agg", 0, 1), ("agg", 0, 2), ("agg", 1, 2),
                  ("max", 0, 3), ("att", 0, None), ("max", 0, 4), ("att", 0, None)]
        PASSES = PASSES[0:{0: 1, 1: 2, 2: 3, 3: 5, 4: 7}.get(stop_after, 9)]
        gather_base = [GROUPS * sum(k in ("agg", "max") for k, _, _ in PASSES[:n]) for n in range(len(PASSES))]
        FIRST_MAX = 5
        max_base = [GROUPS * sum(k == "max" for k, _, _ in PASSES[:n]) for n in range(len(PASSES))]
        att_base = [GROUPS * sum(k == "att" for k, _, _ in PASSES[:n]) for n in range(len(PASSES))]

        def landed(n, g, h):
            return (g - h) * (16 * G // 2) + 16 * G * (landed_base(n) // 2 + 1)

        def landed_base(n):
            return gather_base[n] - (gather_base[FIRST_MAX] if n >= FIRST_MAX else 0)

        def landed_sem(n, h):
            return s[f"rows_landed{h + (2 if n >= FIRST_MAX else 0)}"]

        def spilled(n, g, h):
            return (g - h) * 8 + 16 * (max_base[n] // 2 + 1)

        def reloaded(n, g, h):
            return (g - h) * 8 + 16 * (att_base[n] // 2 + 1)

        ACCf = ACC[:, :, :].rearrange("p b f -> p (b f)")
        TABf = TAB[:, :, :].rearrange("p b f -> p (b f)")
        PSf = PS[:, :, :].rearrange("p b f -> p (b f)")
        src_i = ACCf[0:EP, 0:EC].bitcast(i32)
        dst_i = ACCf[0:EP, EC:2 * EC].bitcast(i32)
        key_block = ACCf[0:EP, 2 * EC:3 * EC]
        mask, scan, prod, pos = (U[0:EP, 0, t * EC:(t + 1) * EC] for t in range(4))
        rec = [TABf[0:EP, 2 * EC * l:2 * EC * (l + 1)].bitcast(i32).rearrange("p (j x) -> p j x", x=2) for l in range(2)]
        place = [onehot[0:EP, :, :, :].rearrange("p h g d -> p (h g d)")[:, 0:EC].bitcast(i32),
                 rows[0:EP, :, :, :].rearrange("p h g r -> p (h g r)")[:, 0:EC].bitcast(i32)]
        chunk = ACCf[:, 0:CH * 2 * P].bitcast(i32).rearrange("p (c r) -> p c r", r=2 * P)
        split = ACCf[:, CH * 2 * P:CH * 3 * P].rearrange("p (c e) -> p c e", e=P)
        tile_tab = U[:, 1, 0:2 * TILES]
        step_tab = U[:, 1, 2 * TILES:2 * TILES + STEPS + TILES]
        block_row = U[0:1, 0, 0:STEPS + TILES]
        zero_row = U[0:1, 0, STEPS + TILES:STEPS + 2 * TILES]

        def agg_slot(h, k):
            return PS[:, 3 * h + k // PER_BANK, (k % PER_BANK) * RW:(k % PER_BANK) * RW + RW]

        def exp_slot(k):
            return PS[:, 6, 2 * H * k:2 * H * (k + 1)]

        @block.sync
        def _(sp):
            for t, name in ((0, "src"), (1, "dst")):
                sp.dma_start((src_i, dst_i)[t],
                             a[name].rearrange("(p j) -> p j", p=EP)).then_inc(s["edges_loaded"], 16)
            for n, name in enumerate(vec_names):
                v = a[name]
                flat = v if len(v.shape) == 1 else v.rearrange("h f -> (h f)")
                sp.dma_start(vec[:, n, :], flat.partition_broadcast(P)).then_inc(s["vec_loaded"], 16)
            for n, name in enumerate(W_names):
                sp.dma_start(Wt[:, n, :], a[name]).then_inc(s["w_loaded"], 16)
            sp.dma_start(wih[:, :, :], a["L2_gnn_w_ih"].rearrange("(t p) n -> p t n", p=P)).then_inc(s["w_loaded"], 16)
            sp.dma_start(whh[:, :], a["L2_gnn_w_hh"]).then_inc(s["w_loaded"], 16)
            sp.dma_start(gru_b[:, 0, :], a["L2_gnn_b_ih"].rearrange("(o n) -> o n", o=1)).then_inc(s["w_loaded"], 16)
            sp.dma_start(gru_b[:, 1, :], a["L2_gnn_b_hh"].rearrange("(o n) -> o n", o=1)).then_inc(s["w_loaded"], 16)
            sp.wait_ge(s["pad_ready"], 3)
            sp.dma_start(X[:, 0:NB - 1, :], a["x"][0:(NB - 1) * P, :].rearrange("(b p) f -> p b f", p=P))\
              .then_inc(s["x_loaded"], 16)
            sp.dma_start(X[0:TAIL, NB - 1, :], a["x"][(NB - 1) * P:N, :]).then_inc(s["x_loaded"], 16)
            for l in range(2):
                sp.dma_start(list_d[l][E:ROWS, :].rearrange("(p j) x -> p j x", j=8), pad_rec[:, :, :])\
                  .then_inc(s["pad_stored"], 16)
            for l in range(2):
                sp.wait_ge(s["scattered"], l + 1)
                sp.wait_ge(s["pad_stored"], 32)
                sp.wait_ge(s["chunk_free"], l + 1)
                full = (CH - 1) * P * P
                sp.dma_start(chunk[:, 0:CH - 1, :],
                             list_d[l][0:full, :].rearrange("(c q e) x -> q c (e x)", q=P, e=P))\
                  .then_inc(s["chunk_loaded"], 16)
                sp.dma_start(chunk[0:TILES - (CH - 1) * P, CH - 1, :],
                             list_d[l][full:ROWS, :].rearrange("(q e) x -> q (e x)", e=P))\
                  .then_inc(s["chunk_loaded"], 16)

            def spill_at(g):
                return spill_d[g] if isinstance(g, int) else spill_d[ds(g, 1), :, :].rearrange("g p r -> (g p) r")

            for n, (kind, l, t) in enumerate(PASSES):
                if t is not None and l == 0:
                    sp.wait_ge(s["table_ready"], t + 1)
                    sp.dma_start(table_d[t].rearrange("(b p) f -> p b f", p=P), TAB[:, :, :])\
                      .then_inc(s["table_stored"], 16)
                if kind == "max":
                    def store(g, h):
                        sp.wait_ge(landed_sem(n, h), landed(n, g, h))
                        sp.dma_start(spill_at(g), rows[:, h, :, :].rearrange("p g r -> p (g r)"))\
                          .then_inc(s[f"spilled{h}"], 16)
                    pairs(sp, store)
                if kind == "att":
                    for h in range(HALVES):
                        sp.wait_ge(s[f"spilled{h}"], 8 * max_base[n])

                    def reload(g, h):
                        need(sp, "groups_done", n * GROUPS + g - 1)
                        sp.dma_start(rows[:, h, :, :].rearrange("p g r -> p (g r)"), spill_at(g))\
                          .then_inc(s[f"reload{h}"], 16)
                    pairs(sp, reload)
            sp.wait_ge(s["w_loaded"], 16 * (len(W_names) + 4))
            sp.wait_ge(s["out_ready"], 1)
            sp.dma_start(out[0:(NB - 1) * P, :].rearrange("(b p) f -> p b f", p=P), X[:, 0:NB - 1, :])\
              .then_inc(s["out_stored"], 16)
            sp.dma_start(out[(NB - 1) * P:N, :], X[0:TAIL, NB - 1, :]).then_inc(s["out_stored"], 16)
            sp.wait_ge(s["out_stored"], 32)


        @block.gpsimd
        def _(pool):
            g_ = nc.gpsimd
            g_.memset(X[:, NB - 1, :], 0.0).then_inc(s["pad_ready"], 1)
            g_.memset(pad_rec[:, :, 0:1], NO_KEY).then_inc(s["pad_ready"], 1)
            g_.memset(pad_rec[:, :, 1:2], 0).then_inc(s["pad_ready"], 1)
            g_.iota(iota_row[:, :], pattern=[[1, P]], base=0, channel_multiplier=0,
                    allow_small_or_imprecise_dtypes=True).then_inc(s["const_ready"], 1)
            g_.memset(ones[:, :], 1.0).then_inc(s["const_ready"], 1)
            g_.memset(ident[:, :], 0.0).then_inc(s["const_ready"], 1)
            g_.memset(below[:, :], 0.0).then_inc(s["const_ready"], 1)
            g_.memset(far_ident[:, :, :], 0.0).then_inc(s["const_ready"], 1)
            pool.wait_ge(s["const_ready"], 5)
            g_.affine_select(out=ident[:, :], in_=ident[:, :], compare_op=ALU.not_equal, fill=1.0, base=0,
                             pattern=[[-1, P]], channel_multiplier=1).then_inc(s["const_ready"], 1)
            g_.affine_select(out=below[:, :], in_=below[:, :], compare_op=ALU.is_ge, fill=1.0, base=0,
                             pattern=[[-1, P]], channel_multiplier=1).then_inc(s["const_ready"], 1)
            g_.affine_select(out=far_ident[:, :, :], in_=far_ident[:, :, :], compare_op=ALU.not_equal, fill=FAR,
                             base=0, pattern=[[0, H], [-1, P]], channel_multiplier=1).then_inc(s["const_ready"], 1)

            for l in range(2):
                pool.wait_ge(s[f"placed{l}"], 3)

                def scatter(g, h, l=l):
                    n_col = EC // G
                    if not (isinstance(g, int) and g + l * n_col < HALVES):
                        pool.wait_ge(s[f"rec_landed{h}"], (g - h) * 64 + l * n_col * 64)
                        pool.sem_inc(s["pool_turn"])
                    g_.tensor_copy(rec_slot[:, h, :, :], rec[l][:, ds(g * G, G), :]).then_inc(s["rec_copied"], 1)
                    g_.tensor_copy(idx_slot[0:EP, h, :], place[l][:, ds(g * G, G)]).then_inc(s["rec_copied"], 1)
                    pool.wait_ge(s["rec_copied"], g * 2 + (2 + l * n_col * 2))
                    pool.sem_inc(s["pool_turn"])
                    for k in range(G):
                        g_.indirect_dma_start(
                            out=list_d[l][:, :], out_offset=bass.IndirectOffsetOnAxis(ap=idx_slot[0:EP, h, k:k + 1], axis=0),
                            in_=rec_slot[:, h, k, :], in_offset=None).then_inc(s[f"rec_landed{h}"], 16)
                pairs(pool, scatter, EC // G)
                for h in range(HALVES):
                    pool.wait_ge(s[f"rec_landed{h}"], 64 * (EC // G) * (l + 1))
                pool.sem_inc(s["scattered"])

            for n, (kind, l, t) in enumerate(PASSES):
                if t is None:
                    continue
                if n == FIRST_MAX:
                    for h in range(HALVES):
                        pool.wait_ge(landed_sem(n - 1, h), 16 * G * gather_base[n] // 2)
                pool.wait_ge(s["table_stored"], 16 * (t + 1))
                pool.wait_ge(s["tables_ready"], l + 1)

                def gather(g, h, n=n, kind=kind, l=l, t=t):
                    if not (isinstance(g, int) and g + landed_base(n) < HALVES):
                        pool.wait_ge(landed_sem(n, h), (g - h) * (16 * G // 2) + 16 * G * (landed_base(n) // 2))
                        pool.sem_inc(s["pool_turn"])
                    g_.tensor_copy(idx_slot[:, h, :], other[l][:, ds(g * G, G)]).then_inc(s["idx_copied"], 1)
                    pool.wait_ge(s["idx_copied"], g + (gather_base[n] + 1))
                    pool.sem_inc(s["pool_turn"])
                    pool.wait_ge(s["groups_done"], g + (n * GROUPS - 1))
                    pool.sem_inc(s["pool_turn"])
                    if kind == "max" and not (isinstance(g, int) and g + max_base[n] < HALVES):
                        pool.wait_ge(s[f"spilled{h}"], (g - h) * 8 + 8 * max_base[n])
                        pool.sem_inc(s["pool_turn"])
                    for k in range(G):
                        g_.indirect_dma_start(
                            out=rows[:, h, k, :], out_offset=None, in_=table_d[t][:, :],
                            in_offset=bass.IndirectOffsetOnAxis(ap=idx_slot[:, h, k:k + 1], axis=0)).then_inc(landed_sem(n, h), 16)
                pairs(pool, gather)

        @block.scalar
        def _(act):
            c_ = nc.scalar
            sqrts = [0]

            def sqrt_of(ap):
                sqrts[0] += 1
                act.wait_ge(s["var_ready"], sqrts[0])
                c_.activation(ap, ap, ACT.Sqrt).then_inc(s["sd_ready"], 1)

            mms = [0]

            def dense_copies(src):
                n = mms[0]
                mms[0] += 1
                act.wait_ge(s["mm_src_ready"], n + 1)
                with act.Fori(0, NMG, 1) as g:
                    c_.activation(stage[:, :, :], src[:, ds(g * MG, MG), 0:D], ACT.Copy).then_inc(s["stage_ready"], 1)
                    act.wait_ge(s["tr_done"], g + (NMG * n + 1))
                    c_.activation(stageT[:, :, :].rearrange("p k f -> p (k f)"), PSf[:, 0:MG * D], ACT.Copy)\
                      .then_inc(s["stageT_ready"], 1)

            sqrt_of(stat[:, 0, :])
            if stop_after < 1:
                return
            sqrt_of(dinv[:, :])
            dense_copies(UA)
            if stop_after < 2:
                return
            sqrt_of(stat[:, 0, :])
            dense_copies(UA)
            if stop_after < 3:
                return
            sqrt_of(stat[:, 0, :])
            act.wait_ge(s["gru_src"], 1)
            with act.Fori(0, NB, 1) as b:
                c_.activation(stage[:, 0, :], TAB[:, ds(b, 1), 0:D], ACT.Copy).then_inc(s["gru_stage"], 1)
                c_.activation(stage[:, 1, :], ACC[:, ds(b, 1), 0:D], ACT.Copy).then_inc(s["gru_stage"], 1)
                c_.activation(stage[:, 2, :], ACC2[:, ds(b, 1), 0:D], ACT.Copy).then_inc(s["gru_stage"], 1)
                act.wait_ge(s["gru_tr"], b + 1)
                c_.activation(stageT[:, 0:3, :].rearrange("p k f -> p (k f)"), PS[:, 0, 0:3 * D], ACT.Copy)\
                  .then_inc(s["gru_T"], 1)
                act.wait_ge(s["gru_a2T"], b + 1)
                c_.activation(aT[:, :, :].rearrange("p k f -> p (k f)"), PS[:, 2, 0:2 * D], ACT.Copy)\
                  .then_inc(s["gru_aT"], 1)
                act.wait_ge(s["gru_gates"], b + 1)
                c_.activation(rz[:, :, :].rearrange("p k f -> p (k f)"), PS[:, 3, 0:2 * D], ACT.Sigmoid)\
                  .then_inc(s["gru_rz"], 1)
                act.wait_ge(s["gru_pre"], b + 1)
                c_.activation(nn[:, :], nn[:, :], ACT.Tanh).then_inc(s["gru_n"], 1)
            if stop_after < 4:
                return
            sqrt_of(stat[:, 0, :])
            atts = [n for n, (kind, _, _) in enumerate(PASSES) if kind == "att"]
            for j, n in enumerate(atts):
                dense_copies(UA)

                def turn(g):
                    act.wait_ge(s["turned"], g + (att_base[n] + 1))
                    if not (isinstance(g, int) and g + att_base[n] < 1):
                        act.wait_ge(s["expanded"], g + att_base[n])
                    c_.activation(ohT[:, :, :].rearrange("p k e -> p (k e)"), PSf[:, 6 * 512:6 * 512 + G * P], ACT.Copy)\
                      .then_inc(s["turn_copied"], 1)

                turn(0)

                def att(g, h):
                    act.wait_ge(s["logits"], g + (att_base[n] + 1))
                    c_.activation(rows[:, h, :, D:RW], small[:, h, :, :], ACT.Exp).then_inc(s["weights"], 1)
                    if not (isinstance(g, int) and g + 1 >= GROUPS):
                        turn(g + 1)
                pairs(act, att, peel_last=True)
                act.wait_ge(s["self_logit"], j + 1)
                c_.activation(wself[:, :, :], wtmp[:, :, :], ACT.Exp).then_inc(s["self_w"], 1)
                sqrt_of(bn[:, 2, :])
                act.wait_ge(s["elu_src"], j + 1)
                c_.activation(UB, UB, ACT.Exp).then_inc(s["elu_exp"], 1)

        @block.tensor
        def _(pe):
            t_ = nc.tensor
            pe.wait_ge(s["const_ready"], 8)
            for l in range(2):
                pe.wait_ge(s["counts_ready"], l + 1)
                t_.matmul(PS[0:EP, 0, 0:NB], ones[0:EP, 0:EP], cnt[0:EP, 0, :], start=True, stop=True)
                t_.matmul(PS[0:EP, 1, 0:NB], below[0:EP, 0:EP], cnt[0:EP, 0, :], start=True, stop=True)\
                  .then_inc(s["prefix_ready"], 1)

            def turn_tables(l):
                for x in range(2):
                    pe.wait_ge(s["chunk_split"], 4 * l + 2 * x + 2)
                    for c in range(CH):
                        n = min(P, TILES - c * P)
                        last = t_.transpose(PSf[:, c * P:c * P + n], split[0:n, c, :], ident[0:n, 0:n])
                    last.then_inc(s["chunk_turned"], 1)

            mms = [0]

            def dense(weight):
                n = mms[0]
                mms[0] += 1
                if n == 0:
                    pe.wait_ge(s["w_loaded"], 16 * (len(W_names) + 4))
                with pe.Fori(0, NMG, 1) as g:
                    pe.wait_ge(s["stage_ready"], g + (NMG * n + 1))
                    for k in range(MG):
                        last = t_.transpose(PSf[:, k * P:(k + 1) * P], stage[:, k, :], ident[:, :])
                    last.then_inc(s["tr_done"], 1)
                    pe.wait_ge(s["stageT_ready"], g + (NMG * n + 1))
                    pe.wait_ge(s["mm_used"], g + (NMG * n + 1))
                    for k in range(MG):
                        last = t_.matmul(PSf[:, 1024 + k * P:1024 + (k + 1) * P], stageT[:, k, :], weight,
                                         start=True, stop=True)
                    last.then_inc(s["mm_ready"], 1)

            def psum_free(n, g):
                need(pe, "sums_used", n * GROUPS if isinstance(g, int) and g < HALVES else g + (n * GROUPS - 1))

            def sum_pass(n, kind, l):
                def body(g, h):
                    pe.wait_ge(s["onehot_ready"], g + (n * GROUPS + 1))
                    if kind == "agg":
                        pe.wait_ge(landed_sem(n, h), landed(n, g, h))
                    psum_free(n, g)
                    for k in range(G):
                        if kind == "agg":
                            last = t_.matmul(agg_slot(h, k), onehot[:, h, k, :], rows[:, h, k, :], start=True, stop=True)
                        else:
                            last = t_.matmul(agg_slot(h, k)[:, 0:1], onehot[:, h, k, :], ones[:, 0:1],
                                             start=True, stop=True)
                    last.then_inc(s["groups_done"], 1)
                pairs(pe, body)

            def max_pass(n):
                def body(g, h):
                    pe.wait_ge(s["onehot_ready"], g + (n * GROUPS + 1))
                    pe.wait_ge(landed_sem(n, h), landed(n, g, h))
                    if isinstance(g, int) and g == 0:
                        psum_free(n, g)
                    for k in range(G):
                        if not (isinstance(g, int) and g + max_base[n] < 1):
                            pe.wait_ge(s["max_used"], g * G + ((max_base[n] - 1) * G + k + 1))
                        t_.matmul(PS[:, k, :], far[:, h, k * P:(k + 1) * P],
                                  far_ident[:, :, :].rearrange("p h e -> p (h e)"), start=True, stop=False)
                        for hd in range(H):
                            last = t_.matmul(PS[:, k, hd * P:(hd + 1) * P],
                                             rows[:, h, k, D + hd:D + hd + 1].broadcast_to([P, P]), ident[:, :],
                                             start=False, stop=(hd == H - 1))
                        last.then_inc(s["max_ready"], 1)
                    pe.wait_ge(s["max_ready"], g * G + (max_base[n] + 1) * G)
                    pe.sem_inc(s["groups_done"])
                pairs(pe, body)

            def att_pass(n):
                regs = [pe.alloc_register(f"pe_block{k}_{n}") for k in range(G)]

                def expand(g, h):
                    if isinstance(g, int) and g == 0:
                        psum_free(n, 0)
                    pe.wait_ge(s["onehot_ready"], g + (n * GROUPS + 1))
                    if not (isinstance(g, int) and g + att_base[n] < 1):
                        pe.wait_ge(s["logits"], g + att_base[n])
                    for k in range(G):
                        last = t_.transpose(PSf[:, 6 * 512 + k * P:6 * 512 + (k + 1) * P], onehot[:, h, k, :],
                                            ident[:, :])
                    last.then_inc(s["turned"], 1)
                    pe.load(regs, block_of[0][0:1, ds(g * G, G)])
                    blocks = [pe.snap(r, min_val=0, max_val=NB - 1) for r in regs]
                    pe.wait_ge(s["turn_copied"], g + (att_base[n] + 1))
                    for k in range(G):
                        last = t_.matmul(exp_slot(k), ohT[:, k, :], T2[:, ds(blocks[k], 1), :],
                                         start=True, stop=True)
                    last.then_inc(s["expanded"], 1)

                pe.wait_ge(s["t2_ready"], att_base[n] // GROUPS + 1)
                expand(0, 0)

                def body(g, h):
                    if not (isinstance(g, int) and g + 1 >= GROUPS):
                        expand(g + 1, 1 - h)
                    pe.wait_ge(s["weighted"], g + (att_base[n] + 1))
                    psum_free(n, g)
                    for k in range(G):
                        last = t_.matmul(agg_slot(h, k), onehot[:, h, k, :], rows[:, h, k, :], start=True, stop=True)
                    last.then_inc(s["groups_done"], 1)
                pairs(pe, body, peel_last=True)

            def column_sums(view, n):
                pe.wait_ge(s["bn_src"], n)
                flat = view.rearrange("p b f -> p (b f)")
                for c in range((NB - 1) // 4):
                    t_.matmul(PS[:, 6, :], ones[:, :], flat[:, c * 512:(c + 1) * 512], start=(c == 0), stop=False)
                t_.matmul(PS[:, 6, 0:D], ones[0:TAIL, :], view[0:TAIL, NB - 1, :], start=False, stop=True)\
                  .then_inc(s["bn_sum"], 1)

            turn_tables(0)
            sum_pass(0, "deg", 0)
            if stop_after < 1:
                return
            dense(W("L0_gnn_W"))
            turn_tables(1)
            sum_pass(1, "agg", 0)
            if stop_after < 2:
                return
            sum_pass(2, "agg", 0)
            dense(W("L1_gnn_W"))
            if stop_after < 3:
                return
            sum_pass(3, "agg", 0)
            sum_pass(4, "agg", 1)
            pe.wait_ge(s["gru_src"], 1)
            with pe.Fori(0, NB, 1) as b:
                pe.wait_ge(s["gru_stage"], b * 3 + 3)
                for k in range(3):
                    last = t_.transpose(PS[:, 0, k * P:(k + 1) * P], stage[:, k, :], ident[:, :])
                last.then_inc(s["gru_tr"], 1)
                pe.wait_ge(s["gru_T"], b + 1)
                t_.matmul(PS[:, 1, 0:D], stageT[:, 1, :], W("L2_gnn_W_in"), start=True, stop=True)
                t_.matmul(PS[:, 1, D:2 * D], stageT[:, 2, :], W("L2_gnn_W_out"), start=True, stop=True)\
                  .then_inc(s["gru_a"], 1)
                pe.wait_ge(s["gru_a2"], b + 1)
                for k in range(2):
                    last = t_.transpose(PS[:, 2, k * P:(k + 1) * P], a2[:, k, :], ident[:, :])
                last.then_inc(s["gru_a2T"], 1)
                t_.matmul(PS[:, 3, :], ones[0:1, :], gate_b[:, :], start=True, stop=False)
                t_.matmul(PS[:, 3, 0:2 * D], stageT[:, 0, :], whh[:, 0:2 * D], start=False, stop=False)
                t_.matmul(PS[:, 3, 3 * D:4 * D], stageT[:, 0, :], whh[:, 2 * D:3 * D], start=False, stop=False)
                pe.wait_ge(s["gru_aT"], b + 1)
                t_.matmul(PS[:, 3, 0:3 * D], aT[:, 0, :], wih[:, 0, :], start=False, stop=False)
                t_.matmul(PS[:, 3, 0:3 * D], aT[:, 1, :], wih[:, 1, :], start=False, stop=True)\
                  .then_inc(s["gru_gates"], 1)
            if stop_after < 4:
                return
            layers = sum(k == "att" for k, _, _ in PASSES)
            for j in range(layers):
                dense(W(f"L3_gnn_W{j + 1}"))
                max_pass(5 + 2 * j)
                att_pass(6 + 2 * j)
                column_sums(UA, 2 * j + 1)
                column_sums(UB, 2 * j + 2)

        @block.vector
        def _(dve):
            v_ = nc.vector
            chained = [0]

            def link(ins):
                chained[0] += 1
                ins.then_inc(s["dve_chain"], 1)
                dve.wait_ge(s["dve_chain"], chained[0])

            def looped(i, per):
                count = [0]
                start = chained[0]

                def link_in(ins):
                    count[0] += 1
                    assert count[0] <= per
                    ins.then_inc(s["dve_chain"], 1)
                    dve.wait_ge(s["dve_chain"], i * per + (start + count[0]))
                return link_in

            tick = dict(placed=0, var=0, mm=0, table=0)

            def place_list(l, key, oth):
                turn_i = mask.bitcast(i32)
                link(v_.tensor_scalar(turn_i, key, 7, None, ALU.arith_shift_right))
                link(v_.tensor_copy(key_block, turn_i))
                v_.tensor_copy(rec[l][:, :, 0], key).then_inc(s[f"placed{l}"], 1)
                v_.tensor_copy(rec[l][:, :, 1], oth).then_inc(s[f"placed{l}"], 1)
                with dve.Fori(0, NB, 1) as b:
                    lk = looped(b, 1)
                    lk(v_.tensor_scalar(mask, key_block, iota_row[0:EP, ds(b, 1)], 0.0, ALU.is_equal, ALU.add,
                                        accum_out=cnt[0:EP, 0, ds(b, 1)]))
                chained[0] += NB
                link(v_.memset(pos, -1.0))
                dve.sem_inc(s["counts_ready"])
                dve.wait_ge(s["prefix_ready"], l + 1)
                total, upto, start = (cnt[0:EP, t, :] for t in (1, 2, 3))
                link(v_.tensor_copy(total, PS[0:EP, 0, 0:NB]))
                link(v_.tensor_tensor_scan(upto, total, total, 0.0, ALU.add, ALU.max))
                link(v_.tensor_tensor(start, upto, total, ALU.subtract))
                link(v_.tensor_copy(cnt_i[0:1, :], start[0:1, :]))
                link(v_.tensor_scalar(first_tile[l][:, :], cnt_i[0:1, :], 7, None, ALU.arith_shift_right))
                link(v_.tensor_tensor(start, start, PS[0:EP, 1, 0:NB], ALU.add))
                with dve.Fori(0, NB, 1) as b:
                    lk = looped(b, 4)
                    lk(v_.tensor_scalar(mask, key_block, iota_row[0:EP, ds(b, 1)], None, ALU.is_equal))
                    lk(v_.tensor_tensor_scan(scan, mask, mask, cnt[0:EP, 3, ds(b, 1)], ALU.add, ALU.max))
                    lk(v_.tensor_tensor(prod, mask, scan, ALU.mult))
                    lk(v_.tensor_tensor(pos, pos, prod, ALU.add))
                chained[0] += 4 * NB
                v_.tensor_copy(place[l], pos).then_inc(s[f"placed{l}"], 1)
                dve.wait_ge(s[f"placed{l}"], 3)

            def step_tables(l):
                link(v_.memset(zero_row, 0.0))
                link(v_.memset(step_cnt[:, 0:2], 0.0))
                dve.wait_ge(s["chunk_loaded"], 32 * (l + 1))
                tail = TILES - (CH - 1) * P
                for x in range(2):
                    v_.tensor_copy(split[:, 0:CH - 1, :],
                                   chunk[:, 0:CH - 1, :].rearrange("p c (e x) -> p c e x", x=2)[:, :, :, x])\
                      .then_inc(s["chunk_split"], 1)
                    v_.tensor_copy(split[0:tail, CH - 1, :],
                                   chunk[0:tail, CH - 1, :].rearrange("p (e x) -> p e x", x=2)[:, :, x])\
                      .then_inc(s["chunk_split"], 1)
                    link(v_.memset(tile_tab[:, TILES:2 * TILES], 0.0 if x else float(NO_KEY)))
                    dve.wait_ge(s["chunk_turned"], 2 * l + x + 1)
                    link(v_.tensor_copy(tile_tab[:, 0:TILES], PSf[:, 0:TILES]))
                    with dve.Fori(0, NB, 1) as b:
                        lk = looped(b, 1 if x else 4)
                        t0 = dve.value_load(first_tile[l][0:1, ds(b, 1)], min_val=0, max_val=TILES - 1)
                        if x == 0:
                            lk(v_.tensor_scalar(step_tab[:, ds(t0 + b, TILES)], tile_tab[:, ds(t0, TILES)],
                                                step_cnt[:, 0:1], None, ALU.add))
                            lk(v_.tensor_scalar(block_row[:, ds(t0 + b, TILES)], zero_row, step_cnt[0:1, 1:2], None,
                                                ALU.add))
                            lk(v_.tensor_scalar(step_cnt[:, 0:1], step_cnt[:, 0:1], -float(P), None, ALU.add))
                            lk(v_.tensor_scalar(step_cnt[:, 1:2], step_cnt[:, 1:2], 1.0, None, ALU.add))
                        else:
                            lk(v_.tensor_scalar(step_tab[:, ds(t0 + b, TILES)], tile_tab[:, ds(t0, TILES)],
                                                0.0, None, ALU.add))
                    chained[0] += NB * (1 if x else 4)
                    if x == 0:
                        link(v_.tensor_copy(rel_key[l][:, 0:STEPS], step_tab[:, 0:STEPS]))
                        link(v_.tensor_copy(block_of[l][:, 0:STEPS], block_row[:, 0:STEPS]))
                    else:
                        link(v_.tensor_copy(other[l][:, :], step_tab[:, 0:STEPS]))
                dve.sem_inc(s["tables_ready"])

            def over_nodes(v):
                return v.unsqueeze(1).broadcast_to([P, NB, D])

            def over_features(st):
                return st.unsqueeze(2).broadcast_to([P, NB, D])

            def sqrt_by_act():
                tick["var"] += 1
                dve.sem_inc(s["var_ready"])
                dve.wait_ge(s["sd_ready"], tick["var"])

            def norm_relu(dst):
                var, mean = stat[:, 0, :], stat[:, 1, :]
                link(v_.tensor_reduce(mean, X[:, :, :], AX.X, ALU.add))
                link(v_.tensor_scalar(mean, mean, 1.0 / D, None, ALU.mult))
                link(v_.tensor_tensor(dst, X[:, :, :], over_features(mean), ALU.subtract))
                link(v_.tensor_tensor(UB, dst, dst, ALU.mult))
                link(v_.tensor_reduce(var, UB, AX.X, ALU.add))
                link(v_.tensor_scalar(var, var, 1.0 / D, EPS, ALU.mult, ALU.add))
                sqrt_by_act()
                link(v_.reciprocal(mean, var))
                link(v_.scalar_tensor_tensor(dst, dst, 0.0, over_features(mean), ALU.max, ALU.mult))

            def dense_results(take):
                n = tick["mm"]
                tick["mm"] += 1
                dve.sem_inc(s["mm_src_ready"])
                with dve.Fori(0, NMG, 1) as g:
                    dve.wait_ge(s["mm_ready"], g + (NMG * n + 1))
                    take(PSf[:, 1024:1024 + MG * D].rearrange("p (k f) -> p k f", f=D), ds(g * MG, MG))\
                        .then_inc(s["mm_used"], 1)
                dve.wait_ge(s["mm_used"], NMG * (n + 1) + 1)

            regs = [dve.alloc_register(f"dve_block{k}") for k in range(G)]

            def blocks_of(l, g):
                dve.sem_inc(s["dve_turn"])
                dve.load(regs, block_of[l][0:1, ds(g * G, G)])
                return [dve.snap(r, min_val=0, max_val=NB - 1) for r in regs]

            def make_onehot(n, l, g, h, op=ALU.is_equal):
                need(dve, "groups_done", n * GROUPS + g - 1 if isinstance(g, int) else g + (n * GROUPS - 1))
                out = onehot[:, h, :, :] if op == ALU.is_equal else \
                    far[:, h, 0:G * P].rearrange("p (g d) -> p g d", d=P)
                v_.tensor_tensor(out, iota_row[:, :].unsqueeze(1).broadcast_to([P, G, P]),
                                 rel_key[l][:, ds(g * G, G)].unsqueeze(2).broadcast_to([P, G, P]), op)\
                  .then_inc(s["onehot_ready"], 1)

            def add_sums(n, l, g, h, acc, width, lk):
                dve.wait_ge(s["groups_done"], g + (n * GROUPS + 1))
                for k, b in enumerate(blocks_of(l, g)):
                    if width == 1:
                        lk(v_.tensor_tensor(acc[:, ds(b, 1)], acc[:, ds(b, 1)], agg_slot(h, k)[:, 0:1], ALU.add))
                    else:
                        lk(v_.tensor_tensor(acc[:, ds(b, 1), :], acc[:, ds(b, 1), :], agg_slot(h, k).unsqueeze(1),
                                            ALU.add))
                dve.sem_inc(s["sums_used"])

            def sum_pass(n, l, acc, width=RW):
                def body(g, h):
                    make_onehot(n, l, g, h)
                    add_sums(n, l, g, h, acc, width, looped(g, G))
                pairs(dve, body)
                chained[0] += GROUPS * G

            def max_pass(n):
                def body(g, h):
                    make_onehot(n, 0, g, h, ALU.not_equal)
                    for k in range(G):
                        dve.wait_ge(s["max_ready"], g * G + (max_base[n] * G + k + 1))
                        v_.tensor_reduce(tmax[:, k, :], PS[:, k, :].rearrange("p (h e) -> p h e", e=P), AX.X, ALU.max)\
                          .then_inc(s["max_used"], 1)
                    dve.wait_ge(s["max_used"], g * G + (max_base[n] + 1) * G)
                    lk = looped(g, G)
                    for k, b in enumerate(blocks_of(0, g)):
                        lk(v_.tensor_tensor(M[:, ds(b, 1), :], M[:, ds(b, 1), :], tmax[:, k, :].unsqueeze(1), ALU.max))
                    dve.sem_inc(s["sums_used"])
                pairs(dve, body)
                chained[0] += GROUPS * G

            def att_pass(n):
                PER = 3 + G
                make_onehot(n, 0, 0, 0)

                def body(g, h):
                    if not (isinstance(g, int) and g + 1 >= GROUPS):
                        make_onehot(n, 0, g + 1, 1 - h)
                    first = looped(g, PER)
                    terms = PS[:, 6, 0:2 * H * G].rearrange("p (g t) -> p g t", t=2 * H)
                    dve.wait_ge(s["expanded"], g + (att_base[n] + 1))
                    dve.wait_ge(s[f"reload{h}"], reloaded(n, g, h))
                    first(v_.tensor_tensor(small[:, h, :, :], rows[:, h, :, D:RW], terms[:, :, 0:H], ALU.add))
                    first(v_.scalar_tensor_tensor(small2[:, h, :, :], small[:, h, :, :], SLOPE, small[:, h, :, :],
                                                  ALU.mult, ALU.max))
                    first(v_.tensor_tensor(small[:, h, :, :], small2[:, h, :, :], terms[:, :, H:2 * H], ALU.subtract))
                    dve.sem_inc(s["logits"])
                    if isinstance(g, int) and g == 0:
                        dve.sem_inc(s["dve_chain"], G)
                    else:
                        add_sums(n, 0, g - 1, 1 - h, ACC, RW, first)
                    dve.wait_ge(s["weights"], g + (att_base[n] + 1))
                    feats = rows[:, h, :, 0:D].rearrange("p g (h f) -> p g h f", f=FH)
                    v_.tensor_tensor(feats, feats, rows[:, h, :, D:RW].unsqueeze(3).broadcast_to([P, G, H, FH]),
                                     ALU.mult).then_inc(s["weighted"], 1)
                pairs(dve, body, peel_last=True)
                chained[0] += GROUPS * PER
                add_sums(n, 0, GROUPS - 1, (GROUPS - 1) % HALVES, ACC, RW, link)

            dve.wait_ge(s["const_ready"], 8)
            dve.wait_ge(s["edges_loaded"], 32)
            dve.sem_inc(s["mm_used"])
            place_list(0, dst_i, src_i)
            place_list(1, src_i, dst_i)
            dve.sem_inc(s["chunk_free"])
            step_tables(0)
            dve.sem_inc(s["chunk_free"])
            dve.wait_ge(s["x_loaded"], 32)
            norm_relu(UA)
            link(v_.memset(deg[:, :], 0.0))
            sum_pass(0, 0, deg, 1)
            dve.wait_ge(s["vec_loaded"], 16 * len(vec_names))

            def finish():
                dve.sem_inc(s["out_ready"])

            if stop_after < 1:
                link(v_.tensor_tensor(X[:, :, :], UA, over_features(deg[:, :]), ALU.add))
                return finish()

            link(v_.tensor_scalar(dinv[:, :], deg[:, :], 1.0, None, ALU.add))
            sqrt_by_act()
            link(v_.reciprocal(stat[:, 2, :], dinv[:, :]))
            link(v_.tensor_copy(dinv[:, :], stat[:, 2, :]))
            dve.wait_ge(s["scattered"], 2)
            link(v_.memset(TAB[:, :, D:RW], 1.0))

            def scaled(ps, blk):
                return v_.tensor_tensor(TAB[:, blk, 0:D], ps, dinv[:, blk].unsqueeze(2).broadcast_to([P, MG, D]),
                                        ALU.mult)
            dense_results(scaled)
            dve.sem_inc(s["table_ready"])
            step_tables(1)
            link(v_.memset(ACC[:, :, :], 0.0))
            sum_pass(1, 0, ACC)
            link(v_.tensor_tensor(UA, ACC[:, :, 0:D], TAB[:, :, 0:D], ALU.add))
            link(v_.tensor_tensor(UA, UA, over_features(dinv[:, :]), ALU.mult))
            link(v_.tensor_tensor(UA, UA, over_nodes(V("L0_gnn_b")), ALU.add))
            link(v_.scalar_tensor_tensor(X[:, :, :], UA, 0.0, X[:, :, :], ALU.max, ALU.add))
            if stop_after < 2:
                return finish()

            norm_relu(TAB[:, :, 0:D])
            dve.sem_inc(s["table_ready"])
            link(v_.memset(ACC[:, :, :], 0.0))
            sum_pass(2, 0, ACC)
            link(v_.tensor_tensor(UA, ACC[:, :, 0:D], TAB[:, :, 0:D], ALU.add))
            dense_results(lambda ps, blk: v_.tensor_tensor(X[:, blk, :], X[:, blk, :], ps, ALU.add))
            link(v_.tensor_tensor(X[:, :, :], X[:, :, :], over_nodes(V("L1_gnn_b")), ALU.add))
            if stop_after < 3:
                return finish()

            norm_relu(TAB[:, :, 0:D])
            dve.sem_inc(s["table_ready"])
            link(v_.memset(ACC[:, :, :], 0.0))
            link(v_.memset(ACC2, 0.0))
            sum_pass(3, 0, ACC)
            sum_pass(4, 1, ACC2)
            for t, acc in ((0, ACC[:, :, :]), (1, ACC2)):
                link(v_.tensor_scalar(has[:, t, :], acc[:, :, D], 1.0, None, ALU.min))
                link(v_.tensor_scalar(stat[:, 2, :], acc[:, :, D], 1.0, None, ALU.max))
                link(v_.reciprocal(inv[:, t, :], stat[:, 2, :]))
                link(v_.tensor_tensor(acc[:, :, 0:D], acc[:, :, 0:D], over_features(inv[:, t, :]), ALU.mult))
            link(v_.tensor_tensor(gate_b[:, 0:2 * D], gru_b[:, 0, 0:2 * D], gru_b[:, 1, 0:2 * D], ALU.add))
            link(v_.tensor_copy(gate_b[:, 2 * D:3 * D], gru_b[:, 0, 2 * D:3 * D]))
            link(v_.tensor_copy(gate_b[:, 3 * D:4 * D], gru_b[:, 1, 2 * D:3 * D]))
            dve.sem_inc(s["gru_src"])
            with dve.Fori(0, NB, 1) as b:
                lk = looped(b, 8)
                dve.wait_ge(s["gru_a"], b + 1)
                for t, name in ((0, "L2_gnn_b_in"), (1, "L2_gnn_b_out")):
                    lk(v_.scalar_tensor_tensor(a2[:, t, :], V(name), has[:, t, ds(b, 1)], PS[:, 1, t * D:(t + 1) * D],
                                               ALU.mult, ALU.add))
                dve.sem_inc(s["gru_a2"])
                dve.wait_ge(s["gru_rz"], b + 1)
                lk(v_.tensor_tensor(gt[:, :], rz[:, 0, :], PS[:, 3, 3 * D:4 * D], ALU.mult))
                lk(v_.tensor_tensor(nn[:, :], gt[:, :], PS[:, 3, 2 * D:3 * D], ALU.add))
                dve.sem_inc(s["gru_pre"])
                dve.wait_ge(s["gru_n"], b + 1)
                lk(v_.tensor_tensor(gt[:, :].unsqueeze(1), TAB[:, ds(b, 1), 0:D], nn[:, :].unsqueeze(1), ALU.subtract))
                lk(v_.tensor_tensor(gt[:, :], gt[:, :], rz[:, 1, :], ALU.mult))
                lk(v_.tensor_tensor(gt[:, :], gt[:, :], nn[:, :], ALU.add))
                lk(v_.tensor_tensor(X[:, ds(b, 1), :], X[:, ds(b, 1), :], gt[:, :].unsqueeze(1), ALU.add))
            chained[0] += 8 * NB
            if stop_after < 4:
                return finish()

            norm_relu(UA)
            layers = sum(k == "att" for k, _, _ in PASSES)
            for j in range(layers):
                p = f"L3_gnn_"
                dense_results(lambda ps, blk: v_.tensor_copy(TAB[:, blk, 0:D], ps))
                heads = UA.rearrange("p b (h f) -> p b h f", f=FH)
                link(v_.tensor_tensor(UA, TAB[:, :, 0:D], over_nodes(V(f"{p}a{j + 1}_src")), ALU.mult))
                link(v_.tensor_reduce(TAB[:, :, D:RW], heads, AX.X, ALU.add))
                dve.sem_inc(s["table_ready"])
                link(v_.tensor_tensor(UA, TAB[:, :, 0:D], over_nodes(V(f"{p}a{j + 1}_dst")), ALU.mult))
                link(v_.tensor_reduce(T2[:, :, 0:H], heads, AX.X, ALU.add))
                link(v_.memset(M[:, :, :], FAR))
                max_pass(5 + 2 * j)
                link(v_.tensor_tensor(M[:, :, :], M[:, :, :], TAB[:, :, D:RW], ALU.max))
                link(v_.tensor_tensor(M[:, :, :], M[:, :, :], T2[:, :, 0:H], ALU.add))
                link(v_.scalar_tensor_tensor(T2[:, :, H:2 * H], M[:, :, :], SLOPE, M[:, :, :], ALU.mult, ALU.max))
                link(v_.memset(ACC[:, :, :], 0.0))
                dve.sem_inc(s["t2_ready"])
                att_pass(6 + 2 * j)
                link(v_.tensor_tensor(wtmp[:, :, :], TAB[:, :, D:RW], T2[:, :, 0:H], ALU.add))
                link(v_.scalar_tensor_tensor(wself[:, :, :], wtmp[:, :, :], SLOPE, wtmp[:, :, :], ALU.mult, ALU.max))
                link(v_.tensor_tensor(wtmp[:, :, :], wself[:, :, :], T2[:, :, H:2 * H], ALU.subtract))
                dve.sem_inc(s["self_logit"])
                dve.wait_ge(s["self_w"], j + 1)
                wide = wself[:, :, :].unsqueeze(3).broadcast_to([P, NB, H, FH])
                link(v_.tensor_tensor(heads, TAB[:, :, 0:D].rearrange("p b (h f) -> p b h f", f=FH), wide, ALU.mult))
                link(v_.tensor_tensor(UA, UA, ACC[:, :, 0:D], ALU.add))
                link(v_.tensor_tensor(wtmp[:, :, :], wself[:, :, :], ACC[:, :, D:RW], ALU.add))
                link(v_.reciprocal(wself[:, :, :], wtmp[:, :, :]))
                link(v_.tensor_tensor(heads, heads, wide, ALU.mult))
                link(v_.tensor_tensor(UA, UA, over_nodes(V(f"{p}b{j + 1}")), ALU.add))
                sums = PS[:, 6, :].rearrange("p (k f) -> p f k", f=D)
                dve.sem_inc(s["bn_src"])
                dve.wait_ge(s["bn_sum"], 2 * j + 1)
                link(v_.tensor_reduce(bn[:, 0, :], sums, AX.X, ALU.add))
                link(v_.tensor_scalar(bn[:, 1, :], bn[:, 0, :], 1.0 / N, None, ALU.mult))
                link(v_.tensor_tensor(UA, UA, over_nodes(bn[:, 1, :]), ALU.subtract))
                link(v_.tensor_tensor(UB, UA, UA, ALU.mult))
                dve.sem_inc(s["bn_src"])
                dve.wait_ge(s["bn_sum"], 2 * j + 2)
                link(v_.tensor_reduce(bn[:, 0, :], sums, AX.X, ALU.add))
                link(v_.tensor_scalar(bn[:, 2, :], bn[:, 0, :], 1.0 / N, EPS, ALU.mult, ALU.add))
                sqrt_by_act()
                link(v_.reciprocal(bn[:, 0, :], bn[:, 2, :]))
                link(v_.tensor_tensor(bn[:, 3, :], bn[:, 0, :], V(f"{p}g{j + 1}"), ALU.mult))
                link(v_.tensor_tensor(UA, UA, over_nodes(bn[:, 3, :]), ALU.mult))
                link(v_.tensor_tensor(UA, UA, over_nodes(V(f"{p}beta{j + 1}")), ALU.add))
                link(v_.tensor_scalar(UB, UA, 0.0, None, ALU.min))
                dve.sem_inc(s["elu_src"])
                dve.wait_ge(s["elu_exp"], j + 1)
                link(v_.tensor_scalar(UB, UB, -1.0, None, ALU.add))
                link(v_.scalar_tensor_tensor(UA, UA, 0.0, UB, ALU.max, ALU.add))
            link(v_.tensor_tensor(X[:, :, :], X[:, :, :], UA, ALU.add))
            finish()


_INS = ["x", "src", "dst", "L0_gnn_W", "L0_gnn_b", "L1_gnn_W", "L1_gnn_b", "L2_gnn_W_in", "L2_gnn_b_in",
        "L2_gnn_W_out", "L2_gnn_b_out", "L2_gnn_w_ih", "L2_gnn_w_hh", "L2_gnn_b_ih", "L2_gnn_b_hh", "L3_gnn_W1",
        "L3_gnn_a1_src", "L3_gnn_a1_dst", "L3_gnn_b1", "L3_gnn_g1", "L3_gnn_beta1", "L3_gnn_W2", "L3_gnn_a2_src",
        "L3_gnn_a2_dst", "L3_gnn_b2", "L3_gnn_g2", "L3_gnn_beta2"]
_TRANSPOSED = {"L1_gnn_W", "L2_gnn_W_in", "L2_gnn_W_out", "L2_gnn_w_ih", "L2_gnn_w_hh"}


def kernel(**inputs):
    import numpy as _np
    import concourse.bacc as _bacc
    from concourse import mybir as _mybir
    from concourse.bass_utils import run_bass_kernel_spmd as _run

    nc = _bacc.Bacc("TRN2", target_bir_lowering=False, num_devices=1)
    arrays, aps = {}, {}
    for name in _INS:
        a = _np.asarray(inputs[name])
        a = _np.ascontiguousarray(a.T if name in _TRANSPOSED else a)
        arrays[f"in_{name}_dram"] = a
        aps[name] = nc.dram_tensor(f"in_{name}_dram", a.shape, _mybir.dt.from_np(a.dtype), kind="ExternalInput").ap()
    out = nc.dram_tensor("out_dram", aps["x"].shape, _mybir.dt.float32, kind="ExternalOutput").ap()
    gnn_kernel(nc, aps, out)
    return _run(nc, [arrays], core_ids=[0]).results[0]["out_dram"]
```

```python
import concourse.bass as bass
from concourse import mybir
from contextlib import ExitStack


def gnn_kernel(nc, a, out, stop_after=9):
    f32, bf16 = mybir.dt.float32, mybir.dt.bfloat16
    i32, u32, i16, u16 = mybir.dt.int32, mybir.dt.uint32, mybir.dt.int16, mybir.dt.uint16
    ALU, ACT, AX = mybir.AluOpType, mybir.ActivationFunctionType, mybir.AxisListType
    ds = bass.ds

    P = 128
    N, D = a["x"].shape
    E = a["src"].shape[0]
    NB = -(-N // P)
    NP = NB * P
    TAIL = N - (NB - 1) * P
    H, FH = a["L3_gnn_a1_src"].shape
    EPS = 1e-5
    SLOPE = 0.2
    SPLIT = 3
    RW = D + H
    RT = RW + SPLIT * H // 2
    G = 8
    HALVES = 2
    TILES = -(-E // P)
    STEPS = -(-(TILES + NB - 1) // (G * HALVES)) * G * HALVES
    TILES = STEPS - NB + 1
    GROUPS = STEPS // G
    ROWS = TILES * P
    EP = 125
    EC = E // EP
    assert EP * EC == E and EC % (2 * G) == 0
    CH = -(-TILES // P)
    NO_KEY = 20000
    FAR = -1.0e30
    MG = 7
    NMG = NB // MG
    assert MG * NMG == NB
    PER_BANK = 3
    MAXB = 4

    def dram(name, shape, dt):
        return nc.dram_tensor(name, shape, dt, kind="Internal").ap()

    list_d = [dram(f"edge_list{l}", [ROWS, 2], i32) for l in range(2)]
    table_d = [dram(f"table{k}", [NP, RT], f32) for k in range(5)]
    spill_d = dram("gathered_rows", [GROUPS, P, G * RT], f32)

    ctx = ExitStack()
    with ctx:
        def sb(name, shape, dt):
            return ctx.enter_context(nc.sbuf_tensor(name, shape, dt))

        def sem(name):
            return ctx.enter_context(nc.semaphore(name))

        X = sb("X", [P, NB, D], f32)
        TAB = sb("TAB", [P, NB, RT], f32)
        ACC = sb("ACC", [P, NB, RW], f32)
        U = sb("U", [P, 2, NB * RW], f32)
        UA = U[:, 0, 0:NB * D].rearrange("p (b f) -> p b f", f=D)
        UB = U[:, 1, 0:NB * D].rearrange("p (b f) -> p b f", f=D)
        ACC2 = U[:, 1, :].rearrange("p (b f) -> p b f", f=RW)
        ACC_ODD = U[:, 0, :].rearrange("p (b f) -> p b f", f=RW)
        rows = sb("rows", [P, HALVES, G, RT], f32)
        onehot = sb("onehot", [P, HALVES, G, P], f32)
        far = onehot[:, :, :, :].rearrange("p h g d -> p h (g d)").bitcast(bf16)
        ohT = sb("ohT", [P, G, P], bf16)
        other = [sb(f"other{l}", [P, STEPS], u16) for l in range(2)]
        rel_key = [sb(f"rel_key{l}", [P, STEPS + G], i16) for l in range(2)]
        block_of = [sb(f"block_of{l}", [1, STEPS + G], i32) for l in range(2)]
        idx_slot = sb("idx_slot", [P, HALVES, G], u32)
        rec_slot = sb("rec_slot", [EP, HALVES, G, 2], i32)
        first_tile = [sb(f"first_tile{l}", [1, NB], i32) for l in range(2)]
        dinv = sb("dinv", [P, NB], f32)
        stat = sb("stat", [P, 4, NB], f32)
        deg = sb("deg", [P, NB], f32)
        has = sb("has", [P, 2, NB], f32)
        inv = sb("inv", [P, 2, NB], f32)
        M = sb("M", [P, 2, NB, H], f32)
        T2 = sb("T2", [P, NB, 2 * H], f32)
        T2s = U[:, 1, 0:NB * SPLIT * H].bitcast(bf16).rearrange("p (b s t) -> p b s t", s=SPLIT, t=2 * H)
        headT = U[0:SPLIT, 0, 0:G * H * P // 2].bitcast(bf16).rearrange("p (q r) -> p q r", q=G // 2)
        terms = sb("terms", [P, G, 2 * H], f32)
        wself = sb("wself", [P, NB, H], f32)
        wtmp = sb("wtmp", [P, NB, H], f32)
        small = sb("small", [P, HALVES, G, H], f32)
        small2 = sb("small2", [P, HALVES, G, H], f32)
        tmax = sb("tmax", [P, G, H], f32)
        iota_row = sb("iota_row", [P, P], f32)
        ident = sb("ident", [P, P], f32)
        below = sb("below", [P, P], f32)
        far_ident = sb("far_ident", [P, H, P], bf16)
        ones = sb("ones", [P, P], f32)
        ones_b = sb("ones_b", [SPLIT, P], bf16)
        ident_b = sb("ident_b", [P, P], bf16)
        pad_rec = sb("pad_rec", [(ROWS - E) // 8, 8, 2], i32)
        step_cnt = sb("step_cnt", [P, 2], f32)
        cnt = sb("cnt", [P, 4, NB], f32)
        cnt_i = sb("cnt_i", [P, NB], i32)
        W_names = ["L0_gnn_W", "L1_gnn_W", "L2_gnn_W_in", "L2_gnn_W_out", "L3_gnn_W1", "L3_gnn_W2"]
        Wt = sb("Wt", [P, len(W_names), D], f32)
        wih = sb("wih", [P, 2, 3 * D], f32)
        whh = sb("whh", [P, 3 * D], f32)
        vec_names = ["L0_gnn_b", "L1_gnn_b", "L2_gnn_b_in", "L2_gnn_b_out", "L3_gnn_b1", "L3_gnn_g1", "L3_gnn_beta1",
                     "L3_gnn_b2", "L3_gnn_g2", "L3_gnn_beta2", "L3_gnn_a1_src", "L3_gnn_a1_dst", "L3_gnn_a2_src",
                     "L3_gnn_a2_dst"]
        vec = sb("vec", [P, len(vec_names), D], f32)

        def V(name):
            return vec[:, vec_names.index(name), :]

        def W(name):
            return Wt[:, W_names.index(name), :]

        gru_b = sb("gru_b", [1, 2, 3 * D], f32)
        gate_b = sb("gate_b", [1, 4 * D], f32)
        stage, stageT = (onehot[:, :, :, :].rearrange("p h g d -> p (h g d)")[:, t * MG * D:(t + 1) * MG * D]
                         .rearrange("p (k f) -> p k f", f=D) for t in range(2))
        a2 = sb("a2", [P, 2, D], f32)
        aT = sb("aT", [P, 2, D], f32)
        rz = sb("rz", [P, 2, D], f32)
        nn = sb("nn", [P, D], f32)
        gt = sb("gt", [P, D], f32)
        bn = ohT[:, :, :].rearrange("p g d -> p (g d)").bitcast(f32).rearrange("p (g d) -> p g d", d=P)

        PS = ctx.enter_context(nc.psum_tensor("PS", [P, 8, 512], f32))

        s = {}
        for name in ["edges_loaded", "vec_loaded", "w_loaded", "x_loaded", "const_ready", "pad_ready", "pad_stored",
                     "counts_ready", "prefix_ready", "placed0", "placed1", "rec_copied", "rec_landed0", "rec_landed1",
                     "rec_issued", "scattered", "chunk_loaded", "chunk_split", "chunk_turned", "chunk_free",
                     "tables_ready", "idx_copied", "pool_turn", "rows_landed0", "rows_landed1", "rows_landed2", "rows_landed3",
                     "onehot_ready", "groups_done", "sums_used", "far_ready", "max_ready", "max_used", "spilled0",
                     "spilled1", "reload0", "reload1", "turned", "turn_copied", "heads_turned", "heads_copied", "expanded", "logits", "weights",
                     "weighted", "dve_chain", "var_ready", "sd_ready", "mm_src_ready", "stage_ready", "tr_done",
                     "stageT_ready", "mm_ready", "mm_used", "table_ready", "table_stored", "gru_src", "gru_stage",
                     "gru_tr", "gru_T", "gru_a", "gru_a2", "gru_a2T", "gru_aT", "gru_gates", "gru_rz", "gru_pre",
                     "gru_n", "gru_used", "bn_src", "bn_sum", "elu_src", "elu_exp", "self_logit", "self_w", "out_ready",
                     "out_stored", "act_turn", "dve_turn", "t2_ready", "deg_ready"]:
            s[name] = sem(name)

        block = ctx.enter_context(nc.Block())

        def need(eng, name, value):
            if not (isinstance(value, int) and value <= 0):
                eng.wait_ge(s[name], value)

        def pairs(eng, body, groups=GROUPS, peel_last=False):
            last = groups - HALVES if peel_last else groups
            for h in range(HALVES):
                body(h, h)
            with eng.Fori(HALVES, last - 1, HALVES) as g0:
                for h in range(HALVES):
                    body(g0 + h, h)
            for g in range(last, groups):
                body(g, g % HALVES)

        PASSES = [("deg", 0, None), ("agg", 0, 0), ("agg", 0, 1), ("agg", 0, 2), ("agg", 1, 2),
                  ("max", 0, 3), ("att", 0, None), ("max", 0, 4), ("att", 0, None)]
        PASSES = PASSES[0:{0: 1, 1: 2, 2: 3, 3: 5, 4: 7}.get(stop_after, 9)]
        gather_base = [GROUPS * sum(k in ("agg", "max") for k, _, _ in PASSES[:n]) for n in range(len(PASSES))]
        FIRST_MAX = 5
        max_base = [GROUPS * sum(k == "max" for k, _, _ in PASSES[:n]) for n in range(len(PASSES))]
        att_base = [GROUPS * sum(k == "att" for k, _, _ in PASSES[:n]) for n in range(len(PASSES))]

        def landed(n, g, h):
            return (g - h) * (16 * G // 2) + 16 * G * (landed_base(n) // 2 + 1)

        def landed_base(n):
            return gather_base[n] - (gather_base[FIRST_MAX] if n >= FIRST_MAX else 0)

        def landed_sem(n, h):
            return s[f"rows_landed{h + (2 if n >= FIRST_MAX else 0)}"]

        def spilled(n, g, h):
            return (g - h) * 8 + 16 * (max_base[n] // 2 + 1)

        def reloaded(n, g, h):
            return (g - h) * 8 + 16 * (att_base[n] // 2 + 1)

        ACCf = ACC[:, :, :].rearrange("p b f -> p (b f)")
        TABf = TAB[:, :, :].rearrange("p b f -> p (b f)")
        PSf = PS[:, :, :].rearrange("p b f -> p (b f)")
        src_i = ACCf[0:EP, 0:EC].bitcast(i32)
        dst_i = ACCf[0:EP, EC:2 * EC].bitcast(i32)
        key_block = ACCf[0:EP, 2 * EC:3 * EC]
        mask, scan, prod, pos = (U[0:EP, 0, t * EC:(t + 1) * EC] for t in range(4))
        rec = [TABf[0:EP, 2 * EC * l:2 * EC * (l + 1)].bitcast(i32).rearrange("p (j x) -> p j x", x=2) for l in range(2)]
        place = [onehot[0:EP, :, :, :].rearrange("p h g d -> p (h g d)")[:, 0:EC].bitcast(i32),
                 rows[0:EP, :, :, :].rearrange("p h g r -> p (h g r)")[:, 0:EC].bitcast(i32)]
        chunk = ACCf[:, 0:CH * 2 * P].bitcast(i32).rearrange("p (c r) -> p c r", r=2 * P)
        split = ACCf[:, CH * 2 * P:CH * 3 * P].rearrange("p (c e) -> p c e", e=P)
        tile_tab = U[:, 1, 0:2 * TILES]
        step_tab = U[:, 1, 2 * TILES:2 * TILES + STEPS + TILES]
        block_row = U[0:1, 0, 0:STEPS + TILES]
        zero_row = U[0:1, 0, STEPS + TILES:STEPS + 2 * TILES]

        def agg_slot(h, k):
            return PS[:, 3 * h + k // PER_BANK, (k % PER_BANK) * RW:(k % PER_BANK) * RW + RW]

        def exp_slot(k):
            return PS[:, 6, 2 * H * SPLIT * k:2 * H * SPLIT * (k + 1)]

        @block.sync
        def _(sp):
            for t, name in ((0, "src"), (1, "dst")):
                sp.dma_start((src_i, dst_i)[t],
                             a[name].rearrange("(p j) -> p j", p=EP)).then_inc(s["edges_loaded"], 16)
            for n, name in enumerate(vec_names):
                v = a[name]
                flat = v if len(v.shape) == 1 else v.rearrange("h f -> (h f)")
                sp.dma_start(vec[:, n, :], flat.partition_broadcast(P)).then_inc(s["vec_loaded"], 16)
            for n, name in enumerate(W_names):
                sp.dma_start(Wt[:, n, :], a[name]).then_inc(s["w_loaded"], 16)
            sp.dma_start(wih[:, :, :], a["L2_gnn_w_ih"].rearrange("(t p) n -> p t n", p=P)).then_inc(s["w_loaded"], 16)
            sp.dma_start(whh[:, :], a["L2_gnn_w_hh"]).then_inc(s["w_loaded"], 16)
            sp.dma_start(gru_b[:, 0, :], a["L2_gnn_b_ih"].rearrange("(o n) -> o n", o=1)).then_inc(s["w_loaded"], 16)
            sp.dma_start(gru_b[:, 1, :], a["L2_gnn_b_hh"].rearrange("(o n) -> o n", o=1)).then_inc(s["w_loaded"], 16)
            sp.wait_ge(s["pad_ready"], 3)
            sp.dma_start(X[:, 0:NB - 1, :], a["x"][0:(NB - 1) * P, :].rearrange("(b p) f -> p b f", p=P))\
              .then_inc(s["x_loaded"], 16)
            sp.dma_start(X[0:TAIL, NB - 1, :], a["x"][(NB - 1) * P:N, :]).then_inc(s["x_loaded"], 16)
            for l in range(2):
                sp.dma_start(list_d[l][E:ROWS, :].rearrange("(p j) x -> p j x", j=8), pad_rec[:, :, :])\
                  .then_inc(s["pad_stored"], 16)
            for l in range(2):
                sp.wait_ge(s["scattered"], l + 1)
                sp.wait_ge(s["pad_stored"], 32)
                sp.wait_ge(s["chunk_free"], l + 1)
                full = (CH - 1) * P * P
                sp.dma_start(chunk[:, 0:CH - 1, :],
                             list_d[l][0:full, :].rearrange("(c q e) x -> q c (e x)", q=P, e=P))\
                  .then_inc(s["chunk_loaded"], 16)
                sp.dma_start(chunk[0:TILES - (CH - 1) * P, CH - 1, :],
                             list_d[l][full:ROWS, :].rearrange("(q e) x -> q (e x)", e=P))\
                  .then_inc(s["chunk_loaded"], 16)

            def spill_at(g):
                return spill_d[g] if isinstance(g, int) else spill_d[ds(g, 1), :, :].rearrange("g p r -> (g p) r")

            for n, (kind, l, t) in enumerate(PASSES):
                if t is not None and l == 0:
                    sp.wait_ge(s["table_ready"], t + 1)
                    sp.dma_start(table_d[t].rearrange("(b p) f -> p b f", p=P), TAB[:, :, :])\
                      .then_inc(s["table_stored"], 16)
                if kind == "max":
                    def store(g, h):
                        sp.wait_ge(landed_sem(n, h), landed(n, g, h))
                        sp.dma_start(spill_at(g), rows[:, h, :, :].rearrange("p g r -> p (g r)"))\
                          .then_inc(s[f"spilled{h}"], 16)
                    pairs(sp, store)
                if kind == "att":
                    for h in range(HALVES):
                        sp.wait_ge(s[f"spilled{h}"], 8 * max_base[n])

                    def reload(g, h):
                        need(sp, "groups_done", n * GROUPS + g - 1)
                        sp.dma_start(rows[:, h, :, :].rearrange("p g r -> p (g r)"), spill_at(g))\
                          .then_inc(s[f"reload{h}"], 16)
                    pairs(sp, reload)
            sp.wait_ge(s["w_loaded"], 16 * (len(W_names) + 4))
            sp.wait_ge(s["out_ready"], 1)
            sp.dma_start(out[0:(NB - 1) * P, :].rearrange("(b p) f -> p b f", p=P), X[:, 0:NB - 1, :])\
              .then_inc(s["out_stored"], 16)
            sp.dma_start(out[(NB - 1) * P:N, :], X[0:TAIL, NB - 1, :]).then_inc(s["out_stored"], 16)
            sp.wait_ge(s["out_stored"], 32)


        @block.gpsimd
        def _(pool):
            g_ = nc.gpsimd
            g_.memset(X[:, NB - 1, :], 0.0).then_inc(s["pad_ready"], 1)
            g_.memset(pad_rec[:, :, 0:1], NO_KEY).then_inc(s["pad_ready"], 1)
            g_.memset(pad_rec[:, :, 1:2], 0).then_inc(s["pad_ready"], 1)
            g_.iota(iota_row[:, :], pattern=[[1, P]], base=0, channel_multiplier=0,
                    allow_small_or_imprecise_dtypes=True).then_inc(s["const_ready"], 1)
            g_.memset(ones[:, :], 1.0).then_inc(s["const_ready"], 1)
            g_.memset(ident[:, :], 0.0).then_inc(s["const_ready"], 1)
            g_.memset(below[:, :], 0.0).then_inc(s["const_ready"], 1)
            g_.memset(far_ident[:, :, :], 0.0).then_inc(s["const_ready"], 1)
            g_.memset(ones_b[:, :], 1.0).then_inc(s["const_ready"], 1)
            g_.memset(ident_b[:, :], 0.0).then_inc(s["const_ready"], 1)
            pool.wait_ge(s["const_ready"], 7)
            g_.affine_select(out=ident_b[:, :], in_=ident_b[:, :], compare_op=ALU.not_equal, fill=1.0, base=0,
                             pattern=[[-1, P]], channel_multiplier=1).then_inc(s["const_ready"], 1)
            g_.affine_select(out=ident[:, :], in_=ident[:, :], compare_op=ALU.not_equal, fill=1.0, base=0,
                             pattern=[[-1, P]], channel_multiplier=1).then_inc(s["const_ready"], 1)
            g_.affine_select(out=below[:, :], in_=below[:, :], compare_op=ALU.is_ge, fill=1.0, base=0,
                             pattern=[[-1, P]], channel_multiplier=1).then_inc(s["const_ready"], 1)
            g_.affine_select(out=far_ident[:, :, :], in_=far_ident[:, :, :], compare_op=ALU.not_equal, fill=FAR,
                             base=0, pattern=[[0, H], [-1, P]], channel_multiplier=1).then_inc(s["const_ready"], 1)

            for l in range(2):
                pool.wait_ge(s[f"placed{l}"], 3)

                def scatter(g, h, l=l):
                    n_col = EC // G
                    if not (isinstance(g, int) and g + l * n_col < HALVES):
                        pool.wait_ge(s[f"rec_landed{h}"], (g - h) * 64 + l * n_col * 64)
                        pool.sem_inc(s["pool_turn"])
                    g_.tensor_copy(rec_slot[:, h, :, :], rec[l][:, ds(g * G, G), :]).then_inc(s["rec_copied"], 1)
                    g_.tensor_copy(idx_slot[0:EP, h, :], place[l][:, ds(g * G, G)]).then_inc(s["rec_copied"], 1)
                    pool.wait_ge(s["rec_copied"], g * 2 + (2 + l * n_col * 2))
                    pool.sem_inc(s["pool_turn"])
                    for k in range(G):
                        g_.indirect_dma_start(
                            out=list_d[l][:, :], out_offset=bass.IndirectOffsetOnAxis(ap=idx_slot[0:EP, h, k:k + 1], axis=0),
                            in_=rec_slot[:, h, k, :], in_offset=None).then_inc(s[f"rec_landed{h}"], 16)
                pairs(pool, scatter, EC // G)
                for h in range(HALVES):
                    pool.wait_ge(s[f"rec_landed{h}"], 64 * (EC // G) * (l + 1))
                pool.sem_inc(s["scattered"])

            for n, (kind, l, t) in enumerate(PASSES):
                if kind == "att":
                    def weigh(g, h, n=n):
                        pool.wait_ge(s["weights"], g + (att_base[n] + 1))
                        feats = rows[:, h, :, 0:D].rearrange("p g (h f) -> p g h f", f=FH)
                        g_.tensor_tensor(feats, feats, rows[:, h, :, D:RW].unsqueeze(3).broadcast_to([P, G, H, FH]),
                                         ALU.mult).then_inc(s["weighted"], 1)
                    pairs(pool, weigh)
                if t is None:
                    continue
                if n == FIRST_MAX:
                    for h in range(HALVES):
                        pool.wait_ge(landed_sem(n - 1, h), 16 * G * gather_base[n] // 2)
                pool.wait_ge(s["table_stored"], 16 * (t + 1))
                pool.wait_ge(s["tables_ready"], l + 1)

                def gather(g, h, n=n, kind=kind, l=l, t=t):
                    if not (isinstance(g, int) and g + landed_base(n) < HALVES):
                        pool.wait_ge(landed_sem(n, h), (g - h) * (16 * G // 2) + 16 * G * (landed_base(n) // 2))
                        pool.sem_inc(s["pool_turn"])
                    g_.tensor_copy(idx_slot[:, h, :], other[l][:, ds(g * G, G)]).then_inc(s["idx_copied"], 1)
                    pool.wait_ge(s["idx_copied"], g + (gather_base[n] + 1))
                    pool.sem_inc(s["pool_turn"])
                    pool.wait_ge(s["groups_done"], g + (n * GROUPS - 1))
                    pool.sem_inc(s["pool_turn"])
                    if kind == "max" and not (isinstance(g, int) and g + max_base[n] < HALVES):
                        pool.wait_ge(s[f"spilled{h}"], (g - h) * 8 + 8 * max_base[n])
                        pool.sem_inc(s["pool_turn"])
                    for k in range(G):
                        g_.indirect_dma_start(
                            out=rows[:, h, k, :], out_offset=None, in_=table_d[t][:, :],
                            in_offset=bass.IndirectOffsetOnAxis(ap=idx_slot[:, h, k:k + 1], axis=0)).then_inc(landed_sem(n, h), 16)
                pairs(pool, gather)

        @block.scalar
        def _(act):
            c_ = nc.scalar
            sqrts = [0]

            def sqrt_of(ap):
                sqrts[0] += 1
                act.wait_ge(s["var_ready"], sqrts[0])
                c_.activation(ap, ap, ACT.Sqrt).then_inc(s["sd_ready"], 1)

            mms = [0]

            def dense_copies(src):
                n = mms[0]
                mms[0] += 1
                act.wait_ge(s["mm_src_ready"], n + 1)
                with act.Fori(0, NMG, 1) as g:
                    c_.activation(stage[:, :, :], src[:, ds(g * MG, MG), 0:D], ACT.Copy).then_inc(s["stage_ready"], 1)
                    act.wait_ge(s["tr_done"], g + (NMG * n + 1))
                    c_.activation(stageT[:, :, :].rearrange("p k f -> p (k f)"), PSf[:, 0:MG * D], ACT.Copy)\
                      .then_inc(s["stageT_ready"], 1)

            sqrt_of(stat[:, 0, :])
            if stop_after < 1:
                return
            sqrt_of(dinv[:, :])
            dense_copies(UA)
            if stop_after < 2:
                return
            sqrt_of(stat[:, 0, :])
            dense_copies(UA)
            if stop_after < 3:
                return
            sqrt_of(stat[:, 0, :])
            act.wait_ge(s["gru_src"], 1)
            with act.Fori(0, NB, 1) as b:
                c_.activation(stage[:, 0, :], TAB[:, ds(b, 1), 0:D], ACT.Copy).then_inc(s["gru_stage"], 1)
                c_.activation(stage[:, 1, :], ACC[:, ds(b, 1), 0:D], ACT.Copy).then_inc(s["gru_stage"], 1)
                c_.activation(stage[:, 2, :], ACC2[:, ds(b, 1), 0:D], ACT.Copy).then_inc(s["gru_stage"], 1)
                act.wait_ge(s["gru_tr"], b + 1)
                c_.activation(stageT[:, 0:3, :].rearrange("p k f -> p (k f)"), PS[:, 0, 0:3 * D], ACT.Copy)\
                  .then_inc(s["gru_T"], 1)
                act.wait_ge(s["gru_a2T"], b + 1)
                c_.activation(aT[:, :, :].rearrange("p k f -> p (k f)"), PS[:, 2, 0:2 * D], ACT.Copy)\
                  .then_inc(s["gru_aT"], 1)
                act.wait_ge(s["gru_gates"], b + 1)
                c_.activation(rz[:, :, :].rearrange("p k f -> p (k f)"), PS[:, 3, 0:2 * D], ACT.Sigmoid)\
                  .then_inc(s["gru_rz"], 1)
                act.wait_ge(s["gru_pre"], b + 1)
                c_.activation(nn[:, :], nn[:, :], ACT.Tanh).then_inc(s["gru_n"], 1)
            if stop_after < 4:
                return
            sqrt_of(stat[:, 0, :])
            atts = [n for n, (kind, _, _) in enumerate(PASSES) if kind == "att"]
            for j, n in enumerate(atts):
                dense_copies(UA)

                def copy_heads(g, h):
                    for q in range(G // 2):
                        act.wait_ge(s["heads_turned"], g * (G // 2) + (max_base[n - 1] * (G // 2) + q + 1))
                        c_.activation(headT[:, q, :], PS[0:SPLIT, MAXB + q, :].bitcast(bf16), ACT.Copy)\
                          .then_inc(s["heads_copied"], 1)
                act.wait_ge(s["onehot_ready"], (n - 1) * GROUPS + 1)
                pairs(act, copy_heads)

                def turn(g):
                    act.wait_ge(s["turned"], g + (att_base[n] + 1))
                    if not (isinstance(g, int) and g + att_base[n] < 1):
                        act.wait_ge(s["expanded"], g + att_base[n])
                    c_.activation(ohT[:, :, :].rearrange("p k e -> p (k e)"), PSf[:, 6 * 512:6 * 512 + G * P], ACT.Copy)\
                      .then_inc(s["turn_copied"], 1)

                turn(0)

                def att(g, h):
                    act.wait_ge(s["logits"], g + (att_base[n] + 1))
                    c_.activation(rows[:, h, :, D:RW], small[:, h, :, :], ACT.Exp).then_inc(s["weights"], 1)
                    if not (isinstance(g, int) and g + 1 >= GROUPS):
                        turn(g + 1)
                pairs(act, att, peel_last=True)
                act.wait_ge(s["self_logit"], j + 1)
                c_.activation(wself[:, :, :], wtmp[:, :, :], ACT.Exp).then_inc(s["self_w"], 1)
                sqrt_of(bn[:, 2, :])
                act.wait_ge(s["elu_src"], j + 1)
                c_.activation(UB, UB, ACT.Exp).then_inc(s["elu_exp"], 1)

        @block.tensor
        def _(pe):
            t_ = nc.tensor
            pe.wait_ge(s["const_ready"], 11)
            for l in range(2):
                pe.wait_ge(s["counts_ready"], l + 1)
                t_.matmul(PS[0:EP, 0, 0:NB], ones[0:EP, 0:EP], cnt[0:EP, 0, :], start=True, stop=True)
                t_.matmul(PS[0:EP, 1, 0:NB], below[0:EP, 0:EP], cnt[0:EP, 0, :], start=True, stop=True)\
                  .then_inc(s["prefix_ready"], 1)

            def turn_tables(l):
                for x in range(2):
                    pe.wait_ge(s["chunk_split"], 4 * l + 2 * x + 2)
                    for c in range(CH):
                        n = min(P, TILES - c * P)
                        last = t_.transpose(PSf[:, c * P:c * P + n], split[0:n, c, :], ident[0:n, 0:n])
                    last.then_inc(s["chunk_turned"], 1)

            mms = [0]

            def dense(weight):
                n = mms[0]
                mms[0] += 1
                if n == 0:
                    pe.wait_ge(s["w_loaded"], 16 * (len(W_names) + 4))
                with pe.Fori(0, NMG, 1) as g:
                    pe.wait_ge(s["stage_ready"], g + (NMG * n + 1))
                    for k in range(MG):
                        last = t_.transpose(PSf[:, k * P:(k + 1) * P], stage[:, k, :], ident[:, :])
                    last.then_inc(s["tr_done"], 1)
                    pe.wait_ge(s["stageT_ready"], g + (NMG * n + 1))
                    pe.wait_ge(s["mm_used"], g + (NMG * n + 1))
                    for k in range(MG):
                        last = t_.matmul(PSf[:, 1024 + k * P:1024 + (k + 1) * P], stageT[:, k, :], weight,
                                         start=True, stop=True)
                    last.then_inc(s["mm_ready"], 1)

            def psum_free(n, g):
                need(pe, "sums_used", n * GROUPS if isinstance(g, int) and g < HALVES else g + (n * GROUPS - 1))

            def sum_pass(n, kind, l):
                def body(g, h):
                    pe.wait_ge(s["onehot_ready"], g + (n * GROUPS + 1))
                    if kind == "agg":
                        pe.wait_ge(landed_sem(n, h), landed(n, g, h))
                    psum_free(n, g)
                    for k in range(G):
                        if kind == "agg":
                            last = t_.matmul(agg_slot(h, k), onehot[:, h, k, :], rows[:, h, k, 0:RW], start=True, stop=True)
                        else:
                            last = t_.matmul(agg_slot(h, k)[:, 0:1], onehot[:, h, k, :], ones[:, 0:1],
                                             start=True, stop=True)
                    last.then_inc(s["groups_done"], 1)
                pairs(pe, body)

            def max_pass(n):
                mb = max_base[n]

                def turn_heads(g, h):
                    pe.wait_ge(landed_sem(n, h), landed(n, g, h))
                    for q in range(G // 2):
                        bank = PS[0:SPLIT, MAXB + q, :].bitcast(bf16)
                        for k in range(2):
                            parts = rows[:, h, 2 * q + k, RW:RT].bitcast(bf16).rearrange("p (s t) -> p t s", t=H)
                            for hd in range(H):
                                c = (k * H + hd) * P
                                last = t_.transpose(bank[:, c:c + P], parts[:, hd, :], ident_b[:, :])
                        last.then_inc(s["heads_turned"], 1)

                def body(g, h):
                    if isinstance(g, int) and g == 0:
                        psum_free(n, g)
                        turn_heads(g, h)
                    pe.wait_ge(s["onehot_ready"], g + (n * GROUPS + 1))
                    for k in range(G):
                        if not (isinstance(g, int) and g * G + k + mb * G < MAXB):
                            pe.wait_ge(s["max_used"], g * G + (mb * G + k + 1 - MAXB))
                        t_.matmul(PS[:, k % MAXB, :], far[:, h, k * P:(k + 1) * P],
                                  far_ident[:, :, :].rearrange("p h e -> p (h e)"), start=True, stop=False)
                        if k % 2 == 0:
                            pe.wait_ge(s["heads_copied"], g * (G // 2) + (mb * (G // 2) + k // 2 + 1))
                        t_.matmul(PS[:, k % MAXB, :], ones_b[:, :],
                                  headT[:, k // 2, (k % 2) * H * P:(k % 2 + 1) * H * P],
                                  start=False, stop=True).then_inc(s["max_ready"], 1)
                    if not (isinstance(g, int) and g + 1 >= GROUPS):
                        turn_heads(g + 1, 1 - h)
                    pe.wait_ge(s["max_ready"], g * G + (mb + 1) * G)
                    pe.sem_inc(s["groups_done"])
                pairs(pe, body, peel_last=True)

            def att_pass(n):
                regs = [pe.alloc_register(f"pe_block{k}_{n}") for k in range(G)]

                def expand(g, h):
                    if isinstance(g, int) and g == 0:
                        psum_free(n, 0)
                    pe.wait_ge(s["onehot_ready"], g + (n * GROUPS + 1))
                    if not (isinstance(g, int) and g + att_base[n] < 1):
                        pe.wait_ge(s["logits"], g + att_base[n])
                    for k in range(G):
                        last = t_.transpose(PSf[:, 6 * 512 + k * P:6 * 512 + (k + 1) * P], onehot[:, h, k, :],
                                            ident[:, :])
                    last.then_inc(s["turned"], 1)
                    pe.load(regs, block_of[0][0:1, ds(g * G, G)])
                    blocks = [pe.snap(r, min_val=0, max_val=NB - 1) for r in regs]
                    pe.wait_ge(s["turn_copied"], g + (att_base[n] + 1))
                    for k in range(G):
                        last = t_.matmul(exp_slot(k), ohT[:, k, :], T2s[:, ds(blocks[k], 1), :, :].rearrange("p b s t -> p (b s t)"),
                                         start=True, stop=True)
                    last.then_inc(s["expanded"], 1)

                pe.wait_ge(s["t2_ready"], att_base[n] // GROUPS + 1)
                expand(0, 0)

                def body(g, h):
                    if not (isinstance(g, int) and g + 1 >= GROUPS):
                        expand(g + 1, 1 - h)
                    pe.wait_ge(s["weighted"], g + (att_base[n] + 1))
                    psum_free(n, g)
                    for k in range(G):
                        last = t_.matmul(agg_slot(h, k), onehot[:, h, k, :], rows[:, h, k, 0:RW], start=True, stop=True)
                    last.then_inc(s["groups_done"], 1)
                pairs(pe, body, peel_last=True)

            def column_sums(view, n):
                pe.wait_ge(s["bn_src"], n)
                flat = view.rearrange("p b f -> p (b f)")
                for c in range((NB - 1) // 4):
                    t_.matmul(PS[:, 6, :], ones[:, :], flat[:, c * 512:(c + 1) * 512], start=(c == 0), stop=False)
                t_.matmul(PS[:, 6, 0:D], ones[0:TAIL, :], view[0:TAIL, NB - 1, :], start=False, stop=True)\
                  .then_inc(s["bn_sum"], 1)

            turn_tables(0)
            sum_pass(0, "deg", 0)
            if stop_after < 1:
                return
            dense(W("L0_gnn_W"))
            turn_tables(1)
            sum_pass(1, "agg", 0)
            if stop_after < 2:
                return
            sum_pass(2, "agg", 0)
            dense(W("L1_gnn_W"))
            if stop_after < 3:
                return
            sum_pass(3, "agg", 0)
            sum_pass(4, "agg", 1)
            pe.wait_ge(s["gru_src"], 1)
            with pe.Fori(0, NB, 1) as b:
                pe.wait_ge(s["gru_stage"], b * 3 + 3)
                for k in range(3):
                    last = t_.transpose(PS[:, 0, k * P:(k + 1) * P], stage[:, k, :], ident[:, :])
                last.then_inc(s["gru_tr"], 1)
                pe.wait_ge(s["gru_T"], b + 1)
                t_.matmul(PS[:, 1, 0:D], stageT[:, 1, :], W("L2_gnn_W_in"), start=True, stop=True)
                t_.matmul(PS[:, 1, D:2 * D], stageT[:, 2, :], W("L2_gnn_W_out"), start=True, stop=True)\
                  .then_inc(s["gru_a"], 1)
                pe.wait_ge(s["gru_a2"], b + 1)
                for k in range(2):
                    last = t_.transpose(PS[:, 2, k * P:(k + 1) * P], a2[:, k, :], ident[:, :])
                last.then_inc(s["gru_a2T"], 1)
                t_.matmul(PS[:, 3, :], ones[0:1, :], gate_b[:, :], start=True, stop=False)
                t_.matmul(PS[:, 3, 0:2 * D], stageT[:, 0, :], whh[:, 0:2 * D], start=False, stop=False)
                t_.matmul(PS[:, 3, 3 * D:4 * D], stageT[:, 0, :], whh[:, 2 * D:3 * D], start=False, stop=False)
                pe.wait_ge(s["gru_aT"], b + 1)
                t_.matmul(PS[:, 3, 0:3 * D], aT[:, 0, :], wih[:, 0, :], start=False, stop=False)
                t_.matmul(PS[:, 3, 0:3 * D], aT[:, 1, :], wih[:, 1, :], start=False, stop=True)\
                  .then_inc(s["gru_gates"], 1)
            if stop_after < 4:
                return
            layers = sum(k == "att" for k, _, _ in PASSES)
            for j in range(layers):
                dense(W(f"L3_gnn_W{j + 1}"))
                max_pass(5 + 2 * j)
                att_pass(6 + 2 * j)
                column_sums(UA, 2 * j + 1)
                column_sums(UB, 2 * j + 2)

        @block.vector
        def _(dve):
            v_ = nc.vector
            chained = [0]

            def link(ins):
                chained[0] += 1
                ins.then_inc(s["dve_chain"], 1)
                dve.wait_ge(s["dve_chain"], chained[0])

            def looped(i, per):
                count = [0]
                start = chained[0]

                def link_in(ins, ahead=0):
                    count[0] += 1
                    assert count[0] <= per
                    ins.then_inc(s["dve_chain"], 1)
                    need(dve, "dve_chain", i * per + (start + count[0] - ahead))
                return link_in

            tick = dict(placed=0, var=0, mm=0, table=0)

            def place_list(l, key, oth):
                turn_i = mask.bitcast(i32)
                link(v_.tensor_scalar(turn_i, key, 7, None, ALU.arith_shift_right))
                link(v_.tensor_copy(key_block, turn_i))
                v_.tensor_copy(rec[l][:, :, 0], key).then_inc(s[f"placed{l}"], 1)
                v_.tensor_copy(rec[l][:, :, 1], oth).then_inc(s[f"placed{l}"], 1)
                with dve.Fori(0, NB, 1) as b:
                    lk = looped(b, 1)
                    lk(v_.tensor_scalar(mask, key_block, iota_row[0:EP, ds(b, 1)], 0.0, ALU.is_equal, ALU.add,
                                        accum_out=cnt[0:EP, 0, ds(b, 1)]))
                chained[0] += NB
                link(v_.memset(pos, -1.0))
                dve.sem_inc(s["counts_ready"])
                dve.wait_ge(s["prefix_ready"], l + 1)
                total, upto, start = (cnt[0:EP, t, :] for t in (1, 2, 3))
                link(v_.tensor_copy(total, PS[0:EP, 0, 0:NB]))
                link(v_.tensor_tensor_scan(upto, total, total, 0.0, ALU.add, ALU.max))
                link(v_.tensor_tensor(start, upto, total, ALU.subtract))
                link(v_.tensor_copy(cnt_i[0:1, :], start[0:1, :]))
                link(v_.tensor_scalar(first_tile[l][:, :], cnt_i[0:1, :], 7, None, ALU.arith_shift_right))
                link(v_.tensor_tensor(start, start, PS[0:EP, 1, 0:NB], ALU.add))
                with dve.Fori(0, NB, 1) as b:
                    lk = looped(b, 4)
                    lk(v_.tensor_scalar(mask, key_block, iota_row[0:EP, ds(b, 1)], None, ALU.is_equal))
                    lk(v_.tensor_tensor_scan(scan, mask, mask, cnt[0:EP, 3, ds(b, 1)], ALU.add, ALU.max))
                    lk(v_.tensor_tensor(prod, mask, scan, ALU.mult))
                    lk(v_.tensor_tensor(pos, pos, prod, ALU.add))
                chained[0] += 4 * NB
                v_.tensor_copy(place[l], pos).then_inc(s[f"placed{l}"], 1)
                dve.wait_ge(s[f"placed{l}"], 3)

            def step_tables(l):
                link(v_.memset(zero_row, 0.0))
                link(v_.memset(step_cnt[:, 0:2], 0.0))
                dve.wait_ge(s["chunk_loaded"], 32 * (l + 1))
                tail = TILES - (CH - 1) * P
                for x in range(2):
                    v_.tensor_copy(split[:, 0:CH - 1, :],
                                   chunk[:, 0:CH - 1, :].rearrange("p c (e x) -> p c e x", x=2)[:, :, :, x])\
                      .then_inc(s["chunk_split"], 1)
                    v_.tensor_copy(split[0:tail, CH - 1, :],
                                   chunk[0:tail, CH - 1, :].rearrange("p (e x) -> p e x", x=2)[:, :, x])\
                      .then_inc(s["chunk_split"], 1)
                    link(v_.memset(tile_tab[:, TILES:2 * TILES], 0.0 if x else float(NO_KEY)))
                    dve.wait_ge(s["chunk_turned"], 2 * l + x + 1)
                    link(v_.tensor_copy(tile_tab[:, 0:TILES], PSf[:, 0:TILES]))
                    with dve.Fori(0, NB, 1) as b:
                        lk = looped(b, 1 if x else 4)
                        t0 = dve.value_load(first_tile[l][0:1, ds(b, 1)], min_val=0, max_val=TILES - 1)
                        if x == 0:
                            lk(v_.tensor_scalar(step_tab[:, ds(t0 + b, TILES)], tile_tab[:, ds(t0, TILES)],
                                                step_cnt[:, 0:1], None, ALU.add))
                            lk(v_.tensor_scalar(block_row[:, ds(t0 + b, TILES)], zero_row, step_cnt[0:1, 1:2], None,
                                                ALU.add))
                            lk(v_.tensor_scalar(step_cnt[:, 0:1], step_cnt[:, 0:1], -float(P), None, ALU.add))
                            lk(v_.tensor_scalar(step_cnt[:, 1:2], step_cnt[:, 1:2], 1.0, None, ALU.add))
                        else:
                            lk(v_.tensor_scalar(step_tab[:, ds(t0 + b, TILES)], tile_tab[:, ds(t0, TILES)],
                                                0.0, None, ALU.add))
                    chained[0] += NB * (1 if x else 4)
                    if x == 0:
                        link(v_.tensor_copy(rel_key[l][:, 0:STEPS], step_tab[:, 0:STEPS]))
                        link(v_.tensor_copy(block_of[l][:, 0:STEPS], block_row[:, 0:STEPS]))
                    else:
                        link(v_.tensor_copy(other[l][:, :], step_tab[:, 0:STEPS]))
                dve.sem_inc(s["tables_ready"])

            def over_nodes(v):
                return v.unsqueeze(1).broadcast_to([P, NB, D])

            def over_features(st):
                return st.unsqueeze(2).broadcast_to([P, NB, D])

            def sqrt_by_act():
                tick["var"] += 1
                dve.sem_inc(s["var_ready"])
                dve.wait_ge(s["sd_ready"], tick["var"])

            def norm_relu(dst):
                var, mean = stat[:, 0, :], stat[:, 1, :]
                link(v_.tensor_reduce(mean, X[:, :, :], AX.X, ALU.add))
                link(v_.tensor_scalar(mean, mean, 1.0 / D, None, ALU.mult))
                link(v_.tensor_tensor(dst, X[:, :, :], over_features(mean), ALU.subtract))
                link(v_.tensor_tensor(UB, dst, dst, ALU.mult))
                link(v_.tensor_reduce(var, UB, AX.X, ALU.add))
                link(v_.tensor_scalar(var, var, 1.0 / D, EPS, ALU.mult, ALU.add))
                sqrt_by_act()
                link(v_.reciprocal(mean, var))
                link(v_.scalar_tensor_tensor(dst, dst, 0.0, over_features(mean), ALU.max, ALU.mult))

            def dense_results(take):
                n = tick["mm"]
                tick["mm"] += 1
                dve.sem_inc(s["mm_src_ready"])
                with dve.Fori(0, NMG, 1) as g:
                    dve.wait_ge(s["mm_ready"], g + (NMG * n + 1))
                    take(PSf[:, 1024:1024 + MG * D].rearrange("p (k f) -> p k f", f=D), ds(g * MG, MG))\
                        .then_inc(s["mm_used"], 1)
                dve.wait_ge(s["mm_used"], NMG * (n + 1) + 1)

            regs = [dve.alloc_register(f"dve_block{k}") for k in range(G)]

            def blocks_of(l, g):
                dve.sem_inc(s["dve_turn"])
                dve.load(regs, block_of[l][0:1, ds(g * G, G)])
                return [dve.snap(r, min_val=0, max_val=NB - 1) for r in regs]

            def make_onehot(n, l, g, h, op=ALU.is_equal):
                need(dve, "groups_done", n * GROUPS + g - 1 if isinstance(g, int) else g + (n * GROUPS - 1))
                out = onehot[:, h, :, :] if op == ALU.is_equal else \
                    far[:, h, 0:G * P].rearrange("p (g d) -> p g d", d=P)
                v_.tensor_tensor(out, iota_row[:, :].unsqueeze(1).broadcast_to([P, G, P]),
                                 rel_key[l][:, ds(g * G, G)].unsqueeze(2).broadcast_to([P, G, P]), op)\
                  .then_inc(s["onehot_ready"], 1)

            def add_sums(n, l, g, h, accs, lk):
                dve.wait_ge(s["groups_done"], g + (n * GROUPS + 1))
                for k, b in enumerate(blocks_of(l, g)):
                    acc = accs[k % len(accs)]
                    at = (slice(None), ds(b, 1)) + (slice(None),) * (len(acc.shape) - 2)
                    term = agg_slot(h, k)[:, 0:1] if len(acc.shape) == 2 else agg_slot(h, k).unsqueeze(1)
                    lk(v_.tensor_tensor(acc[at], acc[at], term, ALU.add), ahead=0 if k == G - 1 else len(accs) - 1)
                dve.sem_inc(s["sums_used"])

            def sum_pass(n, l, *accs):
                make_onehot(n, l, 0, 0)

                def body(g, h):
                    if not (isinstance(g, int) and g + 1 >= GROUPS):
                        make_onehot(n, l, g + 1, 1 - h)
                    add_sums(n, l, g, h, accs, looped(g, G))
                pairs(dve, body, peel_last=True)
                chained[0] += GROUPS * G

            def max_pass(n):
                make_onehot(n, 0, 0, 0, ALU.not_equal)

                def body(g, h):
                    if not (isinstance(g, int) and g + 1 >= GROUPS):
                        make_onehot(n, 0, g + 1, 1 - h, ALU.not_equal)
                    blocks = blocks_of(0, g)
                    for k in range(G):
                        dve.wait_ge(s["max_ready"], g * G + (max_base[n] * G + k + 1))
                        v_.tensor_reduce(tmax[:, k, :], PS[:, k % MAXB, :].rearrange("p (h e) -> p h e", e=P), AX.X, ALU.max)\
                          .then_inc(s["max_used"], 1)
                    lk = looped(g, G)
                    dve.wait_ge(s["max_used"], g * G + (max_base[n] + 1) * G)
                    for k, b in enumerate(blocks):
                        m = M[:, k % 2, ds(b, 1), :]
                        lk(v_.tensor_tensor(m, m, tmax[:, k, :].unsqueeze(1), ALU.max), ahead=0 if k == G - 1 else 1)
                    dve.sem_inc(s["sums_used"])
                pairs(dve, body, peel_last=True)
                chained[0] += GROUPS * G

            def split_parts(parts, value, rest, work):
                link(v_.tensor_copy(parts[0], value))
                link(v_.tensor_copy(work, parts[0]))
                link(v_.tensor_tensor(rest, value, work, ALU.subtract))
                link(v_.tensor_copy(parts[1], rest))
                link(v_.tensor_copy(work, parts[1]))
                link(v_.tensor_tensor(rest, rest, work, ALU.subtract))
                link(v_.tensor_copy(parts[2], rest))

            def att_pass(n):
                PER = 4 + G
                make_onehot(n, 0, 0, 0)

                def body(g, h):
                    first = looped(g, PER)
                    dve.wait_ge(s["expanded"], g + (att_base[n] + 1))
                    first(v_.tensor_reduce(terms[:, :, :], PS[:, 6, 0:2 * H * G * SPLIT]
                                           .rearrange("p (g s t) -> p g t s", s=SPLIT, t=2 * H), AX.X, ALU.add))
                    dve.wait_ge(s[f"reload{h}"], reloaded(n, g, h))
                    first(v_.tensor_tensor(small[:, h, :, :], rows[:, h, :, D:RW], terms[:, :, 0:H], ALU.add))
                    first(v_.scalar_tensor_tensor(small2[:, h, :, :], small[:, h, :, :], SLOPE, small[:, h, :, :],
                                                  ALU.mult, ALU.max))
                    first(v_.tensor_tensor(small[:, h, :, :], small2[:, h, :, :], terms[:, :, H:2 * H], ALU.subtract))
                    dve.sem_inc(s["logits"])
                    if not (isinstance(g, int) and g + 1 >= GROUPS):
                        make_onehot(n, 0, g + 1, 1 - h)
                    if isinstance(g, int) and g == 0:
                        dve.sem_inc(s["dve_chain"], G)
                    else:
                        add_sums(n, 0, g - 1, 1 - h, (ACC[:, :, :], ACC_ODD), first)
                pairs(dve, body, peel_last=True)
                chained[0] += GROUPS * PER + G
                start = chained[0] - G
                count = [0]

                def last(ins, ahead=0):
                    count[0] += 1
                    ins.then_inc(s["dve_chain"], 1)
                    dve.wait_ge(s["dve_chain"], start + count[0] - ahead)
                add_sums(n, 0, GROUPS - 1, (GROUPS - 1) % HALVES, (ACC[:, :, :], ACC_ODD), last)
                link(v_.tensor_tensor(ACC[:, :, :], ACC[:, :, :], ACC_ODD, ALU.add))

            dve.wait_ge(s["const_ready"], 11)
            dve.wait_ge(s["edges_loaded"], 32)
            dve.sem_inc(s["mm_used"])
            place_list(0, dst_i, src_i)
            place_list(1, src_i, dst_i)
            dve.sem_inc(s["chunk_free"])
            step_tables(0)
            dve.sem_inc(s["chunk_free"])
            dve.wait_ge(s["x_loaded"], 32)
            norm_relu(UA)
            link(v_.memset(deg[:, :], 0.0))
            sum_pass(0, 0, deg[:, :])
            dve.wait_ge(s["vec_loaded"], 16 * len(vec_names))

            def finish():
                dve.sem_inc(s["out_ready"])

            if stop_after < 1:
                link(v_.tensor_tensor(X[:, :, :], UA, over_features(deg[:, :]), ALU.add))
                return finish()

            link(v_.tensor_scalar(dinv[:, :], deg[:, :], 1.0, None, ALU.add))
            sqrt_by_act()
            link(v_.reciprocal(stat[:, 2, :], dinv[:, :]))
            link(v_.tensor_copy(dinv[:, :], stat[:, 2, :]))
            dve.wait_ge(s["scattered"], 2)
            link(v_.memset(TAB[:, :, D:RT], 1.0))

            def scaled(ps, blk):
                return v_.tensor_tensor(TAB[:, blk, 0:D], ps, dinv[:, blk].unsqueeze(2).broadcast_to([P, MG, D]),
                                        ALU.mult)
            dense_results(scaled)
            dve.sem_inc(s["table_ready"])
            step_tables(1)
            link(v_.memset(ACC[:, :, :], 0.0))
            sum_pass(1, 0, ACC[:, :, :])
            link(v_.tensor_tensor(UA, ACC[:, :, 0:D], TAB[:, :, 0:D], ALU.add))
            link(v_.tensor_tensor(UA, UA, over_features(dinv[:, :]), ALU.mult))
            link(v_.tensor_tensor(UA, UA, over_nodes(V("L0_gnn_b")), ALU.add))
            link(v_.scalar_tensor_tensor(X[:, :, :], UA, 0.0, X[:, :, :], ALU.max, ALU.add))
            if stop_after < 2:
                return finish()

            norm_relu(TAB[:, :, 0:D])
            dve.sem_inc(s["table_ready"])
            link(v_.memset(ACC[:, :, :], 0.0))
            sum_pass(2, 0, ACC[:, :, :])
            link(v_.tensor_tensor(UA, ACC[:, :, 0:D], TAB[:, :, 0:D], ALU.add))
            dense_results(lambda ps, blk: v_.tensor_tensor(X[:, blk, :], X[:, blk, :], ps, ALU.add))
            link(v_.tensor_tensor(X[:, :, :], X[:, :, :], over_nodes(V("L1_gnn_b")), ALU.add))
            if stop_after < 3:
                return finish()

            norm_relu(TAB[:, :, 0:D])
            dve.sem_inc(s["table_ready"])
            link(v_.memset(ACC[:, :, :], 0.0))
            link(v_.memset(ACC2, 0.0))
            sum_pass(3, 0, ACC[:, :, :])
            sum_pass(4, 1, ACC2)
            for t, acc in ((0, ACC[:, :, :]), (1, ACC2)):
                link(v_.tensor_scalar(has[:, t, :], acc[:, :, D], 1.0, None, ALU.min))
                link(v_.tensor_scalar(stat[:, 2, :], acc[:, :, D], 1.0, None, ALU.max))
                link(v_.reciprocal(inv[:, t, :], stat[:, 2, :]))
                link(v_.tensor_tensor(acc[:, :, 0:D], acc[:, :, 0:D], over_features(inv[:, t, :]), ALU.mult))
            link(v_.tensor_tensor(gate_b[:, 0:2 * D], gru_b[:, 0, 0:2 * D], gru_b[:, 1, 0:2 * D], ALU.add))
            link(v_.tensor_copy(gate_b[:, 2 * D:3 * D], gru_b[:, 0, 2 * D:3 * D]))
            link(v_.tensor_copy(gate_b[:, 3 * D:4 * D], gru_b[:, 1, 2 * D:3 * D]))
            dve.sem_inc(s["gru_src"])
            with dve.Fori(0, NB, 1) as b:
                lk = looped(b, 8)
                dve.wait_ge(s["gru_a"], b + 1)
                for t, name in ((0, "L2_gnn_b_in"), (1, "L2_gnn_b_out")):
                    lk(v_.scalar_tensor_tensor(a2[:, t, :], V(name), has[:, t, ds(b, 1)], PS[:, 1, t * D:(t + 1) * D],
                                               ALU.mult, ALU.add))
                dve.sem_inc(s["gru_a2"])
                dve.wait_ge(s["gru_rz"], b + 1)
                lk(v_.tensor_tensor(gt[:, :], rz[:, 0, :], PS[:, 3, 3 * D:4 * D], ALU.mult))
                lk(v_.tensor_tensor(nn[:, :], gt[:, :], PS[:, 3, 2 * D:3 * D], ALU.add))
                dve.sem_inc(s["gru_pre"])
                dve.wait_ge(s["gru_n"], b + 1)
                lk(v_.tensor_tensor(gt[:, :].unsqueeze(1), TAB[:, ds(b, 1), 0:D], nn[:, :].unsqueeze(1), ALU.subtract))
                lk(v_.tensor_tensor(gt[:, :], gt[:, :], rz[:, 1, :], ALU.mult))
                lk(v_.tensor_tensor(gt[:, :], gt[:, :], nn[:, :], ALU.add))
                lk(v_.tensor_tensor(X[:, ds(b, 1), :], X[:, ds(b, 1), :], gt[:, :].unsqueeze(1), ALU.add))
            chained[0] += 8 * NB
            if stop_after < 4:
                return finish()

            norm_relu(UA)
            layers = sum(k == "att" for k, _, _ in PASSES)
            for j in range(layers):
                p = f"L3_gnn_"
                dense_results(lambda ps, blk: v_.tensor_copy(TAB[:, blk, 0:D], ps))
                heads = UA.rearrange("p b (h f) -> p b h f", f=FH)
                link(v_.tensor_tensor(UA, TAB[:, :, 0:D], over_nodes(V(f"{p}a{j + 1}_src")), ALU.mult))
                link(v_.tensor_reduce(TAB[:, :, D:RW], heads, AX.X, ALU.add))
                head_parts = TAB[:, :, RW:RT].bitcast(bf16).rearrange("p b (s t) -> p s b t", t=H)
                split_parts([head_parts[:, t] for t in range(SPLIT)], TAB[:, :, D:RW], wtmp[:, :, :], wself[:, :, :])
                dve.sem_inc(s["table_ready"])
                link(v_.tensor_tensor(UA, TAB[:, :, 0:D], over_nodes(V(f"{p}a{j + 1}_dst")), ALU.mult))
                link(v_.tensor_reduce(T2[:, :, 0:H], heads, AX.X, ALU.add))
                link(v_.memset(M[:, :, :, :], FAR))
                max_pass(5 + 2 * j)
                top = M[:, 0]
                link(v_.tensor_tensor(top, top, M[:, 1], ALU.max))
                link(v_.tensor_tensor(top, top, TAB[:, :, D:RW], ALU.max))
                link(v_.tensor_tensor(top, top, T2[:, :, 0:H], ALU.add))
                link(v_.scalar_tensor_tensor(T2[:, :, H:2 * H], top, SLOPE, top, ALU.mult, ALU.max))
                split_parts([T2s[:, :, t, :] for t in range(SPLIT)], T2[:, :, :],
                            UA[:, :, 0:2 * H], UA[:, :, 2 * H:4 * H])
                link(v_.memset(ACC[:, :, :], 0.0))
                link(v_.memset(ACC_ODD, 0.0))
                dve.sem_inc(s["t2_ready"])
                att_pass(6 + 2 * j)
                link(v_.tensor_tensor(wtmp[:, :, :], TAB[:, :, D:RW], T2[:, :, 0:H], ALU.add))
                link(v_.scalar_tensor_tensor(wself[:, :, :], wtmp[:, :, :], SLOPE, wtmp[:, :, :], ALU.mult, ALU.max))
                link(v_.tensor_tensor(wtmp[:, :, :], wself[:, :, :], T2[:, :, H:2 * H], ALU.subtract))
                dve.sem_inc(s["self_logit"])
                dve.wait_ge(s["self_w"], j + 1)
                wide = wself[:, :, :].unsqueeze(3).broadcast_to([P, NB, H, FH])
                link(v_.tensor_tensor(heads, TAB[:, :, 0:D].rearrange("p b (h f) -> p b h f", f=FH), wide, ALU.mult))
                link(v_.tensor_tensor(UA, UA, ACC[:, :, 0:D], ALU.add))
                link(v_.tensor_tensor(wtmp[:, :, :], wself[:, :, :], ACC[:, :, D:RW], ALU.add))
                link(v_.reciprocal(wself[:, :, :], wtmp[:, :, :]))
                link(v_.tensor_tensor(heads, heads, wide, ALU.mult))
                link(v_.tensor_tensor(UA, UA, over_nodes(V(f"{p}b{j + 1}")), ALU.add))
                sums = PS[:, 6, :].rearrange("p (k f) -> p f k", f=D)
                dve.sem_inc(s["bn_src"])
                dve.wait_ge(s["bn_sum"], 2 * j + 1)
                link(v_.tensor_reduce(bn[:, 0, :], sums, AX.X, ALU.add))
                link(v_.tensor_scalar(bn[:, 1, :], bn[:, 0, :], 1.0 / N, None, ALU.mult))
                link(v_.tensor_tensor(UA, UA, over_nodes(bn[:, 1, :]), ALU.subtract))
                link(v_.tensor_tensor(UB, UA, UA, ALU.mult))
                dve.sem_inc(s["bn_src"])
                dve.wait_ge(s["bn_sum"], 2 * j + 2)
                link(v_.tensor_reduce(bn[:, 0, :], sums, AX.X, ALU.add))
                link(v_.tensor_scalar(bn[:, 2, :], bn[:, 0, :], 1.0 / N, EPS, ALU.mult, ALU.add))
                sqrt_by_act()
                link(v_.reciprocal(bn[:, 0, :], bn[:, 2, :]))
                link(v_.tensor_tensor(bn[:, 3, :], bn[:, 0, :], V(f"{p}g{j + 1}"), ALU.mult))
                link(v_.tensor_tensor(UA, UA, over_nodes(bn[:, 3, :]), ALU.mult))
                link(v_.tensor_tensor(UA, UA, over_nodes(V(f"{p}beta{j + 1}")), ALU.add))
                link(v_.tensor_scalar(UB, UA, 0.0, None, ALU.min))
                dve.sem_inc(s["elu_src"])
                dve.wait_ge(s["elu_exp"], j + 1)
                link(v_.tensor_scalar(UB, UB, -1.0, None, ALU.add))
                link(v_.scalar_tensor_tensor(UA, UA, 0.0, UB, ALU.max, ALU.add))
            link(v_.tensor_tensor(X[:, :, :], X[:, :, :], UA, ALU.add))
            finish()


_INS = ["x", "src", "dst", "L0_gnn_W", "L0_gnn_b", "L1_gnn_W", "L1_gnn_b", "L2_gnn_W_in", "L2_gnn_b_in",
        "L2_gnn_W_out", "L2_gnn_b_out", "L2_gnn_w_ih", "L2_gnn_w_hh", "L2_gnn_b_ih", "L2_gnn_b_hh", "L3_gnn_W1",
        "L3_gnn_a1_src", "L3_gnn_a1_dst", "L3_gnn_b1", "L3_gnn_g1", "L3_gnn_beta1", "L3_gnn_W2", "L3_gnn_a2_src",
        "L3_gnn_a2_dst", "L3_gnn_b2", "L3_gnn_g2", "L3_gnn_beta2"]
_TRANSPOSED = {"L1_gnn_W", "L2_gnn_W_in", "L2_gnn_W_out", "L2_gnn_w_ih", "L2_gnn_w_hh"}


def kernel(**inputs):
    import numpy as _np
    import concourse.bacc as _bacc
    from concourse import mybir as _mybir
    from concourse.bass_utils import run_bass_kernel_spmd as _run

    nc = _bacc.Bacc("TRN2", target_bir_lowering=False, num_devices=1)
    arrays, aps = {}, {}
    for name in _INS:
        a = _np.asarray(inputs[name])
        a = _np.ascontiguousarray(a.T if name in _TRANSPOSED else a)
        arrays[f"in_{name}_dram"] = a
        aps[name] = nc.dram_tensor(f"in_{name}_dram", a.shape, _mybir.dt.from_np(a.dtype), kind="ExternalInput").ap()
    out = nc.dram_tensor("out_dram", aps["x"].shape, _mybir.dt.float32, kind="ExternalOutput").ap()
    gnn_kernel(nc, aps, out)
    return _run(nc, [arrays], core_ids=[0]).results[0]["out_dram"]
```

```python
import concourse.bass as bass
from concourse import mybir
from contextlib import ExitStack


def gnn_kernel(nc, a, out):
    f32, bf16 = mybir.dt.float32, mybir.dt.bfloat16
    i32, u32, i16, u16 = mybir.dt.int32, mybir.dt.uint32, mybir.dt.int16, mybir.dt.uint16
    ALU, ACT, AX = mybir.AluOpType, mybir.ActivationFunctionType, mybir.AxisListType
    ds = bass.ds

    P = 128
    N, D = a["x"].shape
    E = a["src"].shape[0]
    NB = -(-N // P)
    NP = NB * P
    TAIL = N - (NB - 1) * P
    H, FH = a["L3_gnn_a1_src"].shape
    EPS = 1e-5
    SLOPE = 0.2
    SPLIT = 3
    RW = D + H
    G = 8
    HALVES = 2
    PARTS = 2
    RING = 4
    TILES = -(-E // P)
    STEPS = -(-(TILES + NB - 1) // (G * HALVES)) * G * HALVES
    TILES = STEPS - NB + 1
    GROUPS = STEPS // G
    ROWS = TILES * P
    EP = 125
    EC = E // EP
    assert EP * EC == E and EC % (2 * G) == 0
    CH = -(-TILES // P)
    NO_KEY = 20000
    FAR = -1.0e30
    MG = 7
    NMG = NB // MG
    assert MG * NMG == NB
    PER_BANK = 3

    def dram(name, shape, dt):
        return nc.dram_tensor(name, shape, dt, kind="Internal").ap()

    list_d = [dram(f"edge_list{l}", [ROWS, 2], i32) for l in range(2)]
    table_d = [dram(f"table{k}", [NP, RW], f32) for k in range(5)]
    spill_d = dram("gathered_rows", [GROUPS, P, G * RW], f32)

    ctx = ExitStack()
    with ctx:
        def sb(name, shape, dt):
            return ctx.enter_context(nc.sbuf_tensor(name, shape, dt))

        def sem(name):
            return ctx.enter_context(nc.semaphore(name))

        X = sb("X", [P, NB, D], f32)
        TAB = sb("TAB", [P, NB, RW], f32)
        ACC = sb("ACC", [P, NB, RW], f32)
        U = sb("U", [P, 2, NB * RW], f32)
        UA = U[:, 0, 0:NB * D].rearrange("p (b f) -> p b f", f=D)
        UB = U[:, 1, 0:NB * D].rearrange("p (b f) -> p b f", f=D)
        ACC2 = U[:, 1, :].rearrange("p (b f) -> p b f", f=RW)
        ACC_ODD = U[:, 0, :].rearrange("p (b f) -> p b f", f=RW)
        rows = sb("rows", [P, HALVES, G, RW], f32)
        onehot = sb("onehot", [P, HALVES, G, P], f32)
        far = onehot[:, :, :, :].rearrange("p h g d -> p h (g d)").bitcast(bf16)
        ohT = sb("ohT", [P, G, P], bf16)
        other = [sb(f"other{l}", [P, STEPS], u16) for l in range(2)]
        rel_key = [sb(f"rel_key{l}", [P, STEPS + G], i16) for l in range(2)]
        block_of = [sb(f"block_of{l}", [1, STEPS + G], i32) for l in range(2)]
        idx_slot = sb("idx_slot", [P, HALVES, G], u32)
        rec_slot = sb("rec_slot", [EP, HALVES, G, 2], i32)
        first_tile = [sb(f"first_tile{l}", [1, NB], i32) for l in range(2)]
        dinv = sb("dinv", [P, NB], f32)
        stat = sb("stat", [P, 4, NB], f32)
        deg = sb("deg", [P, NB], f32)
        has = sb("has", [P, 2, NB], f32)
        inv = sb("inv", [P, 2, NB], f32)
        M = sb("M", [P, 2, NB, H], f32)
        T2 = sb("T2", [P, NB, 2 * H], f32)
        T2s = U[:, 1, 0:NB * SPLIT * H].bitcast(bf16).rearrange("p (b s t) -> p b s t", s=SPLIT, t=2 * H)
        spread = U[:, 0, 0:G * H * P].rearrange("p (k h d) -> p k h d", h=H, d=P)
        spare = NB * SPLIT * H
        rows4 = [rows[:, h, :, :] for h in range(HALVES)] + \
            [U[:, 1, spare + t * G * RW:spare + (t + 1) * G * RW].rearrange("p (g r) -> p g r", r=RW)
             for t in range(RING - HALVES)]
        spare += (RING - HALVES) * G * RW
        onehot4 = [onehot[:, h, :, :] for h in range(HALVES)] + \
            [U[:, 1, spare + t * G * P:spare + (t + 1) * G * P].rearrange("p (g d) -> p g d", d=P)
             for t in range(RING - HALVES)]
        onehot16 = sb("onehot16", [P, G, P], bf16)
        ident16 = sb("ident16", [P, P], bf16)
        terms = sb("terms", [P, G, 2 * H], f32)
        wself = sb("wself", [P, NB, H], f32)
        wtmp = sb("wtmp", [P, NB, H], f32)
        small = sb("small", [P, HALVES, G, H], f32)
        small2 = sb("small2", [P, HALVES, G, H], f32)
        tmax = sb("tmax", [P, G, H], f32)
        iota_row = sb("iota_row", [P, P], f32)
        ident = sb("ident", [P, P], f32)
        below = sb("below", [P, P], f32)
        ones = sb("ones", [P, P], f32)
        pad_rec = sb("pad_rec", [(ROWS - E) // 8, 8, 2], i32)
        step_cnt = sb("step_cnt", [P, 2], f32)
        cnt = sb("cnt", [P, 4, NB], f32)
        cnt_i = sb("cnt_i", [P, NB], i32)
        ones16 = sb("ones16", [P, 1], bf16)
        next_key = sb("next_key", [EP, 2], i32)
        next_block = sb("next_block", [EP, 1], f32)
        falls = sb("falls", [EP, 2], f32)
        unsorted = sb("unsorted", [1, 1], i32)
        W_names = ["L0_gnn_W", "L1_gnn_W", "L2_gnn_W_in", "L2_gnn_W_out", "L3_gnn_W1", "L3_gnn_W2"]
        Wt = sb("Wt", [P, len(W_names), D], f32)
        wih = sb("wih", [P, 2, 3 * D], f32)
        whh = sb("whh", [P, 3 * D], f32)
        vec_names = ["L0_gnn_b", "L1_gnn_b", "L2_gnn_b_in", "L2_gnn_b_out", "L3_gnn_b1", "L3_gnn_g1", "L3_gnn_beta1",
                     "L3_gnn_b2", "L3_gnn_g2", "L3_gnn_beta2", "L3_gnn_a1_src", "L3_gnn_a1_dst", "L3_gnn_a2_src",
                     "L3_gnn_a2_dst"]
        vec = sb("vec", [P, len(vec_names), D], f32)

        def V(name):
            return vec[:, vec_names.index(name), :]

        def W(name):
            return Wt[:, W_names.index(name), :]

        gru_b = sb("gru_b", [1, 2, 3 * D], f32)
        gate_b = sb("gate_b", [1, 4 * D], f32)
        stage, stageT = (onehot[:, :, :, :].rearrange("p h g d -> p (h g d)")[:, t * MG * D:(t + 1) * MG * D]
                         .rearrange("p (k f) -> p k f", f=D) for t in range(2))
        a2, aT, rz = (U[:, 0, t * 4 * D:(t + 1) * 4 * D].rearrange("p (u k f) -> p u k f", u=2, k=2) for t in range(3))
        nn, gt = (U[:, 0, (12 + 2 * t) * D:(14 + 2 * t) * D].rearrange("p (u f) -> p u f", u=2) for t in range(2))
        bn = ohT[:, :, :].rearrange("p g d -> p (g d)").bitcast(f32).rearrange("p (g d) -> p g d", d=P)

        PS = ctx.enter_context(nc.psum_tensor("PS", [P, 8, 512], f32))

        s = {}
        for name in ["edges_loaded", "vec_loaded", "w_loaded", "x_loaded", "const_ready", "pad_ready", "pad_stored",
                     "counts_ready", "prefix_ready", "placed0", "placed1", "rec_copied", "rec_landed0",
                     "rec_landed1", "listed0", "listed1", "next_loaded", "order_ready", "order_summed",
                     "unsorted_known", "rec_stored", "table_chain", "chunk_loaded", "chunk_split", "chunk_turned",
                     "chunk_free", "tables_ready", "idx_copied", "pool_turn", "rows_landed0", "rows_landed1",
                     "rows_landed2", "rows_landed3", "onehot_ready", "groups_done", "sums_used", "max_ready",
                     "max_used", "spilled0", "spilled1", "reload0", "reload1", "reload2", "reload3", "narrowed",
                     "terms_taken", "turned", "turn_copied", "act_spread", "dve_spread", "expanded", "logits",
                     "weights", "weighted", "dve_chain", "var_ready", "sd_ready", "mm_src_ready", "stage_ready",
                     "tr_done", "stageT_ready", "mm_ready", "mm_used", "table_ready", "table_stored", "gru_src",
                     "gru_stage", "gru_tr", "gru_T", "gru_a", "gru_a2", "gru_a2T", "gru_aT", "gru_gates", "gru_rz",
                     "gru_pre", "gru_n", "bn_src", "bn_sum", "elu_src", "elu_exp", "self_logit", "self_w",
                     "out_ready", "out_stored", "dve_turn", "t2_ready"]:
            s[name] = sem(name)

        block = ctx.enter_context(nc.Block())

        def need(eng, name, value):
            if not (isinstance(value, int) and value <= 0):
                eng.wait_ge(s[name], value)

        def pairs(eng, body, groups=GROUPS, peel_last=False):
            last = groups - HALVES if peel_last else groups
            for h in range(HALVES):
                body(h, h)
            with eng.Fori(HALVES, last - 1, HALVES) as g0:
                for h in range(HALVES):
                    body(g0 + h, h)
            for g in range(last, groups):
                body(g, g % HALVES)

        def quads(eng, body):
            last = GROUPS - GROUPS % RING
            for q in range(RING):
                body(q, q)
            with eng.Fori(RING, last - RING + 1, RING) as g0:
                for q in range(RING):
                    body(g0 + q, q)
            for g in range(last, GROUPS):
                body(g, g % RING)

        def gru_blocks(eng, body):
            with eng.Fori(0, NB // 2, 1) as i:
                body(i, i * 2, 2)
            if NB % 2:
                body(NB // 2, NB - 1, 1)

        PASSES = [("deg", 0, None), ("agg", 0, 0), ("agg", 0, 1), ("agg", 0, 2), ("agg", 1, 2),
                  ("max", 0, 3), ("att", 0, None), ("max", 0, 4), ("att", 0, None)]
        gather_base = [GROUPS * sum(k in ("agg", "max") for k, _, _ in PASSES[:n]) for n in range(len(PASSES))]
        FIRST_MAX = 5
        max_base = [GROUPS * sum(k == "max" for k, _, _ in PASSES[:n]) for n in range(len(PASSES))]
        att_base = [GROUPS * sum(k == "att" for k, _, _ in PASSES[:n]) for n in range(len(PASSES))]

        def landed(n, g, h):
            return (g - h) * (16 * G // 2) + 16 * G * (landed_base(n) // 2 + 1)

        def landed_base(n):
            return gather_base[n] - (gather_base[FIRST_MAX] if n >= FIRST_MAX else 0)

        def landed_sem(n, h):
            return s[f"rows_landed{h + (2 if n >= FIRST_MAX else 0)}"]

        def spilled(n, g, h):
            return (g - h) * 8 + 16 * (max_base[n] // 2 + 1)

        def reloaded(n, g, q):
            return (g - q) * (16 * PARTS // RING) + 16 * PARTS * (att_base[n] // GROUPS * len(range(q, GROUPS, RING)) + 1)

        ACCf = ACC[:, :, :].rearrange("p b f -> p (b f)")
        TABf = TAB[:, :, :].rearrange("p b f -> p (b f)")
        PSf = PS[:, :, :].rearrange("p b f -> p (b f)")
        src_i = ACCf[0:EP, 0:EC].bitcast(i32)
        dst_i = ACCf[0:EP, EC:2 * EC].bitcast(i32)
        key_block = ACCf[0:EP, 2 * EC:3 * EC].bitcast(bf16)[:, 0:EC]
        block_i, pos = (U[0:EP, 0, t * EC:(t + 1) * EC] for t in range(2))
        mask = U[0:EP, 0, 2 * EC:3 * EC].bitcast(bf16)[:, 0:EC]
        rec = [TABf[0:EP, 2 * EC * l:2 * EC * (l + 1)].bitcast(i32).rearrange("p (j x) -> p j x", x=2) for l in range(2)]
        place = [onehot[0:EP, :, :, :].rearrange("p h g d -> p (h g d)")[:, 0:EC].bitcast(i32),
                 rows[0:EP, :, :, :].rearrange("p h g r -> p (h g r)")[:, 0:EC].bitcast(i32)]
        chunk = ACCf[:, 0:CH * 2 * P].bitcast(i32).rearrange("p (c r) -> p c r", r=2 * P)
        split = ACCf[:, CH * 2 * P:CH * 3 * P].rearrange("p (c e) -> p c e", e=P)
        tabs = U[:, :, :].rearrange("p t f -> p (t f)").bitcast(i16)
        key_tab, other_tab = (tabs[:, x * 2 * TILES:(x + 1) * 2 * TILES] for x in range(2))
        key_step, other_step, block_row = (tabs[:, 4 * TILES + x * (STEPS + TILES):4 * TILES + (x + 1) * (STEPS + TILES)]
                                           for x in range(3))
        block_row = block_row[0:1, :]
        zero_row = tabs[0:1, 4 * TILES + 3 * (STEPS + TILES):5 * TILES + 3 * (STEPS + TILES)]
        step_sum = U[:, 1, 0:STEPS]
        step_upto = U[:, 1, STEPS:2 * STEPS + 1]
        block_upto = U[:, 1, 2 * STEPS + 2:2 * STEPS + 3 + NB]

        scan = PSf[0:EP, 2048:2048 + EC]

        def agg_slot(h, k):
            return PS[:, 3 * h + k // PER_BANK, (k % PER_BANK) * RW:(k % PER_BANK) * RW + RW]

        turned16 = PS[:, 6, :].bitcast(bf16)[:, 0:G * P]

        def exp_slot(k):
            return PS[:, 7, 2 * H * SPLIT * k:2 * H * SPLIT * (k + 1)]

        @block.sync
        def _(sp):
            for t, name in ((0, "src"), (1, "dst")):
                sp.dma_start((src_i, dst_i)[t],
                             a[name].rearrange("(p j) -> p j", p=EP)).then_inc(s["edges_loaded"], 16)
            sp.dma_start(next_key[0:EP - 1, :], a["dst"].rearrange("(p j) -> p j", p=EP)[1:EP, 0:2])\
              .then_inc(s["next_loaded"], 16)
            for n, name in enumerate(vec_names):
                v = a[name]
                flat = v if len(v.shape) == 1 else v.rearrange("h f -> (h f)")
                sp.dma_start(vec[:, n, :], flat.partition_broadcast(P)).then_inc(s["vec_loaded"], 16)
            for n, name in enumerate(W_names):
                sp.dma_start(Wt[:, n, :], a[name]).then_inc(s["w_loaded"], 16)
            sp.dma_start(wih[:, :, :], a["L2_gnn_w_ih"].rearrange("(t p) n -> p t n", p=P)).then_inc(s["w_loaded"], 16)
            sp.dma_start(whh[:, :], a["L2_gnn_w_hh"]).then_inc(s["w_loaded"], 16)
            sp.dma_start(gru_b[:, 0, :], a["L2_gnn_b_ih"].rearrange("(o n) -> o n", o=1)).then_inc(s["w_loaded"], 16)
            sp.dma_start(gru_b[:, 1, :], a["L2_gnn_b_hh"].rearrange("(o n) -> o n", o=1)).then_inc(s["w_loaded"], 16)
            sp.wait_ge(s["pad_ready"], 3)
            sp.dma_start(X[:, 0:NB - 1, :], a["x"][0:(NB - 1) * P, :].rearrange("(b p) f -> p b f", p=P))\
              .then_inc(s["x_loaded"], 16)
            sp.dma_start(X[0:TAIL, NB - 1, :], a["x"][(NB - 1) * P:N, :]).then_inc(s["x_loaded"], 16)
            for l in range(2):
                sp.dma_start(list_d[l][E:ROWS, :].rearrange("(p j) x -> p j x", j=8), pad_rec[:, :, :])\
                  .then_inc(s["pad_stored"], 16)
            for l in range(2):
                sp.wait_ge(s[f"listed{l}"], 1)
                sp.wait_ge(s["pad_stored"], 32)
                sp.wait_ge(s["chunk_free"], l + 1)
                full = (CH - 1) * P * P
                sp.dma_start(chunk[:, 0:CH - 1, :],
                             list_d[l][0:full, :].rearrange("(c q e) x -> q c (e x)", q=P, e=P))\
                  .then_inc(s["chunk_loaded"], 16)
                sp.dma_start(chunk[0:TILES - (CH - 1) * P, CH - 1, :],
                             list_d[l][full:ROWS, :].rearrange("(q e) x -> q (e x)", e=P))\
                  .then_inc(s["chunk_loaded"], 16)

            def spill_at(g):
                return spill_d[g] if isinstance(g, int) else spill_d[ds(g, 1), :, :].rearrange("g p r -> (g p) r")

            for n, (kind, l, t) in enumerate(PASSES):
                if t is not None and l == 0:
                    sp.wait_ge(s["table_ready"], t + 1)
                    sp.dma_start(table_d[t].rearrange("(b p) f -> p b f", p=P), TAB[:, :, :])\
                      .then_inc(s["table_stored"], 16)
                if kind == "max":
                    def store(g, h):
                        sp.wait_ge(landed_sem(n, h), landed(n, g, h))
                        sp.dma_start(spill_at(g), rows[:, h, :, :].rearrange("p g r -> p (g r)"))\
                          .then_inc(s[f"spilled{h}"], 16)
                    pairs(sp, store)
                if kind == "att":
                    for h in range(HALVES):
                        sp.wait_ge(s[f"spilled{h}"], 8 * max_base[n])

                    sp.wait_ge(s["t2_ready"], att_base[n] // GROUPS + 1)
                    sp.wait_ge(s["groups_done"], n * GROUPS)

                    def reload(g, q):
                        if not (isinstance(g, int) and g < RING):
                            sp.wait_ge(s["groups_done"], g + (n * GROUPS - RING + 1))
                        for part in range(PARTS):
                            at = slice(part * P // PARTS, (part + 1) * P // PARTS)
                            sp.dma_start(rows4[q][at].rearrange("p g r -> p (g r)"), spill_at(g)[at, :])\
                              .then_inc(s[f"reload{q}"], 16)
                    quads(sp, reload)
            sp.wait_ge(s["w_loaded"], 16 * (len(W_names) + 4))
            sp.wait_ge(s["out_ready"], 1)
            sp.dma_start(out[0:(NB - 1) * P, :].rearrange("(b p) f -> p b f", p=P), X[:, 0:NB - 1, :])\
              .then_inc(s["out_stored"], 16)
            sp.dma_start(out[(NB - 1) * P:N, :], X[0:TAIL, NB - 1, :]).then_inc(s["out_stored"], 16)
            sp.wait_ge(s["out_stored"], 32)


        @block.gpsimd
        def _(pool):
            g_ = nc.gpsimd
            g_.memset(X[:, NB - 1, :], 0.0).then_inc(s["pad_ready"], 1)
            g_.memset(pad_rec[:, :, 0:1], NO_KEY).then_inc(s["pad_ready"], 1)
            g_.memset(pad_rec[:, :, 1:2], 0).then_inc(s["pad_ready"], 1)
            g_.iota(iota_row[:, :], pattern=[[1, P]], base=0, channel_multiplier=0,
                    allow_small_or_imprecise_dtypes=True).then_inc(s["const_ready"], 1)
            g_.memset(ones[:, :], 1.0).then_inc(s["const_ready"], 1)
            g_.memset(ident[:, :], 0.0).then_inc(s["const_ready"], 1)
            g_.memset(below[:, :], 0.0).then_inc(s["const_ready"], 1)
            pool.wait_ge(s["const_ready"], 4)
            g_.affine_select(out=ident[:, :], in_=ident[:, :], compare_op=ALU.not_equal, fill=1.0, base=0,
                             pattern=[[-1, P]], channel_multiplier=1).then_inc(s["const_ready"], 1)
            g_.affine_select(out=below[:, :], in_=below[:, :], compare_op=ALU.is_ge, fill=1.0, base=0,
                             pattern=[[-1, P]], channel_multiplier=1).then_inc(s["const_ready"], 1)

            pool.wait_ge(s["placed0"], 2)
            pool.wait_ge(s["unsorted_known"], 1)
            breaks = pool.value_load(unsorted[0:1, 0:1], min_val=0, max_val=E)
            with pool.If(breaks == 0):
                g_.dma_start(list_d[0][0:E, :].rearrange("(p j) x -> p j x", p=EP), rec[0]).then_inc(s["rec_stored"], 16)
                pool.wait_ge(s["rec_stored"], 16)
                pool.sem_inc(s["listed0"])

            def scatter_list(l, before):
                pool.wait_ge(s[f"placed{l}"], 3)

                def scatter(g, h):
                    n_col = EC // G
                    if not (isinstance(g, int) and g + before * n_col < HALVES):
                        pool.wait_ge(s[f"rec_landed{h}"], (g - h) * 64 + before * n_col * 64)
                        pool.sem_inc(s["pool_turn"])
                    g_.tensor_copy(rec_slot[:, h, :, :], rec[l][:, ds(g * G, G), :]).then_inc(s["rec_copied"], 1)
                    g_.tensor_copy(idx_slot[0:EP, h, :], place[l][:, ds(g * G, G)]).then_inc(s["rec_copied"], 1)
                    pool.wait_ge(s["rec_copied"], g * 2 + (2 + before * n_col * 2))
                    pool.sem_inc(s["pool_turn"])
                    for k in range(G):
                        g_.indirect_dma_start(
                            out=list_d[l][:, :], out_offset=bass.IndirectOffsetOnAxis(ap=idx_slot[0:EP, h, k:k + 1], axis=0),
                            in_=rec_slot[:, h, k, :], in_offset=None).then_inc(s[f"rec_landed{h}"], 16)
                pairs(pool, scatter, EC // G)
                for h in range(HALVES):
                    pool.wait_ge(s[f"rec_landed{h}"], 64 * (EC // G) * (before + 1))
                pool.sem_inc(s[f"listed{l}"])

            scatter_list(1, 0)
            with pool.If(breaks != 0):
                scatter_list(0, 1)

            for n, (kind, l, t) in enumerate(PASSES):
                if kind == "att":
                    def weigh(g, q, n=n):
                        pool.wait_ge(s["weights"], g + (att_base[n] + 1))
                        feats = rows4[q][:, :, 0:D].rearrange("p g (h f) -> p g h f", f=FH)
                        g_.tensor_tensor(feats, feats, rows4[q][:, :, D:RW].unsqueeze(3).broadcast_to([P, G, H, FH]),
                                         ALU.mult).then_inc(s["weighted"], 1)
                    quads(pool, weigh)
                if t is None:
                    continue
                if n == FIRST_MAX:
                    for h in range(HALVES):
                        pool.wait_ge(landed_sem(n - 1, h), 16 * G * gather_base[n] // 2)
                pool.wait_ge(s["table_stored"], 16 * (t + 1))
                pool.wait_ge(s["tables_ready"], l + 1)

                def gather(g, h, n=n, kind=kind, l=l, t=t):
                    if not (isinstance(g, int) and g + landed_base(n) < HALVES):
                        pool.wait_ge(landed_sem(n, h), (g - h) * (16 * G // 2) + 16 * G * (landed_base(n) // 2))
                        pool.sem_inc(s["pool_turn"])
                    g_.tensor_copy(idx_slot[:, h, :], other[l][:, ds(g * G, G)]).then_inc(s["idx_copied"], 1)
                    pool.wait_ge(s["idx_copied"], g + (gather_base[n] + 1))
                    pool.sem_inc(s["pool_turn"])
                    pool.wait_ge(s["groups_done"], g + (n * GROUPS - 1))
                    pool.sem_inc(s["pool_turn"])
                    if kind == "max" and not (isinstance(g, int) and g + max_base[n] < HALVES):
                        pool.wait_ge(s[f"spilled{h}"], (g - h) * 8 + 8 * max_base[n])
                        pool.sem_inc(s["pool_turn"])
                    for k in range(G):
                        g_.indirect_dma_start(
                            out=rows[:, h, k, :], out_offset=None, in_=table_d[t][:, :],
                            in_offset=bass.IndirectOffsetOnAxis(ap=idx_slot[:, h, k:k + 1], axis=0))\
                          .then_inc(landed_sem(n, h), 16)
                pairs(pool, gather)

        @block.scalar
        def _(act):
            c_ = nc.scalar
            sqrts = [0]

            def sqrt_of(ap):
                sqrts[0] += 1
                act.wait_ge(s["var_ready"], sqrts[0])
                c_.activation(ap, ap, ACT.Sqrt).then_inc(s["sd_ready"], 1)

            mms = [0]

            def dense_copies(src):
                n = mms[0]
                mms[0] += 1
                act.wait_ge(s["mm_src_ready"], n + 1)
                with act.Fori(0, NMG, 1) as g:
                    c_.activation(stage[:, :, :], src[:, ds(g * MG, MG), 0:D], ACT.Copy).then_inc(s["stage_ready"], 1)
                    act.wait_ge(s["tr_done"], g + (NMG * n + 1))
                    c_.activation(stageT[:, :, :].rearrange("p k f -> p (k f)"), PSf[:, 0:MG * D], ACT.Copy)\
                      .then_inc(s["stageT_ready"], 1)

            sqrt_of(stat[:, 0, :])
            sqrt_of(dinv[:, :])
            dense_copies(UA)
            sqrt_of(stat[:, 0, :])
            dense_copies(UA)
            sqrt_of(stat[:, 0, :])
            act.wait_ge(s["gru_src"], 1)

            def gru(turn, b, width):
                for u in range(width):
                    for k, src in enumerate((TAB[:, ds(b + u, 1), 0:D], ACC[:, ds(b + u, 1), 0:D],
                                             ACC2[:, ds(b + u, 1), 0:D])):
                        c_.activation(stage[:, 3 * u + k, :], src, ACT.Copy).then_inc(s["gru_stage"], 1)
                for u in range(width):
                    act.wait_ge(s["gru_tr"], b + (u + 1))
                    c_.activation(stageT[:, 3 * u:3 * u + 3, :].rearrange("p k f -> p (k f)"), PS[:, 4 * u, 0:3 * D],
                                  ACT.Copy).then_inc(s["gru_T"], 1)
                for u in range(width):
                    act.wait_ge(s["gru_a2T"], b + (u + 1))
                    c_.activation(aT[:, u, :, :].rearrange("p k f -> p (k f)"), PS[:, 4 * u + 2, 0:2 * D], ACT.Copy)\
                      .then_inc(s["gru_aT"], 1)
                for u in range(width):
                    act.wait_ge(s["gru_gates"], b + (u + 1))
                    c_.activation(rz[:, u, :, :].rearrange("p k f -> p (k f)"), PS[:, 4 * u + 3, 0:2 * D], ACT.Sigmoid)\
                      .then_inc(s["gru_rz"], 1)
                for u in range(width):
                    act.wait_ge(s["gru_pre"], b + (u + 1))
                    c_.activation(nn[:, u, :], nn[:, u, :], ACT.Tanh).then_inc(s["gru_n"], 1)
            gru_blocks(act, gru)
            sqrt_of(stat[:, 0, :])
            atts = [n for n, (kind, _, _) in enumerate(PASSES) if kind == "att"]
            for j, n in enumerate(atts):
                dense_copies(UA)

                def spread_heads(g, h):
                    mb = max_base[n - 1]
                    act.wait_ge(s["onehot_ready"], g + ((n - 1) * GROUPS + 1))
                    act.wait_ge(landed_sem(n - 1, h), landed(n - 1, g, h))
                    for k in range(G):
                        if not (isinstance(g, int) and g + mb < 1):
                            act.wait_ge(s["max_ready"], g * G + ((mb - 1) * G + k + 1))
                        for hd in range(H - k % 2):
                            last = c_.activation(spread[:, k, hd, :], far[:, h, k * P:(k + 1) * P], ACT.Identity,
                                                 scale=FAR, bias=rows[:, h, k, D + hd:D + hd + 1])
                        last.then_inc(s["act_spread"], 1)
                pairs(act, spread_heads)

                ab = att_base[n]

                def narrow(g, q):
                    act.wait_ge(s["onehot_ready"], g + (n * GROUPS + 1))
                    if not (isinstance(g, int) and g + ab < 1):
                        act.wait_ge(s["turned"], g + ab)
                    c_.activation(onehot16[:, :, :], onehot4[q], ACT.Copy).then_inc(s["narrowed"], 1)

                def copy_turned(g):
                    act.wait_ge(s["turned"], g + (ab + 1))
                    if not (isinstance(g, int) and g + ab < 1):
                        act.wait_ge(s["expanded"], g + ab)
                    c_.activation(ohT[:, :, :].rearrange("p k e -> p (k e)"), turned16, ACT.Copy)\
                      .then_inc(s["turn_copied"], 1)

                for g in range(2):
                    narrow(g, g)
                    copy_turned(g)

                def att(g, q):
                    ahead = not (isinstance(g, int) and g + 2 >= GROUPS)
                    if ahead:
                        narrow(g + 2, (q + 2) % RING)
                    act.wait_ge(s["logits"], g + (ab + 1))
                    c_.activation(rows4[q][:, :, D:RW], small[:, q % HALVES, :, :], ACT.Exp).then_inc(s["weights"], 1)
                    if ahead:
                        copy_turned(g + 2)
                quads(act, att)
                act.wait_ge(s["self_logit"], j + 1)
                c_.activation(wself[:, :, :], wtmp[:, :, :], ACT.Exp).then_inc(s["self_w"], 1)
                sqrt_of(bn[:, 2, :])
                act.wait_ge(s["elu_src"], j + 1)
                c_.activation(UB, UB, ACT.Exp).then_inc(s["elu_exp"], 1)

        @block.tensor
        def _(pe):
            t_ = nc.tensor
            pe.wait_ge(s["const_ready"], 6)
            pe.wait_ge(s["order_ready"], 1)
            t_.matmul(PS[0:EP, 2, 0:1], ones[0:EP, 0:EP], falls[:, 0:1], start=True, stop=False)
            t_.matmul(PS[0:EP, 2, 0:1], ones[0:EP, 0:EP], falls[:, 1:2], start=False, stop=True)\
              .then_inc(s["order_summed"], 1)
            for turn in range(2):
                pe.wait_ge(s["counts_ready"], turn + 1)
                t_.matmul(PS[0:EP, 0, 0:NB], ones[0:EP, 0:EP], cnt[0:EP, 0, :], start=True, stop=True)
                t_.matmul(PS[0:EP, 1, 0:NB], below[0:EP, 0:EP], cnt[0:EP, 0, :], start=True, stop=True)\
                  .then_inc(s["prefix_ready"], 1)

            def turn_tables(l):
                for x in range(2):
                    pe.wait_ge(s["chunk_split"], 4 * l + 2 * x + 2)
                    for c in range(CH):
                        n = min(P, TILES - c * P)
                        last = t_.transpose(PSf[:, c * P:c * P + n], split[0:n, c, :], ident[0:n, 0:n])
                    last.then_inc(s["chunk_turned"], 1)

            mms = [0]

            def dense(weight):
                n = mms[0]
                mms[0] += 1
                if n == 0:
                    pe.wait_ge(s["w_loaded"], 16 * (len(W_names) + 4))
                with pe.Fori(0, NMG, 1) as g:
                    pe.wait_ge(s["stage_ready"], g + (NMG * n + 1))
                    for k in range(MG):
                        last = t_.transpose(PSf[:, k * P:(k + 1) * P], stage[:, k, :], ident[:, :])
                    last.then_inc(s["tr_done"], 1)
                    pe.wait_ge(s["stageT_ready"], g + (NMG * n + 1))
                    pe.wait_ge(s["mm_used"], g + (NMG * n + 1))
                    for k in range(MG):
                        last = t_.matmul(PSf[:, 1024 + k * P:1024 + (k + 1) * P], stageT[:, k, :], weight,
                                         start=True, stop=True)
                    last.then_inc(s["mm_ready"], 1)

            def psum_free(n, g):
                need(pe, "sums_used", n * GROUPS if isinstance(g, int) and g < HALVES else g + (n * GROUPS - 1))

            def sum_pass(n, kind, l):
                def body(g, h):
                    pe.wait_ge(s["onehot_ready"], g + (n * GROUPS + 1))
                    if kind == "agg":
                        pe.wait_ge(landed_sem(n, h), landed(n, g, h))
                    psum_free(n, g)
                    for k in range(G):
                        if kind == "agg":
                            last = t_.matmul(agg_slot(h, k), onehot[:, h, k, :], rows[:, h, k, 0:RW], start=True, stop=True)
                        else:
                            last = t_.matmul(PS[:, 3 * h, k:k + 1], far[:, h, k * P:(k + 1) * P], ones16[:, :],
                                             start=True, stop=True)
                    last.then_inc(s["groups_done"], 1)
                pairs(pe, body)

            def max_pass(n):
                mb = max_base[n]

                def body(g, h):
                    if isinstance(g, int) and g == 0:
                        psum_free(n, g)
                    for k in range(G):
                        pe.wait_ge(s["act_spread"], g * G + (mb * G + k + 1))
                        if k % 2:
                            pe.wait_ge(s["dve_spread"], g * (G // 2) + (mb * (G // 2) + k // 2 + 1))
                        if not (isinstance(g, int) and g + mb < 1):
                            pe.wait_ge(s["max_used"], g * G + ((mb - 1) * G + k + 1))
                        for hd in range(H):
                            last = t_.transpose(PS[:, k, hd * P:(hd + 1) * P], spread[:, k, hd, :], ident[:, :])
                        last.then_inc(s["max_ready"], 1)
                    pe.wait_ge(s["max_ready"], g * G + (mb + 1) * G)
                    pe.sem_inc(s["groups_done"])
                pairs(pe, body)

            def att_pass(n):
                regs = [pe.alloc_register(f"pe_block{k}_{n}") for k in range(G)]

                ab = att_base[n]

                def turn(g):
                    pe.wait_ge(s["narrowed"], g + (ab + 1))
                    if not (isinstance(g, int) and g + ab < 1):
                        pe.wait_ge(s["turn_copied"], g + ab)
                    for k in range(G):
                        last = t_.transpose(turned16[:, k * P:(k + 1) * P], onehot16[:, k, :], ident16[:, :])
                    last.then_inc(s["turned"], 1)

                def expand(g):
                    pe.load(regs, block_of[0][0:1, ds(g * G, G)])
                    blocks = [pe.snap(r, min_val=0, max_val=NB - 1) for r in regs]
                    pe.wait_ge(s["turn_copied"], g + (ab + 1))
                    if not (isinstance(g, int) and g + ab < 1):
                        pe.wait_ge(s["terms_taken"], g + ab)
                    for k in range(G):
                        two_terms = T2s[:, ds(blocks[k], 1), :, :].rearrange("p b s t -> p (b s t)")
                        last = t_.matmul(exp_slot(k), ohT[:, k, :], two_terms, start=True, stop=True)
                    last.then_inc(s["expanded"], 1)

                psum_free(n, 0)
                turn(0)
                turn(1)
                pe.wait_ge(s["t2_ready"], ab // GROUPS + 1)
                expand(0)

                def body(g, q):
                    if not (isinstance(g, int) and g + 2 >= GROUPS):
                        turn(g + 2)
                    if not (isinstance(g, int) and g + 1 >= GROUPS):
                        expand(g + 1)
                    pe.wait_ge(s["weighted"], g + (ab + 1))
                    psum_free(n, g)
                    for k in range(G):
                        last = t_.matmul(agg_slot(q % HALVES, k), onehot4[q][:, k, :], rows4[q][:, k, 0:RW],
                                         start=True, stop=True)
                    last.then_inc(s["groups_done"], 1)
                quads(pe, body)

            def column_sums(view, n):
                pe.wait_ge(s["bn_src"], n)
                flat = view.rearrange("p b f -> p (b f)")
                for c in range((NB - 1) // 4):
                    t_.matmul(PS[:, 6, :], ones[:, :], flat[:, c * 512:(c + 1) * 512], start=(c == 0), stop=False)
                t_.matmul(PS[:, 6, 0:D], ones[0:TAIL, :], view[0:TAIL, NB - 1, :], start=False, stop=True)\
                  .then_inc(s["bn_sum"], 1)

            turn_tables(0)
            sum_pass(0, "deg", 0)
            dense(W("L0_gnn_W"))
            turn_tables(1)
            sum_pass(1, "agg", 0)
            sum_pass(2, "agg", 0)
            dense(W("L1_gnn_W"))
            sum_pass(3, "agg", 0)
            sum_pass(4, "agg", 1)
            pe.wait_ge(s["gru_src"], 1)

            def gru(turn, b, width):
                for u in range(width):
                    pe.wait_ge(s["gru_stage"], b * 3 + (3 * u + 3))
                    for k in range(3):
                        last = t_.transpose(PS[:, 4 * u, k * P:(k + 1) * P], stage[:, 3 * u + k, :], ident[:, :])
                    last.then_inc(s["gru_tr"], 1)
                for u in range(width):
                    pe.wait_ge(s["gru_T"], b + (u + 1))
                    for k, name in ((0, "L2_gnn_W_in"), (1, "L2_gnn_W_out")):
                        last = t_.matmul(PS[:, 4 * u + 1, k * D:(k + 1) * D], stageT[:, 3 * u + 1 + k, :], W(name),
                                         start=True, stop=True)
                    last.then_inc(s["gru_a"], 1)
                for u in range(width):
                    pe.wait_ge(s["gru_a2"], b + (u + 1))
                    for k in range(2):
                        last = t_.transpose(PS[:, 4 * u + 2, k * P:(k + 1) * P], a2[:, u, k, :], ident[:, :])
                    last.then_inc(s["gru_a2T"], 1)
                for u in range(width):
                    gates, hT = PS[:, 4 * u + 3, :], stageT[:, 3 * u, :]
                    t_.matmul(gates, ones[0:1, :], gate_b[:, :], start=True, stop=False)
                    t_.matmul(gates[:, 0:2 * D], hT, whh[:, 0:2 * D], start=False, stop=False)
                    t_.matmul(gates[:, 3 * D:4 * D], hT, whh[:, 2 * D:3 * D], start=False, stop=False)
                    pe.wait_ge(s["gru_aT"], b + (u + 1))
                    t_.matmul(gates[:, 0:3 * D], aT[:, u, 0, :], wih[:, 0, :], start=False, stop=False)
                    t_.matmul(gates[:, 0:3 * D], aT[:, u, 1, :], wih[:, 1, :], start=False, stop=True)\
                      .then_inc(s["gru_gates"], 1)
            gru_blocks(pe, gru)
            layers = sum(k == "att" for k, _, _ in PASSES)
            for j in range(layers):
                dense(W(f"L3_gnn_W{j + 1}"))
                max_pass(5 + 2 * j)
                att_pass(6 + 2 * j)
                column_sums(UA, 2 * j + 1)
                column_sums(UB, 2 * j + 2)

        @block.vector
        def _(dve):
            v_ = nc.vector
            chained = [0]

            def link(ins):
                chained[0] += 1
                ins.then_inc(s["dve_chain"], 1)
                dve.wait_ge(s["dve_chain"], chained[0])

            def looped(i, per):
                count = [0]
                start = chained[0]

                def link_in(ins, ahead=0):
                    count[0] += 1
                    assert count[0] <= per
                    ins.then_inc(s["dve_chain"], 1)
                    need(dve, "dve_chain", i * per + (start + count[0] - ahead))
                return link_in

            tick = dict(var=0, mm=0)

            def block_of_keys(key):
                turn_i = block_i.bitcast(i32)
                link(v_.tensor_scalar(turn_i, key, 7, None, ALU.arith_shift_right))
                link(v_.tensor_copy(key_block, turn_i))

            def records(l, key, oth):
                v_.tensor_copy(rec[l][:, :, 0], key).then_inc(s[f"placed{l}"], 1)
                v_.tensor_copy(rec[l][:, :, 1], oth).then_inc(s[f"placed{l}"], 1)

            def check_order():
                dve.wait_ge(s["next_loaded"], 16)
                link(v_.memset(falls[:, :], 0.0))
                link(v_.tensor_tensor(mask[:, 0:EC - 1], key_block[:, 0:EC - 1], key_block[:, 1:EC], ALU.is_gt))
                link(v_.tensor_reduce(falls[:, 0:1], mask[:, 0:EC - 1], AX.X, ALU.add))
                link(v_.tensor_scalar(next_key[0:EP - 1, :], next_key[0:EP - 1, :], 7, None, ALU.arith_shift_right))
                link(v_.tensor_copy(next_block[0:EP - 1, :], next_key[0:EP - 1, 0:1]))
                link(v_.tensor_tensor(falls[0:EP - 1, 1:2], key_block[0:EP - 1, EC - 1:EC], next_block[0:EP - 1, :],
                                      ALU.is_gt))
                dve.sem_inc(s["order_ready"])
                dve.wait_ge(s["order_summed"], 1)
                v_.tensor_copy(unsorted[:, :], PS[0:1, 2, 0:1]).then_inc(s["unsorted_known"], 1)

            def place_list(l, turn):
                with dve.Fori(0, NB, 1) as b:
                    lk = looped(b, 1)
                    lk(v_.tensor_scalar(mask, key_block, iota_row[0:EP, ds(b, 1)], 0.0, ALU.is_equal, ALU.add,
                                        accum_out=cnt[0:EP, 0, ds(b, 1)]))
                chained[0] += NB
                link(v_.memset(pos, 0.0))
                dve.sem_inc(s["counts_ready"])
                dve.wait_ge(s["prefix_ready"], turn + 1)
                total, upto, start = (cnt[0:EP, t, :] for t in (1, 2, 3))
                link(v_.tensor_copy(total, PS[0:EP, 0, 0:NB]))
                link(v_.tensor_tensor_scan(upto, total, total, 0.0, ALU.add, ALU.max))
                link(v_.tensor_tensor(start, upto, total, ALU.subtract))
                link(v_.tensor_copy(cnt_i[0:1, :], start[0:1, :]))
                link(v_.tensor_scalar(first_tile[l][:, :], cnt_i[0:1, :], 7, None, ALU.arith_shift_right))
                link(v_.tensor_tensor(start, start, PS[0:EP, 1, 0:NB], ALU.add))
                with dve.Fori(0, NB, 1) as b:
                    lk = looped(b, 3)
                    lk(v_.tensor_scalar(mask, key_block, iota_row[0:EP, ds(b, 1)], None, ALU.is_equal))
                    lk(v_.tensor_tensor_scan(scan, mask, mask, cnt[0:EP, 3, ds(b, 1)], ALU.add, ALU.max))
                    dve.sem_inc(s["dve_turn"])
                    lk(v_.copy_predicated(pos, mask.bitcast(u16), scan))
                chained[0] += 3 * NB
                v_.tensor_scalar(place[l], pos, -1.0, None, ALU.add).then_inc(s[f"placed{l}"], 1)
                dve.wait_ge(s[f"placed{l}"], 3)

            def tile_tables(l):
                dve.wait_ge(s["chunk_loaded"], 32 * (l + 1))
                tail = TILES - (CH - 1) * P
                for x, tab in ((0, key_tab), (1, other_tab)):
                    v_.tensor_copy(split[:, 0:CH - 1, :],
                                   chunk[:, 0:CH - 1, :].rearrange("p c (e x) -> p c e x", x=2)[:, :, :, x])\
                      .then_inc(s["chunk_split"], 1)
                    v_.tensor_copy(split[0:tail, CH - 1, :],
                                   chunk[0:tail, CH - 1, :].rearrange("p (e x) -> p e x", x=2)[:, :, x])\
                      .then_inc(s["chunk_split"], 1)
                    link(v_.memset(tab[:, TILES:2 * TILES], 0 if x else NO_KEY))
                    dve.wait_ge(s["chunk_turned"], 2 * l + x + 1)
                    link(v_.tensor_copy(tab[:, 0:TILES], PSf[:, 0:TILES]))
                link(v_.memset(zero_row, 0))
                link(v_.memset(step_cnt[:, 0:2], 0.0))

            def step_tables_of_block(l, b):
                def lk(i, ins):
                    ins.then_inc(s["table_chain"], 1)
                    dve.wait_ge(s["table_chain"], b * 5 + (NB * 5 * l + i))
                t0 = dve.value_load(first_tile[l][0:1, ds(b, 1)], min_val=0, max_val=TILES - 1)
                lk(1, v_.tensor_scalar(key_step[:, ds(t0 + b, TILES)], key_tab[:, ds(t0, TILES)],
                                       step_cnt[:, 0:1], None, ALU.add))
                lk(2, v_.tensor_scalar(other_step[:, ds(t0 + b, TILES)], other_tab[:, ds(t0, TILES)],
                                       0.0, None, ALU.add))
                lk(3, v_.tensor_scalar(block_row[:, ds(t0 + b, TILES)], zero_row, step_cnt[0:1, 1:2], None, ALU.add))
                lk(4, v_.tensor_scalar(step_cnt[:, 0:1], step_cnt[:, 0:1], -float(P), None, ALU.add))
                lk(5, v_.tensor_scalar(step_cnt[:, 1:2], step_cnt[:, 1:2], 1.0, None, ALU.add))

            def finish_tables(l):
                link(v_.tensor_copy(rel_key[l][:, 0:STEPS], key_step[:, 0:STEPS]))
                link(v_.tensor_copy(other[l][:, :], other_step[:, 0:STEPS]))
                link(v_.tensor_copy(block_of[l][:, 0:STEPS], block_row[:, 0:STEPS]))
                dve.sem_inc(s["tables_ready"])

            def over_nodes(v):
                return v.unsqueeze(1).broadcast_to([P, NB, D])

            def over_features(st):
                return st.unsqueeze(2).broadcast_to([P, NB, D])

            def sqrt_by_act():
                tick["var"] += 1
                dve.sem_inc(s["var_ready"])
                dve.wait_ge(s["sd_ready"], tick["var"])

            def norm_relu(dst):
                var, mean = stat[:, 0, :], stat[:, 1, :]
                link(v_.tensor_reduce(mean, X[:, :, :], AX.X, ALU.add))
                link(v_.tensor_scalar(mean, mean, 1.0 / D, None, ALU.mult))
                link(v_.tensor_tensor(dst, X[:, :, :], over_features(mean), ALU.subtract))
                link(v_.tensor_tensor(UB, dst, dst, ALU.mult))
                link(v_.tensor_reduce(var, UB, AX.X, ALU.add))
                link(v_.tensor_scalar(var, var, 1.0 / D, EPS, ALU.mult, ALU.add))
                sqrt_by_act()
                link(v_.reciprocal(mean, var))
                link(v_.scalar_tensor_tensor(dst, dst, 0.0, over_features(mean), ALU.max, ALU.mult))

            def dense_results(take):
                n = tick["mm"]
                tick["mm"] += 1
                dve.sem_inc(s["mm_src_ready"])
                with dve.Fori(0, NMG, 1) as g:
                    dve.wait_ge(s["mm_ready"], g + (NMG * n + 1))
                    take(PSf[:, 1024:1024 + MG * D].rearrange("p (k f) -> p k f", f=D), ds(g * MG, MG))\
                        .then_inc(s["mm_used"], 1)
                dve.wait_ge(s["mm_used"], NMG * (n + 1) + 1)

            regs = [dve.alloc_register(f"dve_block{k}") for k in range(G)]

            def blocks_of(l, g):
                dve.sem_inc(s["dve_turn"])
                dve.load(regs, block_of[l][0:1, ds(g * G, G)])
                return [dve.snap(r, min_val=0, max_val=NB - 1) for r in regs]

            def make_onehot(n, l, g, h, op=ALU.is_equal, ring16=False):
                need(dve, "groups_done", n * GROUPS + g - 1 if isinstance(g, int) else g + (n * GROUPS - 1))
                out = far[:, h, 0:G * P].rearrange("p (g d) -> p g d", d=P) if ring16 else onehot[:, h, :, :]
                v_.tensor_tensor(out, iota_row[:, :].unsqueeze(1).broadcast_to([P, G, P]),
                                 rel_key[l][:, ds(g * G, G)].unsqueeze(2).broadcast_to([P, G, P]), op)\
                  .then_inc(s["onehot_ready"], 1)

            def add_sums(n, l, g, h, accs, lk):
                dve.wait_ge(s["groups_done"], g + (n * GROUPS + 1))
                for k, b in enumerate(blocks_of(l, g)):
                    acc = accs[k % len(accs)]
                    part = acc[:, ds(b, 1), :]
                    lk(v_.tensor_tensor(part, part, agg_slot(h, k).unsqueeze(1), ALU.add), ahead=0 if k == G - 1 else len(accs) - 1)
                dve.sem_inc(s["sums_used"])

            def degree_pass(n, l):
                make_onehot(n, l, 0, 0, ring16=True)

                def body(g, h):
                    if not (isinstance(g, int) and g + 1 >= GROUPS):
                        make_onehot(n, l, g + 1, 1 - h, ring16=True)
                    dve.wait_ge(s["groups_done"], g + (n * GROUPS + 1))
                    v_.tensor_copy(step_sum[:, ds(g * G, G)], PS[:, 3 * h, 0:G]).then_inc(s["sums_used"], 1)
                pairs(dve, body, peel_last=True)
                link(v_.memset(step_upto[:, 0:1], 0.0))
                dve.wait_ge(s["sums_used"], (n + 1) * GROUPS)
                link(v_.tensor_tensor_scan(step_upto[:, 1:], step_sum, step_sum, 0.0, ALU.add, ALU.max))
                link(v_.tensor_copy(block_upto[:, NB:NB + 1], step_upto[:, STEPS:STEPS + 1]))
                with dve.Fori(0, NB, 1) as b:
                    lk = looped(b, 1)
                    t0 = dve.value_load(first_tile[l][0:1, ds(b, 1)], min_val=0, max_val=TILES - 1)
                    lk(v_.tensor_copy(block_upto[:, ds(b, 1)], step_upto[:, ds(t0 + b, 1)]))
                chained[0] += NB
                link(v_.tensor_tensor(deg[:, :], block_upto[:, 1:NB + 1], block_upto[:, 0:NB], ALU.subtract))

            def sum_pass(n, l, *accs, beside=None):
                make_onehot(n, l, 0, 0)

                def body(g, h):
                    if not (isinstance(g, int) and g + 1 >= GROUPS):
                        make_onehot(n, l, g + 1, 1 - h)
                    add_sums(n, l, g, h, accs, looped(g, G))
                if beside is None:
                    pairs(dve, body, peel_last=True)
                else:
                    for h in range(HALVES):
                        body(h, h)
                    with dve.Fori(0, NB, 1) as b:
                        for h in range(HALVES):
                            body(b * HALVES + (HALVES + h), h)
                        beside(b)
                    with dve.Fori(HALVES * (NB + 1), GROUPS - HALVES - 1, HALVES) as g0:
                        for h in range(HALVES):
                            body(g0 + h, h)
                    for h in range(HALVES):
                        body(GROUPS - HALVES + h, h)
                chained[0] += GROUPS * G

            def max_pass(n):
                make_onehot(n, 0, 0, 0, ALU.not_equal, ring16=True)

                def body(g, h):
                    if not (isinstance(g, int) and g + 1 >= GROUPS):
                        make_onehot(n, 0, g + 1, 1 - h, ALU.not_equal, ring16=True)
                    blocks = blocks_of(0, g)
                    dve.wait_ge(landed_sem(n, h), landed(n, g, h))
                    dve.wait_ge(s["onehot_ready"], g + (n * GROUPS + 1))
                    for k in range(1, G, 2):
                        v_.tensor_scalar(spread[:, k, H - 1, :], far[:, h, k * P:(k + 1) * P], FAR,
                                         rows[:, h, k, RW - 1:RW], ALU.mult, ALU.add).then_inc(s["dve_spread"], 1)
                    for k in range(G):
                        dve.wait_ge(s["max_ready"], g * G + (max_base[n] * G + k + 1))
                        v_.tensor_reduce(tmax[:, k, :], PS[:, k, :].rearrange("p (h e) -> p h e", e=P), AX.X, ALU.max)\
                          .then_inc(s["max_used"], 1)
                    lk = looped(g, G)
                    dve.wait_ge(s["max_used"], g * G + (max_base[n] + 1) * G)
                    for k, b in enumerate(blocks):
                        m = M[:, k % 2, ds(b, 1), :]
                        lk(v_.tensor_tensor(m, m, tmax[:, k, :].unsqueeze(1), ALU.max), ahead=0 if k == G - 1 else 1)
                    dve.sem_inc(s["sums_used"])
                pairs(dve, body, peel_last=True)
                chained[0] += GROUPS * G

            def split_parts(parts, value, rest, work):
                link(v_.tensor_copy(parts[0], value))
                link(v_.tensor_copy(work, parts[0]))
                link(v_.tensor_tensor(rest, value, work, ALU.subtract))
                link(v_.tensor_copy(parts[1], rest))
                link(v_.tensor_copy(work, parts[1]))
                link(v_.tensor_tensor(rest, rest, work, ALU.subtract))
                link(v_.tensor_copy(parts[2], rest))

            def att_pass(n):
                PER = 4 + G
                ab = att_base[n]

                def make(g, q):
                    if not (isinstance(g, int) and g < RING):
                        dve.wait_ge(s["groups_done"], g + (n * GROUPS - RING + 1))
                    v_.tensor_tensor(onehot4[q], iota_row[:, :].unsqueeze(1).broadcast_to([P, G, P]),
                                     rel_key[0][:, ds(g * G, G)].unsqueeze(2).broadcast_to([P, G, P]), ALU.is_equal)\
                      .then_inc(s["onehot_ready"], 1)
                make(0, 0)
                make(1, 1)

                def body(g, q):
                    h = q % HALVES
                    if not (isinstance(g, int) and g + 2 >= GROUPS):
                        make(g + 2, (q + 2) % RING)
                    first = looped(g, PER)
                    dve.wait_ge(s["expanded"], g + (ab + 1))
                    first(v_.tensor_reduce(terms[:, :, :], PS[:, 7, 0:2 * H * G * SPLIT]
                                           .rearrange("p (g s t) -> p g t s", s=SPLIT, t=2 * H), AX.X, ALU.add))
                    dve.sem_inc(s["terms_taken"])
                    dve.wait_ge(s[f"reload{q}"], reloaded(n, g, q))
                    first(v_.tensor_tensor(small[:, h, :, :], rows4[q][:, :, D:RW], terms[:, :, 0:H], ALU.add))
                    first(v_.scalar_tensor_tensor(small2[:, h, :, :], small[:, h, :, :], SLOPE, small[:, h, :, :],
                                                  ALU.mult, ALU.max))
                    first(v_.tensor_tensor(small[:, h, :, :], small2[:, h, :, :], terms[:, :, H:2 * H], ALU.subtract))
                    dve.sem_inc(s["logits"])
                    if isinstance(g, int) and g < 2:
                        dve.sem_inc(s["dve_chain"], G)
                    else:
                        add_sums(n, 0, g - 2, h, (ACC[:, :, :], ACC_ODD), first)
                quads(dve, body)
                chained[0] += GROUPS * PER + 2 * G
                start = chained[0] - 2 * G
                count = [0]

                def last(ins, ahead=0):
                    count[0] += 1
                    ins.then_inc(s["dve_chain"], 1)
                    dve.wait_ge(s["dve_chain"], start + count[0] - ahead)
                for g in (GROUPS - 2, GROUPS - 1):
                    add_sums(n, 0, g, g % HALVES, (ACC[:, :, :], ACC_ODD), last)
                link(v_.tensor_tensor(ACC[:, :, :], ACC[:, :, :], ACC_ODD, ALU.add))

            dve.wait_ge(s["const_ready"], 6)
            dve.wait_ge(s["edges_loaded"], 32)
            dve.sem_inc(s["mm_used"])
            link(v_.memset(ones16[:, :], 1.0))
            link(v_.tensor_copy(ident16[:, :], ident[:, :]))
            block_of_keys(dst_i)
            records(0, dst_i, src_i)
            check_order()
            block_of_keys(src_i)
            records(1, src_i, dst_i)
            place_list(1, 0)
            block_of_keys(dst_i)
            place_list(0, 1)
            dve.sem_inc(s["chunk_free"])
            tile_tables(0)
            dve.sem_inc(s["chunk_free"])
            with dve.Fori(0, NB, 1) as b:
                step_tables_of_block(0, b)
            finish_tables(0)
            dve.wait_ge(s["x_loaded"], 32)
            norm_relu(UA)
            degree_pass(0, 0)
            dve.wait_ge(s["vec_loaded"], 16 * len(vec_names))


            link(v_.tensor_scalar(dinv[:, :], deg[:, :], 1.0, None, ALU.add))
            sqrt_by_act()
            link(v_.reciprocal(stat[:, 2, :], dinv[:, :]))
            link(v_.tensor_copy(dinv[:, :], stat[:, 2, :]))
            dve.wait_ge(s["listed1"], 1)
            link(v_.memset(TAB[:, :, D:RW], 1.0))

            def scaled(ps, blk):
                return v_.tensor_tensor(TAB[:, blk, 0:D], ps, dinv[:, blk].unsqueeze(2).broadcast_to([P, MG, D]),
                                        ALU.mult)
            dense_results(scaled)
            dve.sem_inc(s["table_ready"])
            tile_tables(1)
            link(v_.memset(ACC[:, :, :], 0.0))
            sum_pass(1, 0, ACC[:, :, :], beside=lambda b: step_tables_of_block(1, b))
            finish_tables(1)
            link(v_.tensor_tensor(UA, ACC[:, :, 0:D], TAB[:, :, 0:D], ALU.add))
            link(v_.tensor_tensor(UA, UA, over_features(dinv[:, :]), ALU.mult))
            link(v_.tensor_tensor(UA, UA, over_nodes(V("L0_gnn_b")), ALU.add))
            link(v_.scalar_tensor_tensor(X[:, :, :], UA, 0.0, X[:, :, :], ALU.max, ALU.add))

            norm_relu(TAB[:, :, 0:D])
            dve.sem_inc(s["table_ready"])
            link(v_.memset(ACC[:, :, :], 0.0))
            sum_pass(2, 0, ACC[:, :, :])
            link(v_.tensor_tensor(UA, ACC[:, :, 0:D], TAB[:, :, 0:D], ALU.add))
            dense_results(lambda ps, blk: v_.tensor_tensor(X[:, blk, :], X[:, blk, :], ps, ALU.add))
            link(v_.tensor_tensor(X[:, :, :], X[:, :, :], over_nodes(V("L1_gnn_b")), ALU.add))

            norm_relu(TAB[:, :, 0:D])
            dve.sem_inc(s["table_ready"])
            link(v_.memset(ACC[:, :, :], 0.0))
            link(v_.memset(ACC2, 0.0))
            sum_pass(3, 0, ACC[:, :, :])
            sum_pass(4, 1, ACC2)
            for t, acc in ((0, ACC[:, :, :]), (1, ACC2)):
                link(v_.tensor_scalar(has[:, t, :], acc[:, :, D], 1.0, None, ALU.min))
                link(v_.tensor_scalar(stat[:, 2, :], acc[:, :, D], 1.0, None, ALU.max))
                link(v_.reciprocal(inv[:, t, :], stat[:, 2, :]))
                link(v_.tensor_tensor(acc[:, :, 0:D], acc[:, :, 0:D], over_features(inv[:, t, :]), ALU.mult))
            link(v_.tensor_tensor(gate_b[:, 0:2 * D], gru_b[:, 0, 0:2 * D], gru_b[:, 1, 0:2 * D], ALU.add))
            link(v_.tensor_copy(gate_b[:, 2 * D:3 * D], gru_b[:, 0, 2 * D:3 * D]))
            link(v_.tensor_copy(gate_b[:, 3 * D:4 * D], gru_b[:, 1, 2 * D:3 * D]))
            dve.sem_inc(s["gru_src"])

            def gru(turn, b, width):
                lk = looped(turn, 16)
                for u in range(width):
                    dve.wait_ge(s["gru_a"], b + (u + 1))
                    for t, name in ((0, "L2_gnn_b_in"), (1, "L2_gnn_b_out")):
                        lk(v_.scalar_tensor_tensor(a2[:, u, t, :], V(name), has[:, t, ds(b + u, 1)],
                                                   PS[:, 4 * u + 1, t * D:(t + 1) * D], ALU.mult, ALU.add))
                    dve.sem_inc(s["gru_a2"])
                for u in range(width):
                    dve.wait_ge(s["gru_rz"], b + (u + 1))
                    lk(v_.tensor_tensor(gt[:, u, :], rz[:, u, 0, :], PS[:, 4 * u + 3, 3 * D:4 * D], ALU.mult))
                    lk(v_.tensor_tensor(nn[:, u, :], gt[:, u, :], PS[:, 4 * u + 3, 2 * D:3 * D], ALU.add))
                    dve.sem_inc(s["gru_pre"])
                for u in range(width):
                    dve.wait_ge(s["gru_n"], b + (u + 1))
                    g1, n1, x1 = gt[:, u, :], nn[:, u, :], X[:, ds(b + u, 1), :]
                    lk(v_.tensor_tensor(g1.unsqueeze(1), TAB[:, ds(b + u, 1), 0:D], n1.unsqueeze(1), ALU.subtract))
                    lk(v_.tensor_tensor(g1, g1, rz[:, u, 1, :], ALU.mult))
                    lk(v_.tensor_tensor(g1, g1, n1, ALU.add))
                    lk(v_.tensor_tensor(x1, x1, g1.unsqueeze(1), ALU.add))
            gru_blocks(dve, gru)
            chained[0] += 8 * NB

            norm_relu(UA)
            layers = sum(k == "att" for k, _, _ in PASSES)
            for j in range(layers):
                dense_results(lambda ps, blk: v_.tensor_copy(TAB[:, blk, 0:D], ps))
                heads = UA.rearrange("p b (h f) -> p b h f", f=FH)
                link(v_.tensor_tensor(UA, TAB[:, :, 0:D], over_nodes(V(f"L3_gnn_a{j + 1}_src")), ALU.mult))
                link(v_.tensor_reduce(TAB[:, :, D:RW], heads, AX.X, ALU.add))
                dve.sem_inc(s["table_ready"])
                link(v_.tensor_tensor(UA, TAB[:, :, 0:D], over_nodes(V(f"L3_gnn_a{j + 1}_dst")), ALU.mult))
                link(v_.tensor_reduce(T2[:, :, 0:H], heads, AX.X, ALU.add))
                link(v_.memset(M[:, :, :, :], FAR))
                max_pass(5 + 2 * j)
                top = M[:, 0]
                link(v_.tensor_tensor(top, top, M[:, 1], ALU.max))
                link(v_.tensor_tensor(top, top, TAB[:, :, D:RW], ALU.max))
                link(v_.tensor_tensor(top, top, T2[:, :, 0:H], ALU.add))
                link(v_.scalar_tensor_tensor(T2[:, :, H:2 * H], top, SLOPE, top, ALU.mult, ALU.max))
                split_parts([T2s[:, :, t, :] for t in range(SPLIT)], T2[:, :, :],
                            UA[:, :, 0:2 * H], UA[:, :, 2 * H:4 * H])
                link(v_.memset(ACC[:, :, :], 0.0))
                link(v_.memset(ACC_ODD, 0.0))
                dve.sem_inc(s["t2_ready"])
                att_pass(6 + 2 * j)
                link(v_.tensor_tensor(wtmp[:, :, :], TAB[:, :, D:RW], T2[:, :, 0:H], ALU.add))
                link(v_.scalar_tensor_tensor(wself[:, :, :], wtmp[:, :, :], SLOPE, wtmp[:, :, :], ALU.mult, ALU.max))
                link(v_.tensor_tensor(wtmp[:, :, :], wself[:, :, :], T2[:, :, H:2 * H], ALU.subtract))
                dve.sem_inc(s["self_logit"])
                dve.wait_ge(s["self_w"], j + 1)
                wide = wself[:, :, :].unsqueeze(3).broadcast_to([P, NB, H, FH])
                link(v_.tensor_tensor(heads, TAB[:, :, 0:D].rearrange("p b (h f) -> p b h f", f=FH), wide, ALU.mult))
                link(v_.tensor_tensor(UA, UA, ACC[:, :, 0:D], ALU.add))
                link(v_.tensor_tensor(wtmp[:, :, :], wself[:, :, :], ACC[:, :, D:RW], ALU.add))
                link(v_.reciprocal(wself[:, :, :], wtmp[:, :, :]))
                link(v_.tensor_tensor(heads, heads, wide, ALU.mult))
                link(v_.tensor_tensor(UA, UA, over_nodes(V(f"L3_gnn_b{j + 1}")), ALU.add))
                sums = PS[:, 6, :].rearrange("p (k f) -> p f k", f=D)
                dve.sem_inc(s["bn_src"])
                dve.wait_ge(s["bn_sum"], 2 * j + 1)
                link(v_.tensor_reduce(bn[:, 0, :], sums, AX.X, ALU.add))
                link(v_.tensor_scalar(bn[:, 1, :], bn[:, 0, :], 1.0 / N, None, ALU.mult))
                link(v_.tensor_tensor(UA, UA, over_nodes(bn[:, 1, :]), ALU.subtract))
                link(v_.tensor_tensor(UB, UA, UA, ALU.mult))
                dve.sem_inc(s["bn_src"])
                dve.wait_ge(s["bn_sum"], 2 * j + 2)
                link(v_.tensor_reduce(bn[:, 0, :], sums, AX.X, ALU.add))
                link(v_.tensor_scalar(bn[:, 2, :], bn[:, 0, :], 1.0 / N, EPS, ALU.mult, ALU.add))
                sqrt_by_act()
                link(v_.reciprocal(bn[:, 0, :], bn[:, 2, :]))
                link(v_.tensor_tensor(bn[:, 3, :], bn[:, 0, :], V(f"L3_gnn_g{j + 1}"), ALU.mult))
                link(v_.tensor_tensor(UA, UA, over_nodes(bn[:, 3, :]), ALU.mult))
                link(v_.tensor_tensor(UA, UA, over_nodes(V(f"L3_gnn_beta{j + 1}")), ALU.add))
                link(v_.tensor_scalar(UB, UA, 0.0, None, ALU.min))
                dve.sem_inc(s["elu_src"])
                dve.wait_ge(s["elu_exp"], j + 1)
                link(v_.tensor_scalar(UB, UB, -1.0, None, ALU.add))
                link(v_.scalar_tensor_tensor(UA, UA, 0.0, UB, ALU.max, ALU.add))
            link(v_.tensor_tensor(X[:, :, :], X[:, :, :], UA, ALU.add))
            dve.sem_inc(s["out_ready"])


_INS = ["x", "src", "dst", "L0_gnn_W", "L0_gnn_b", "L1_gnn_W", "L1_gnn_b", "L2_gnn_W_in", "L2_gnn_b_in",
        "L2_gnn_W_out", "L2_gnn_b_out", "L2_gnn_w_ih", "L2_gnn_w_hh", "L2_gnn_b_ih", "L2_gnn_b_hh", "L3_gnn_W1",
        "L3_gnn_a1_src", "L3_gnn_a1_dst", "L3_gnn_b1", "L3_gnn_g1", "L3_gnn_beta1", "L3_gnn_W2", "L3_gnn_a2_src",
        "L3_gnn_a2_dst", "L3_gnn_b2", "L3_gnn_g2", "L3_gnn_beta2"]
_TRANSPOSED = {"L1_gnn_W", "L2_gnn_W_in", "L2_gnn_W_out", "L2_gnn_w_ih", "L2_gnn_w_hh"}


def kernel(**inputs):
    import numpy as _np
    import concourse.bacc as _bacc
    from concourse import mybir as _mybir
    from concourse.bass_utils import run_bass_kernel_spmd as _run

    nc = _bacc.Bacc("TRN2", target_bir_lowering=False, num_devices=1)
    arrays, aps = {}, {}
    for name in _INS:
        a = _np.asarray(inputs[name])
        a = _np.ascontiguousarray(a.T if name in _TRANSPOSED else a)
        arrays[f"in_{name}_dram"] = a
        aps[name] = nc.dram_tensor(f"in_{name}_dram", a.shape, _mybir.dt.from_np(a.dtype), kind="ExternalInput").ap()
    out = nc.dram_tensor("out_dram", aps["x"].shape, _mybir.dt.float32, kind="ExternalOutput").ap()
    gnn_kernel(nc, aps, out)
    return _run(nc, [arrays], core_ids=[0]).results[0]["out_dram"]
```
